# Optimizing a Trainium2 kernel written in Bass

```python
import numpy as np
import jax
import jax.numpy as jnp

def _softmax(x, axis=-1):
    return jax.nn.softmax(x, axis=axis)

def _gelu(x):
    return jax.nn.gelu(x, approximate=True)

def _silu(x):
    return jax.nn.silu(x)

def _sigmoid(x):
    return jax.nn.sigmoid(x)

def _layernorm(x, axis=-1, eps=1e-05):
    m = jnp.mean(x, axis=axis, keepdims=True)
    v = jnp.var(x, axis=axis, keepdims=True)
    return (x - m) / jnp.sqrt(v + eps)

def _scatter_add(tgt, idx, src, axis=0):
    return tgt.at[idx].add(src)

def _segment_sum(src, seg, n):
    return jax.ops.segment_sum(src, seg, n)
kernel_name = 'mk_gnn_ffn_d4_gnn_r8_f9174f'

def setup_inputs(seed: int=0):
    np.random.seed(seed)
    _w = jnp.asarray

    def _rec_inputs():
        import jax
        import jax.numpy as jnp
        _gk = jax.random.key(seed)
        x = -0.001003 + 1 * jax.random.normal(jax.random.fold_in(_gk, 1), (384, 512), jnp.float32)
        src = jax.random.randint(jax.random.fold_in(_gk, 2), (6144,), 0, 384, jnp.int32)
        dst = jax.random.randint(jax.random.fold_in(_gk, 3), (6144,), 0, 384, jnp.int32)
        _o = jnp.argsort(dst, stable=True)
        src = src[_o]
        dst = dst[_o]
        edge_attr_64 = 0.000279952 + 1.00013 * jax.random.normal(jax.random.fold_in(_gk, 11), (6144, 64), jnp.float32)
        edge_type_4 = jax.random.randint(jax.random.fold_in(_gk, 13), (6144,), 0, 4, jnp.int32)
        edge_weight = jax.random.uniform(jax.random.fold_in(_gk, 14), (6144,), jnp.float32, 0.0, 0.999995)
        return (x, src, dst, edge_attr_64, edge_type_4, edge_weight)
    x, src, dst, edge_attr_64, edge_type_4, edge_weight = _rec_inputs()

    def _L0_gnn_setup():
        import jax, jax.numpy as jnp
        import numpy as np
        N = 384
        HID = 512
        H = 8
        HD = HID // H
        E = 12288
        LN_EPS = 1e-05
        key = jax.random.key(seed)
        ks = jax.random.split(key, 12)
        x = jax.random.normal(ks[0], (N, HID), jnp.float32)
        lin = jax.random.permutation(ks[1], N * N)[:E]
        edges = jnp.stack([lin // N, lin % N]).astype(jnp.int32)
        s = 0.02
        Wv = jax.random.normal(ks[2], (HID, HID), jnp.float32) * s
        bv = jax.random.normal(ks[3], (HID,), jnp.float32) * s
        Ww = jax.random.normal(ks[4], (2 * HID, 2 * HID), jnp.float32) * s
        bw = jax.random.normal(ks[5], (2 * HID,), jnp.float32) * s
        Wa = jax.random.normal(ks[6], (2 * HD, 1), jnp.float32) * s
        ba = jax.random.normal(ks[7], (1,), jnp.float32) * s
        gamma = jnp.ones((HID,), jnp.float32)
        beta = jnp.zeros((HID,), jnp.float32)
        return dict(x=x, edges=edges, Wv=Wv, bv=bv, Ww=Ww, bw=bw, Wa=Wa, ba=ba, gamma=gamma, beta=beta)
    _L0_gnn_all = _L0_gnn_setup()
    _L0_gnn_in = {k: v for k, v in _L0_gnn_all.items() if k in ('Wv', 'bv', 'Ww', 'bw', 'Wa', 'ba', 'gamma', 'beta')}
    del _L0_gnn_all

    def _L0_ffn_setup():
        import jax, jax.numpy as jnp
        import numpy as np
        B, S, D, DFF, E, K = (4, 256, 512, 1024, 8, 2)
        key = jax.random.key(seed)
        ks = jax.random.split(key, 5)
        x = jax.random.normal(ks[0], (B, S, D), dtype=jnp.float32)
        Wg = jax.random.normal(ks[1], (D, E), dtype=jnp.float32) * 0.02
        bg = jnp.zeros((E,), dtype=jnp.float32)
        W1 = jax.random.normal(ks[2], (E, D, 2 * DFF), dtype=jnp.float32) * 0.02
        b1 = jnp.zeros((E, 2 * DFF), dtype=jnp.float32)
        W2 = jax.random.normal(ks[3], (E, DFF, D), dtype=jnp.float32) * 0.02
        b2 = jnp.zeros((E, D), dtype=jnp.float32)
        return {'x': x, 'Wg': Wg, 'bg': bg, 'W1': W1, 'b1': b1, 'W2': W2, 'b2': b2}
    _L0_ffn_all = _L0_ffn_setup()
    _L0_ffn_in = {k: v for k, v in _L0_ffn_all.items() if k in ('Wg', 'bg', 'W1', 'b1', 'W2', 'b2')}
    del _L0_ffn_all

    def _L1_gnn_setup():
        import jax, jax.numpy as jnp
        import numpy as np
        N_NODES = 2500
        N_EDGES = 40000
        HIDDEN = 512
        EDGE_DIM = 64
        LN_EPS = 1e-05

        def mish(x):
            return x * jnp.tanh(jax.nn.softplus(x))
        key = jax.random.key(seed)
        ks = jax.random.split(key, 8)
        s = lambda fan_in: 1.0 / np.sqrt(fan_in)
        return {'x': jax.random.normal(ks[0], (N_NODES, HIDDEN), dtype=jnp.float32), 'edge_index': jax.random.randint(ks[1], (2, N_EDGES), 0, N_NODES, dtype=jnp.int64), 'edge_attr': jax.random.normal(ks[2], (N_EDGES, EDGE_DIM), dtype=jnp.float32), 'W1': jax.random.normal(ks[3], (2 * HIDDEN + EDGE_DIM, HIDDEN), dtype=jnp.float32) * s(2 * HIDDEN + EDGE_DIM), 'b1': jnp.zeros((HIDDEN,), dtype=jnp.float32), 'W2': jax.random.normal(ks[4], (HIDDEN, HIDDEN), dtype=jnp.float32) * s(HIDDEN), 'b2': jnp.zeros((HIDDEN,), dtype=jnp.float32), 'W3': jax.random.normal(ks[5], (2 * HIDDEN, HIDDEN), dtype=jnp.float32) * s(2 * HIDDEN), 'b3': jnp.zeros((HIDDEN,), dtype=jnp.float32), 'W4': jax.random.normal(ks[6], (HIDDEN, HIDDEN), dtype=jnp.float32) * s(HIDDEN), 'b4': jnp.zeros((HIDDEN,), dtype=jnp.float32), 'gamma': jnp.ones((HIDDEN,), dtype=jnp.float32), 'beta': jnp.zeros((HIDDEN,), dtype=jnp.float32)}
    _L1_gnn_all = _L1_gnn_setup()
    _L1_gnn_in = {k: v for k, v in _L1_gnn_all.items() if k in ('W1', 'b1', 'W2', 'b2', 'W3', 'b3', 'W4', 'b4', 'gamma', 'beta')}
    del _L1_gnn_all

    def _L1_ffn_setup():
        import jax, jax.numpy as jnp
        import numpy as np
        DIM = 512
        FFN_DIM = 1408
        GROUP = 128
        EPS = 1e-05

        def _quantize_weight(w, group_size):
            o, i = w.shape
            wg = w.reshape(o, i // group_size, group_size)
            scale = jnp.mean(jnp.abs(wg), axis=-1, keepdims=True) + EPS
            wq = jnp.clip(jnp.round(wg / scale), -1.0, 1.0) * scale
            return wq.reshape(o, i)

        def _bitlinear(x, w, group_size=GROUP):
            wq = w + jax.lax.stop_gradient(_quantize_weight(w, group_size) - w)
            return jnp.einsum('bsd,fd->bsf', x, wq)
        key = jax.random.key(seed)
        k_x, k_g, k_u, k_d = jax.random.split(key, 4)
        x = jax.random.normal(k_x, (8, 512, DIM), dtype=jnp.float32)
        sd_in = 1.0 / np.sqrt(DIM)
        sd_ffn = 1.0 / np.sqrt(FFN_DIM)
        w_gate = jax.random.normal(k_g, (FFN_DIM, DIM), dtype=jnp.float32) * sd_in
        w_up = jax.random.normal(k_u, (FFN_DIM, DIM), dtype=jnp.float32) * sd_in
        w_down = jax.random.normal(k_d, (DIM, FFN_DIM), dtype=jnp.float32) * sd_ffn
        return {'x': x, 'w_gate': w_gate, 'w_up': w_up, 'w_down': w_down}
    _L1_ffn_all = _L1_ffn_setup()
    _L1_ffn_in = {k: v for k, v in _L1_ffn_all.items() if k in ('w_gate', 'w_up', 'w_down')}
    del _L1_ffn_all

    def _L2_gnn_setup():
        import jax, jax.numpy as jnp
        import numpy as np
        N, E, H, D_IN, D_PRIME = (6250, 100000, 8, 512, 64)

        def _segment_softmax(scores, seg, num_segments):
            smax = jax.ops.segment_max(scores, seg, num_segments=num_segments)
            ex = jnp.exp(scores - smax[seg])
            denom = jax.ops.segment_sum(ex, seg, num_segments=num_segments)
            return ex / denom[seg]
        key = jax.random.key(seed)
        ks = jax.random.split(key, 6)
        x = jax.random.normal(ks[0], (N, D_IN), dtype=jnp.float32)
        edge_index = jax.random.randint(ks[1], (2, E), 0, N)
        Ws = jax.random.normal(ks[2], (H, D_IN, D_PRIME), dtype=jnp.float32) * 0.05
        Wb = jax.random.normal(ks[3], (H, D_PRIME), dtype=jnp.float32) * 0.05
        a_w = jax.random.normal(ks[4], (H, 2 * D_PRIME), dtype=jnp.float32) * 0.05
        a_b = jax.random.normal(ks[5], (H,), dtype=jnp.float32) * 0.05
        return dict(x=x, edge_index=edge_index, Ws=Ws, Wb=Wb, a_w=a_w, a_b=a_b)
    _L2_gnn_all = _L2_gnn_setup()
    _L2_gnn_in = {k: v for k, v in _L2_gnn_all.items() if k in ('Ws', 'Wb', 'a_w', 'a_b')}
    del _L2_gnn_all

    def _L2_ffn_setup():
        import jax, jax.numpy as jnp
        import numpy as np
        import math
        E, K, CAPF = (8, 2, 1.25)
        D, DFF = (512, 256)

        def _moe(x, Wr, br, W1, b1, W2, b2):
            orig = x.shape
            d = orig[-1]
            xf = x.reshape(-1, d)
            N = xf.shape[0]
            logits = xf @ Wr + br
            probs = jax.nn.softmax(logits, axis=-1)
            topk_p, topk_i = jax.lax.top_k(probs, K)
            topk_w = topk_p / (jnp.sum(topk_p, axis=-1, keepdims=True) + 1e-09)
            cap = max(1, int(math.ceil(CAPF * float(N * K) / float(E))))
            flat_e = topk_i.reshape(-1)
            flat_w = topk_w.reshape(-1)
            tok = jnp.repeat(jnp.arange(N), K)
            one_hot = jax.nn.one_hot(flat_e, E, dtype=xf.dtype)
            pos = (jnp.cumsum(one_hot, axis=0) - one_hot)[jnp.arange(N * K), flat_e]
            pos = pos.astype(jnp.int32)
            keep = pos < cap
            w_k = jnp.where(keep, flat_w, 0.0)
            sum_w = jnp.zeros((N,), xf.dtype).at[tok].add(w_k)
            w_norm = w_k / (sum_w[tok] + 1e-09)
            slot = flat_e * cap + pos
            slot_safe = jnp.where(keep, slot, E * cap)
            expert_in = jnp.zeros((E * cap, d), xf.dtype).at[slot_safe].set(xf[tok], mode='drop').reshape(E, cap, d)
            h = jax.nn.gelu(jnp.einsum('ecd,edf->ecf', expert_in, W1) + b1[:, None, :], approximate=False)
            expert_out = (jnp.einsum('ecf,efd->ecd', h, W2) + b2[:, None, :]).reshape(E * cap, d)
            contrib = expert_out[jnp.where(keep, slot, 0)]
            y = jnp.zeros((N, d), xf.dtype).at[tok].add(contrib * w_norm[:, None])
            return y.reshape(orig)
        key = jax.random.key(seed)
        ks = jax.random.split(key, 5)
        s = lambda k, sh, sc: jax.random.normal(k, sh, jnp.float32) * sc
        return {'x': jax.random.normal(ks[0], (8, 512, D), jnp.float32), 'Wr': s(ks[1], (D, E), 1.0 / math.sqrt(D)), 'br': jnp.zeros((E,), jnp.float32), 'W1': s(ks[2], (E, D, DFF), 1.0 / math.sqrt(D)), 'b1': jnp.zeros((E, DFF), jnp.float32), 'W2': s(ks[3], (E, DFF, D), 1.0 / math.sqrt(DFF)), 'b2': jnp.zeros((E, D), jnp.float32)}
    _L2_ffn_all = _L2_ffn_setup()
    _L2_ffn_in = {k: v for k, v in _L2_ffn_all.items() if k in ('Wr', 'br', 'W1', 'b1', 'W2', 'b2')}
    del _L2_ffn_all

    def _L3_gnn_setup():
        import jax, jax.numpy as jnp
        import numpy as np
        DIM = 512
        NUM_REL = 4
        N_NODES = 6250
        N_EDGES = 20000

        def _layer_norm(x, g, b, eps=1e-05):
            mu = jnp.mean(x, axis=-1, keepdims=True)
            var = jnp.mean((x - mu) ** 2, axis=-1, keepdims=True)
            return (x - mu) * jax.lax.rsqrt(var + eps) * g + b
        key = jax.random.key(seed)
        ks = jax.random.split(key, 16)
        s = 1.0 / np.sqrt(DIM)
        inp = {'x': jax.random.normal(ks[0], (N_NODES, DIM), jnp.float32), 'edge_index': jax.random.randint(ks[1], (2, N_EDGES), 0, N_NODES, jnp.int32), 'edge_type': jax.random.randint(ks[2], (N_EDGES,), 0, NUM_REL, jnp.int32), 'edge_weight': jax.random.uniform(ks[3], (N_EDGES,), jnp.float32), 'W_self': jax.random.uniform(ks[4], (DIM, DIM), jnp.float32, -s, s), 'b_self': jnp.zeros((DIM,), jnp.float32), 'W_rel': jax.random.uniform(ks[5], (NUM_REL, DIM, DIM), jnp.float32, -s, s), 'b_rel': jnp.zeros((NUM_REL, DIM), jnp.float32), 'ln1_g': jnp.ones((DIM,), jnp.float32), 'ln1_b': jnp.zeros((DIM,), jnp.float32), 'ln2_g': jnp.ones((DIM,), jnp.float32), 'ln2_b': jnp.zeros((DIM,), jnp.float32), 'W_ffn1': jax.random.uniform(ks[6], (DIM, 2 * DIM), jnp.float32, -s, s), 'b_ffn1': jnp.zeros((2 * DIM,), jnp.float32), 'W_ffn2': jax.random.uniform(ks[7], (2 * DIM, DIM), jnp.float32, -1.0 / np.sqrt(2 * DIM), 1.0 / np.sqrt(2 * DIM)), 'b_ffn2': jnp.zeros((DIM,), jnp.float32)}
        return inp
    _L3_gnn_all = _L3_gnn_setup()
    _L3_gnn_in = {k: v for k, v in _L3_gnn_all.items() if k in ('W_self', 'b_self', 'W_rel', 'b_rel', 'ln1_g', 'ln1_b', 'ln2_g', 'ln2_b', 'W_ffn1', 'b_ffn1', 'W_ffn2', 'b_ffn2')}
    del _L3_gnn_all

    def _L3_ffn_setup():
        import jax, jax.numpy as jnp
        import numpy as np
        SINKHORN_ITERS = 8
        TEMPERATURE = 1.0
        EPS = 1e-10

        def sinkhorn(gates):
            t = jnp.log(jnp.clip(gates, EPS)) / TEMPERATURE

            def body(t, _):
                t = t - jax.nn.logsumexp(t, axis=-2, keepdims=True)
                t = t - jax.nn.logsumexp(t, axis=-1, keepdims=True)
                return (t, None)
            t, _ = jax.lax.scan(body, t, None, length=SINKHORN_ITERS)
            return jnp.exp(t)
        key = jax.random.key(seed)
        k1, k2, k3 = jax.random.split(key, 3)
        b, n, d, e, h = (4, 1024, 512, 8, 1)
        x = jax.random.normal(k1, (b, n, d), dtype=jnp.float32)
        gate_w = jax.random.normal(k2, (h, d, e), dtype=jnp.float32)
        experts = jax.random.normal(k3, (e, d, d), dtype=jnp.float32) / np.sqrt(d)
        return {'x': x, 'gate_w': gate_w, 'experts': experts}
    _L3_ffn_all = _L3_ffn_setup()
    _L3_ffn_in = {k: v for k, v in _L3_ffn_all.items() if k in ('gate_w', 'experts')}
    del _L3_ffn_all
    return {'x': x, 'src': src, 'dst': dst, 'edge_attr_64': edge_attr_64, 'edge_type_4': edge_type_4, 'edge_weight': edge_weight, 'L0_gnn_Wv': _L0_gnn_in['Wv'], 'L0_gnn_bv': _L0_gnn_in['bv'], 'L0_gnn_Ww': _L0_gnn_in['Ww'], 'L0_gnn_bw': _L0_gnn_in['bw'], 'L0_gnn_Wa': _L0_gnn_in['Wa'], 'L0_gnn_ba': _L0_gnn_in['ba'], 'L0_gnn_gamma': _L0_gnn_in['gamma'], 'L0_gnn_beta': _L0_gnn_in['beta'], 'L0_ffn_Wg': _L0_ffn_in['Wg'], 'L0_ffn_bg': _L0_ffn_in['bg'], 'L0_ffn_W1': _L0_ffn_in['W1'], 'L0_ffn_b1': _L0_ffn_in['b1'], 'L0_ffn_W2': _L0_ffn_in['W2'], 'L0_ffn_b2': _L0_ffn_in['b2'], 'L1_gnn_W1': _L1_gnn_in['W1'], 'L1_gnn_b1': _L1_gnn_in['b1'], 'L1_gnn_W2': _L1_gnn_in['W2'], 'L1_gnn_b2': _L1_gnn_in['b2'], 'L1_gnn_W3': _L1_gnn_in['W3'], 'L1_gnn_b3': _L1_gnn_in['b3'], 'L1_gnn_W4': _L1_gnn_in['W4'], 'L1_gnn_b4': _L1_gnn_in['b4'], 'L1_gnn_gamma': _L1_gnn_in['gamma'], 'L1_gnn_beta': _L1_gnn_in['beta'], 'L1_ffn_w_gate': _L1_ffn_in['w_gate'], 'L1_ffn_w_up': _L1_ffn_in['w_up'], 'L1_ffn_w_down': _L1_ffn_in['w_down'], 'L2_gnn_Ws': _L2_gnn_in['Ws'], 'L2_gnn_Wb': _L2_gnn_in['Wb'], 'L2_gnn_a_w': _L2_gnn_in['a_w'], 'L2_gnn_a_b': _L2_gnn_in['a_b'], 'L2_ffn_Wr': _L2_ffn_in['Wr'], 'L2_ffn_br': _L2_ffn_in['br'], 'L2_ffn_W1': _L2_ffn_in['W1'], 'L2_ffn_b1': _L2_ffn_in['b1'], 'L2_ffn_W2': _L2_ffn_in['W2'], 'L2_ffn_b2': _L2_ffn_in['b2'], 'L3_gnn_W_self': _L3_gnn_in['W_self'], 'L3_gnn_b_self': _L3_gnn_in['b_self'], 'L3_gnn_W_rel': _L3_gnn_in['W_rel'], 'L3_gnn_b_rel': _L3_gnn_in['b_rel'], 'L3_gnn_ln1_g': _L3_gnn_in['ln1_g'], 'L3_gnn_ln1_b': _L3_gnn_in['ln1_b'], 'L3_gnn_ln2_g': _L3_gnn_in['ln2_g'], 'L3_gnn_ln2_b': _L3_gnn_in['ln2_b'], 'L3_gnn_W_ffn1': _L3_gnn_in['W_ffn1'], 'L3_gnn_b_ffn1': _L3_gnn_in['b_ffn1'], 'L3_gnn_W_ffn2': _L3_gnn_in['W_ffn2'], 'L3_gnn_b_ffn2': _L3_gnn_in['b_ffn2'], 'L3_ffn_gate_w': _L3_ffn_in['gate_w'], 'L3_ffn_experts': _L3_ffn_in['experts']}

def reference(x, src, dst, edge_attr_64, edge_type_4, edge_weight, L0_gnn_Wv, L0_gnn_bv, L0_gnn_Ww, L0_gnn_bw, L0_gnn_Wa, L0_gnn_ba, L0_gnn_gamma, L0_gnn_beta, L0_ffn_Wg, L0_ffn_bg, L0_ffn_W1, L0_ffn_b1, L0_ffn_W2, L0_ffn_b2, L1_gnn_W1, L1_gnn_b1, L1_gnn_W2, L1_gnn_b2, L1_gnn_W3, L1_gnn_b3, L1_gnn_W4, L1_gnn_b4, L1_gnn_gamma, L1_gnn_beta, L1_ffn_w_gate, L1_ffn_w_up, L1_ffn_w_down, L2_gnn_Ws, L2_gnn_Wb, L2_gnn_a_w, L2_gnn_a_b, L2_ffn_Wr, L2_ffn_br, L2_ffn_W1, L2_ffn_b1, L2_ffn_W2, L2_ffn_b2, L3_gnn_W_self, L3_gnn_b_self, L3_gnn_W_rel, L3_gnn_b_rel, L3_gnn_ln1_g, L3_gnn_ln1_b, L3_gnn_ln2_g, L3_gnn_ln2_b, L3_gnn_W_ffn1, L3_gnn_b_ffn1, L3_gnn_W_ffn2, L3_gnn_b_ffn2, L3_ffn_gate_w, L3_ffn_experts):
    import jax
    import jax.numpy as jnp

    def _L0_gnn_ref(x, edges, Wv, bv, Ww, bw, Wa, ba, gamma, beta):
        import jax, jax.numpy as jnp
        import numpy as np
        N = 384
        HID = 512
        H = 8
        HD = HID // H
        E = 12288
        LN_EPS = 1e-05
        residual = x
        n = x.shape[0]
        out = (x @ Wv + bv).reshape(n, H, HD).transpose(1, 0, 2)
        x1 = x[edges[0]]
        x2 = x[edges[1]]
        e = jnp.concatenate([x1, x2], axis=1) @ Ww + bw
        e = e.reshape(-1, H, 2 * HD).transpose(1, 0, 2)
        e = jax.nn.leaky_relu(e, 0.01)
        w = (e @ Wa + ba)[..., 0]
        mat = jnp.full((H, n, n), -jnp.inf, jnp.float32)
        mat = mat.at[:, edges[0], edges[1]].set(w)
        mat = jax.nn.softmax(mat, axis=-1)
        mat = jnp.nan_to_num(mat)
        y = jnp.matmul(mat, out).transpose(1, 0, 2)
        y = jax.nn.elu(y).reshape(n, HID) + residual
        mu = jnp.mean(y, axis=-1, keepdims=True)
        var = jnp.var(y, axis=-1, keepdims=True)
        y = (y - mu) / jnp.sqrt(var + LN_EPS) * gamma + beta
        return y

    def _L0_ffn_ref(x, Wg, bg, W1, b1, W2, b2):
        import jax, jax.numpy as jnp
        import numpy as np
        B, S, D, DFF, E, K = (4, 256, 512, 1024, 8, 2)
        n_experts = W1.shape[0]
        logits = jnp.einsum('bsd,de->bse', x, Wg) + bg
        topk_vals, topk_idx = jax.lax.top_k(logits, K)
        topk_w = jax.nn.softmax(topk_vals, axis=-1)
        one_hot = jax.nn.one_hot(topk_idx, n_experts, dtype=x.dtype)
        weights_per_expert = jnp.einsum('bske,bsk->bse', one_hot, topk_w)
        h = jnp.einsum('bsd,edf->bsef', x, W1) + b1
        a, g = jnp.split(h, 2, axis=-1)
        act = jax.nn.silu(a) * g
        expert_out = jnp.einsum('bsef,efd->bsed', act, W2) + b2
        return jnp.einsum('bse,bsed->bsd', weights_per_expert, expert_out)

    def _L1_gnn_ref(x, edge_index, edge_attr, W1, b1, W2, b2, W3, b3, W4, b4, gamma, beta):
        import jax, jax.numpy as jnp
        import numpy as np
        N_NODES = 2500
        N_EDGES = 40000
        HIDDEN = 512
        EDGE_DIM = 64
        LN_EPS = 1e-05

        def mish(x):
            return x * jnp.tanh(jax.nn.softplus(x))
        src, dst = (edge_index[0], edge_index[1])
        edge_feat = jnp.concatenate([x[src], x[dst], edge_attr], axis=-1)
        h = mish(edge_feat @ W1 + b1)
        messages = mish(h @ W2 + b2)
        agg = jax.ops.segment_sum(messages, dst, num_segments=x.shape[0])
        u = mish(jnp.concatenate([x, agg], axis=-1) @ W3 + b3)
        out = u @ W4 + b4
        y = x + out
        mu = jnp.mean(y, axis=-1, keepdims=True)
        var = jnp.mean(jnp.square(y - mu), axis=-1, keepdims=True)
        return (y - mu) * jax.lax.rsqrt(var + LN_EPS) * gamma + beta

    def _L1_ffn_ref(x, w_gate, w_up, w_down):
        import jax, jax.numpy as jnp
        import numpy as np
        DIM = 512
        FFN_DIM = 1408
        GROUP = 128
        EPS = 1e-05

        def _quantize_weight(w, group_size):
            o, i = w.shape
            wg = w.reshape(o, i // group_size, group_size)
            scale = jnp.mean(jnp.abs(wg), axis=-1, keepdims=True) + EPS
            wq = jnp.clip(jnp.round(wg / scale), -1.0, 1.0) * scale
            return wq.reshape(o, i)

        def _bitlinear(x, w, group_size=GROUP):
            wq = w + jax.lax.stop_gradient(_quantize_weight(w, group_size) - w)
            return jnp.einsum('bsd,fd->bsf', x, wq)
        gate = _bitlinear(x, w_gate)
        up = _bitlinear(x, w_up)
        h = jax.nn.silu(gate) * up
        return _bitlinear(h, w_down)

    def _L2_gnn_ref(x, edge_index, Ws, Wb, a_w, a_b):
        import jax, jax.numpy as jnp
        import numpy as np
        N, E, H, D_IN, D_PRIME = (6250, 100000, 8, 512, 64)

        def _segment_softmax(scores, seg, num_segments):
            smax = jax.ops.segment_max(scores, seg, num_segments=num_segments)
            ex = jnp.exp(scores - smax[seg])
            denom = jax.ops.segment_sum(ex, seg, num_segments=num_segments)
            return ex / denom[seg]
        v_src, v_tgt = (edge_index[0], edge_index[1])
        n = x.shape[0]
        outs = []
        for h in range(Ws.shape[0]):
            Wx = x @ Ws[h] + Wb[h]
            d = Wx.shape[-1]
            s = Wx[v_tgt] @ a_w[h, :d] + Wx[v_src] @ a_w[h, d:] + a_b[h]
            s = jax.nn.leaky_relu(s, negative_slope=0.2)
            alpha = _segment_softmax(s, v_tgt, n)
            outs.append(jax.ops.segment_sum(alpha[:, None] * Wx[v_src], v_tgt, num_segments=n))
        return jnp.stack(outs, axis=1).reshape(n, -1)

    def _L2_ffn_ref(x, Wr, br, W1, b1, W2, b2):
        import jax, jax.numpy as jnp
        import numpy as np
        import math
        E, K, CAPF = (8, 2, 1.25)
        D, DFF = (512, 256)

        def _moe(x, Wr, br, W1, b1, W2, b2):
            orig = x.shape
            d = orig[-1]
            xf = x.reshape(-1, d)
            N = xf.shape[0]
            logits = xf @ Wr + br
            probs = jax.nn.softmax(logits, axis=-1)
            topk_p, topk_i = jax.lax.top_k(probs, K)
            topk_w = topk_p / (jnp.sum(topk_p, axis=-1, keepdims=True) + 1e-09)
            cap = max(1, int(math.ceil(CAPF * float(N * K) / float(E))))
            flat_e = topk_i.reshape(-1)
            flat_w = topk_w.reshape(-1)
            tok = jnp.repeat(jnp.arange(N), K)
            one_hot = jax.nn.one_hot(flat_e, E, dtype=xf.dtype)
            pos = (jnp.cumsum(one_hot, axis=0) - one_hot)[jnp.arange(N * K), flat_e]
            pos = pos.astype(jnp.int32)
            keep = pos < cap
            w_k = jnp.where(keep, flat_w, 0.0)
            sum_w = jnp.zeros((N,), xf.dtype).at[tok].add(w_k)
            w_norm = w_k / (sum_w[tok] + 1e-09)
            slot = flat_e * cap + pos
            slot_safe = jnp.where(keep, slot, E * cap)
            expert_in = jnp.zeros((E * cap, d), xf.dtype).at[slot_safe].set(xf[tok], mode='drop').reshape(E, cap, d)
            h = jax.nn.gelu(jnp.einsum('ecd,edf->ecf', expert_in, W1) + b1[:, None, :], approximate=False)
            expert_out = (jnp.einsum('ecf,efd->ecd', h, W2) + b2[:, None, :]).reshape(E * cap, d)
            contrib = expert_out[jnp.where(keep, slot, 0)]
            y = jnp.zeros((N, d), xf.dtype).at[tok].add(contrib * w_norm[:, None])
            return y.reshape(orig)
        return _moe(x, Wr, br, W1, b1, W2, b2)

    def _L3_gnn_ref(x, edge_index, edge_type, edge_weight, W_self, b_self, W_rel, b_rel, ln1_g, ln1_b, ln2_g, ln2_b, W_ffn1, b_ffn1, W_ffn2, b_ffn2):
        import jax, jax.numpy as jnp
        import numpy as np
        DIM = 512
        NUM_REL = 4
        N_NODES = 6250
        N_EDGES = 20000

        def _layer_norm(x, g, b, eps=1e-05):
            mu = jnp.mean(x, axis=-1, keepdims=True)
            var = jnp.mean((x - mu) ** 2, axis=-1, keepdims=True)
            return (x - mu) * jax.lax.rsqrt(var + eps) * g + b
        n = x.shape[0]
        src, dst = (edge_index[0], edge_index[1])
        xs = x[src]
        total_msg = jnp.zeros_like(xs)
        for r in range(NUM_REL):
            w_r = jnp.where(edge_type == r, edge_weight, 0.0)
            total_msg = total_msg + (xs @ W_rel[r] + b_rel[r]) * w_r[:, None]
        agg = jax.ops.segment_sum(total_msg, dst, num_segments=n)
        deg = jax.ops.segment_sum(edge_weight, dst, num_segments=n)
        agg = agg / jnp.maximum(deg, 1.0)[:, None]
        h = x @ W_self + b_self + agg
        x1 = _layer_norm(x + h, ln1_g, ln1_b)
        ffn = jax.nn.gelu(x1 @ W_ffn1 + b_ffn1, approximate=False) @ W_ffn2 + b_ffn2
        out = _layer_norm(x1 + ffn, ln2_g, ln2_b)
        return out

    def _L3_ffn_ref(x, gate_w, experts):
        import jax, jax.numpy as jnp
        import numpy as np
        SINKHORN_ITERS = 8
        TEMPERATURE = 1.0
        EPS = 1e-10

        def sinkhorn(gates):
            t = jnp.log(jnp.clip(gates, EPS)) / TEMPERATURE

            def body(t, _):
                t = t - jax.nn.logsumexp(t, axis=-2, keepdims=True)
                t = t - jax.nn.logsumexp(t, axis=-1, keepdims=True)
                return (t, None)
            t, _ = jax.lax.scan(body, t, None, length=SINKHORN_ITERS)
            return jnp.exp(t)
        b, n, d = x.shape
        h = gate_w.shape[0]
        e = experts.shape[0]
        N = b * n
        m = n // e
        x4 = x[:, None]
        gates = jnp.einsum('bhnd,hde->bhne', x4, gate_w)
        xf = jnp.transpose(x4, (1, 0, 2, 3)).reshape(h, N, d)
        gf = jnp.transpose(gates, (1, 0, 2, 3)).reshape(h, N, e)
        cg = sinkhorn(gf)
        vals, idx = jax.lax.top_k(jnp.transpose(cg, (0, 2, 1)), m)
        gate_values = (vals > 0.5).astype(x.dtype)
        gate_values = jnp.transpose(gate_values, (0, 2, 1))
        idx = jnp.transpose(idx, (0, 2, 1))
        routed = xf[jnp.arange(h)[:, None, None], idx]
        outputs = jnp.einsum('hmei,eio->hmeo', routed, experts)
        outputs = outputs * gate_values[..., None]
        o_dim = outputs.shape[-1]
        src = outputs.reshape(h, m * e, o_dim)
        idx_flat = idx.reshape(h, m * e)

        def combine(idxf, srcf):
            s = jnp.zeros((N, o_dim), srcf.dtype).at[idxf].add(srcf)
            c = jnp.zeros((N,), srcf.dtype).at[idxf].add(1.0)
            return s / (c + 1.0)[:, None]
        out = jax.vmap(combine)(idx_flat, src)
        out = out.reshape(h, b, n, o_dim)
        out = jnp.transpose(out, (1, 0, 2, 3))[:, 0]
        return out
    edge_index = jnp.stack([src, dst])
    x = x + _L0_gnn_ref(_layernorm(x, axis=-1), edge_index, L0_gnn_Wv, L0_gnn_bv, L0_gnn_Ww, L0_gnn_bw, L0_gnn_Wa, L0_gnn_ba, L0_gnn_gamma, L0_gnn_beta)
    x = x + _L0_ffn_ref(_layernorm(x, axis=-1)[None], L0_ffn_Wg, L0_ffn_bg, L0_ffn_W1, L0_ffn_b1, L0_ffn_W2, L0_ffn_b2)[0]
    x = x + _L1_gnn_ref(_layernorm(x, axis=-1), edge_index, edge_attr_64, L1_gnn_W1, L1_gnn_b1, L1_gnn_W2, L1_gnn_b2, L1_gnn_W3, L1_gnn_b3, L1_gnn_W4, L1_gnn_b4, L1_gnn_gamma, L1_gnn_beta)
    x = x + _L1_ffn_ref(_layernorm(x, axis=-1)[None], L1_ffn_w_gate, L1_ffn_w_up, L1_ffn_w_down)[0]
    x = x + _L2_gnn_ref(_layernorm(x, axis=-1), edge_index, L2_gnn_Ws, L2_gnn_Wb, L2_gnn_a_w, L2_gnn_a_b)
    x = x + _L2_ffn_ref(_layernorm(x, axis=-1)[None], L2_ffn_Wr, L2_ffn_br, L2_ffn_W1, L2_ffn_b1, L2_ffn_W2, L2_ffn_b2)[0]
    x = x + _L3_gnn_ref(_layernorm(x, axis=-1), edge_index, edge_type_4, edge_weight, L3_gnn_W_self, L3_gnn_b_self, L3_gnn_W_rel, L3_gnn_b_rel, L3_gnn_ln1_g, L3_gnn_ln1_b, L3_gnn_ln2_g, L3_gnn_ln2_b, L3_gnn_W_ffn1, L3_gnn_b_ffn1, L3_gnn_W_ffn2, L3_gnn_b_ffn2)
    x = x + _L3_ffn_ref(_layernorm(x, axis=-1)[None], L3_ffn_gate_w, L3_ffn_experts)[0]
    return x

_drawn_inputs = setup_inputs


def setup_inputs(seed=0):
    import zlib

    import numpy as np

    out = dict(_drawn_inputs(seed))
    spreads = {'L0_gnn_gamma': (1.0, 0.2),
     'L0_gnn_beta': (0.0, 0.1),
     'L0_ffn_bg': (0.0, 0.346),
     'L0_ffn_b1': (0.0, 0.481),
     'L0_ffn_b2': (0.0, 0.1),
     'L1_gnn_b1': (0.0, 0.1),
     'L1_gnn_b2': (0.0, 0.1),
     'L1_gnn_b3': (0.0, 0.291),
     'L1_gnn_b4': (0.0, 0.1),
     'L1_gnn_gamma': (1.0, 0.2),
     'L1_gnn_beta': (0.0, 0.1),
     'L2_ffn_br': (0.0, 0.1),
     'L2_ffn_b1': (0.0, 0.299),
     'L2_ffn_b2': (0.0, 0.1),
     'L3_gnn_b_self': (0.0, 0.269),
     'L3_gnn_b_rel': (0.0, 0.473),
     'L3_gnn_ln1_g': (1.0, 0.2),
     'L3_gnn_ln1_b': (0.0, 0.1),
     'L3_gnn_ln2_g': (1.0, 0.2),
     'L3_gnn_ln2_b': (0.0, 0.1),
     'L3_gnn_b_ffn1': (0.0, 0.464),
     'L3_gnn_b_ffn2': (0.0, 0.1)}
    factors = {'L0_gnn_Ww': 3.035, 'L0_gnn_bw': 38.661, 'L0_gnn_Wa': 3.567, 'L2_gnn_a_b': 20.848}
    for name, (base, spread) in spreads.items():
        noise = np.random.default_rng([zlib.crc32(name.encode()), seed]).standard_normal(out[name].shape)
        drawn = base * np.exp(spread * noise) if base else spread * noise
        out[name] = jnp.asarray(drawn.astype(out[name].dtype))
    for name, factor in factors.items():
        out[name] = (out[name] * factor).astype(out[name].dtype)
    return out
```

```python
from contextlib import ExitStack

import concourse.bass as bass
from concourse import mybir

F32 = mybir.dt.float32
F32R = mybir.dt.float32r
BF16 = mybir.dt.bfloat16
I32 = mybir.dt.int32
ALU = mybir.AluOpType
ACT = mybir.ActivationFunctionType
AX = mybir.AxisListType

P = 128
NODES, DIM, EDGES = 384, 512, 6144
NT, KT = NODES // P, DIM // P
ET = EDGES // P
BLK = 512
NB, SUB = EDGES // BLK, BLK // P
HEADS, HD = 8, 64
EPS = 1e-5
NONE = -3e38
FF0, FF1 = 1024, 1408
JT0, JT1, JT2 = FF0 // P, FF1 // P, 2
EXPERTS = 8
CAP = 120
TOP = NODES // EXPERTS
SINKHORN = 8
SLOTS, SW = 6, 1024
RING = 8

MISH = 4 + 8 * (NB - 1) + 4
N_SMALL = 15

UP0, UP1 = 0, EXPERTS * JT0
UP2 = UP1 + JT1
UP3 = UP2 + EXPERTS * JT2
ADD0, ADD1 = NT, NT + EXPERTS * NT
ADD2 = ADD1 + NT + NT
ADD3 = ADD2 + EXPERTS * NT
ADDED = ADD3 + EXPERTS * NT


class Steps:

    def __init__(self, engine, own):
        self.engine, self.own, self.base, self.local, self.per, self.i = engine, own, {}, {}, {}, None

    def __call__(self, instruction, sem=None):
        sem = sem or self.own
        instruction.then_inc(sem, 1)
        key = sem.name
        self.local[key] = self.local.get(key, 0) + 1
        value = self.base.get(key, 0) + self.local[key]
        if self.i is not None:
            value = self.i * self.per[key] + value
        self.engine.wait_ge(sem, value)

    def fold(self):
        for key, n in self.local.items():
            self.base[key] = self.base.get(key, 0) + n
        self.local = {}

    def skip(self, sem, n):
        self.base[sem.name] = self.base.get(sem.name, 0) + n

    def enter(self, i, per):
        self.fold()
        self.i, self.per = i, {s.name: n for s, n in per.items()}

    def leave(self, iterations):
        for key, n in self.local.items():
            assert n == self.per[key], (key, n, self.per[key])
            self.base[key] = self.base.get(key, 0) + iterations * n
        self.local, self.i = {}, None


def build(nc, a, out, table0, table3):
    with ExitStack() as ctx:
        def sb(name, shape, dt=F32, within=None):
            return (within or ctx).enter_context(nc.sbuf_tensor(name, shape, dt))

        def sem(name):
            return ctx.enter_context(nc.semaphore(name))

        bank = [ctx.enter_context(nc.psum_tensor(f"bank{i}", [P, 512], F32)) for i in range(8)]

        x = sb("x", [P, NT, DIM])
        xn = sb("xn", [P, NT, DIM])
        xT = sb("xT", [P, KT, NODES])
        hold = sb("hold", [P, 3, NT * DIM])
        y = hold[:, 0, :].rearrange("p (t d) -> p t d", t=NT)
        vn = hold[:, 1, :].rearrange("p (t d) -> p t d", t=NT)
        yT = hold[:, 2, :].rearrange("p (k n) -> p k n", k=KT)
        hT = hold[:, :, :].rearrange("p a b -> p (a b)")[:, 0:4096].rearrange("p (a f n) -> p a f n", a=2, f=KT)
        tmp = sb("tmp", [P, 2, DIM])
        wring = sb("wring", [P, SLOTS, SW])
        rows = sb("rows", [P, 6, DIM])
        count = sb("count", [P, NT, NODES])
        stats = sb("stats", [P, 6])
        mv = sb("mv", [P, NT, 2])
        varp = sb("varp", [P, NT])
        rstd = sb("rstd", [P, NT])
        half = sb("half", [P, NT])
        two = sb("two", [P, 1])
        ident = sb("ident", [P, P])
        zeros = sb("zeros", [P, P])
        ones = sb("ones", [P, P])
        upper = sb("upper", [P, P])
        nodeid = sb("nodeid", [P, NT])
        iota = sb("iota", [P, NODES])
        sel8 = sb("sel8", [8, 8, P])
        low8 = sb("low8", [P, 8, 8])
        srcc = sb("srcc", [P, ET], I32)
        dstc = sb("dstc", [P, ET], I32)
        typc = sb("typc", [P, ET], I32)
        ewc = sb("ewc", [P, ET])
        srcf = sb("srcf", [P, ET])
        dstf = sb("dstf", [P, ET])
        pair = sb("pair", [P, ET], I32)
        rrow = sb("rrow", [P, ET], I32)
        logit = sb("logit", [P, ET, HEADS])
        ba = sb("ba", [P, 1])
        wa = sb("wa", [P, 1])
        ab = sb("ab", [P, 8])
        b1e0 = sb("b1e0", [P, EXPERTS, 2 * JT0])
        b1e2 = sb("b1e2", [P, EXPERTS, JT2])
        b2e = sb("b2e", [8, 2, DIM])
        b3c = sb("b3c", [P, KT])
        bf1 = sb("bf1", [P, 8])
        gatew = sb("gatew", [P, 3, KT, 8])
        br = sb("br", [P, 2, 8])
        w1c = sb("w1c", [64, DIM])
        small = sb("small", [P, 8, NT * 8])
        small1 = sb("small1", [P, 4, NT])
        cmp8 = sb("cmp8", [P, 2, NT * 8, 8])
        coef = sb("coef", [P, NT, 8])
        coefT = sb("coefT", [8, NODES])
        mneg = sb("mneg", [P, NT, HEADS])
        den = sb("den", [P, NT, HEADS])
        pq = sb("pq", [P, 2, NT, HEADS])
        eidx = sb("eidx", [P, 2, BLK], I32)

        with ExitStack() as third:
            eh = sb("eh", [P, 2, NT, NODES], within=third)
            eT = sb("eT", [P, 2, NT, NODES], within=third)
            sink = sb("sink", [8, 5, NODES], within=third)
            sinks = sb("sinks", [8, 8], within=third)
            sinka = sb("sinka", [P, 6, NT, 8], within=third)
        with ExitStack() as second:
            tabs1 = sb("tabs1", [P, 2, 2, NT, 512], F32R, within=second)
            em = sb("em", [P, SUB, NODES], F32R, within=second)
            mh = sb("mh", [P, SUB, DIM], F32R, within=second)
            ml = sb("ml", [P, SUB, DIM], F32R, within=second)
        tabs0 = sb("tabs0", [P, 2, 2, NT, 1024], F32R)
        with ExitStack() as second:
            big = sb("big", [P, NT, NODES * HEADS], within=second)
            wdeg = sb("wdeg", [P, ET, 2], F32R, within=second)
        onehot = sb("onehot", [P, 2, 2, NT, BLK], F32R)
        work = sb("work", [P, 3, 4, 512])
        attr = sb("attr", [64, 2, BLK])
        relu4, leaky4 = work[:, 0, :, :], work[:, 1, :, :]
        ebf = work[:, 2, :, :].rearrange("p a b -> p (a b)")[:, 0:1536].bitcast(BF16).rearrange(
            "p (s c n) -> p s c n", s=SUB, c=2)
        mz, mt, mr = work[:, 0, :, :], work[:, 1, :, :], work[:, 2, :, :]
        bigf = big[:, :, :].rearrange("p a b -> p (a b)")
        silu2 = bigf[:, 0:768].rearrange("p (a n) -> p a n", a=2)
        act2 = bigf[:, 768:1536].rearrange("p (a n) -> p a n", a=2)
        qraw = bigf[:, 1536:4608].rearrange("p (a c n) -> p a c n", a=2, c=3)
        qa = bigf[:, 4608:6144]
        qb = bigf[:, 6144:7680]
        qs = cmp8[:, 0, 0:12, 0:3]
        gather = bigf[:, 0:4096].rearrange("p (a n) -> p a n", a=RING)
        stage = bigf[:, 0:6144].rearrange("p (a n) -> p a n", a=4 * NT)
        brel = bigf[:, 7168:9216].rearrange("p (a n) -> p a n", a=4)
        hidT = bigf[:, 0:3072].rearrange("p (f n) -> p f n", f=8)
        msg4 = bigf[:, 4096:6144].rearrange("p (a n) -> p a n", a=4)
        negm = bigf[:, 0:1152].rearrange("p (t n) -> p t n", t=NT)
        srow = bigf[:, 1152:2304].rearrange("p (a n) -> p a n", a=3)
        qT2 = bigf[0:8, 2304:2688]
        prod = bigf[:, 3072:3584]
        qT = hold[:, :, :].rearrange("p a b -> p (a b)")[:, 0:3072].rearrange("p (a c n) -> p a c n", a=2, c=3)

        dve_s, act_s, pool_s = sem("dve_step"), sem("act_step"), sem("pool_step")
        arrive = [sem(f"slot{i}_loaded") for i in range(SLOTS)]
        x_loaded, edges_loaded, small_loaded, rows_loaded = map(sem, ("x_loaded", "edges_loaded", "small_loaded", "rows_loaded"))
        consts_ready, none_ready = sem("consts_ready"), sem("none_ready")
        var_ready, rstd_ready = sem("variance_ready"), sem("deviation_ready")
        nodes_ready, turned, xT_a, xT_v = sem("nodes_ready"), sem("nodes_turned"), sem("xT_act_half"), sem("xT_dve_half")
        value_g, v_ready = sem("value_product"), sem("value_ready")
        table_g, tab_sum, tab_hi, tab_lo = sem("table_product"), sem("table_sum"), sem("table_high"), sem("table_low")
        ix_loaded, at_loaded = sem("block_index_loaded"), [sem("attr_loaded0"), sem("attr_loaded1")]
        oh_ready, em_ready = sem("onehot_ready"), sem("edge_onehot_ready")
        z_g, relu_r, leaky_r, logit_g, logit_r = map(sem, ("z_product", "relu_ready", "leaky_ready", "logit_product", "logit_ready"))
        count_g = sem("count_product")
        pairs_r, filled, written, big_loaded = map(sem, ("pair_rows_ready", "table0_filled", "table0_written", "pair_logits_loaded"))
        max_r, score_r, e_ready, e_turned, eT_ready, y_g = map(sem, ("row_max_ready", "score_ready", "weight_ready", "weight_turned", "weightT_ready", "attention_product"))
        elu_in, elu_ex = sem("elu_input"), sem("elu_exp")
        route_g, route_d, route_a, coefT_g, coefT_r, b2_g = map(sem, ("router_product", "router_dve", "router_act", "coef_turned", "coefT_ready", "expert_bias_product"))
        up_g, silu_r, hid_r, down_g, added = map(sem, ("up_product", "silu_ready", "hidden_ready", "down_product", "down_added"))
        mish_g, mish_in, mish_ex, mish_sq, mish_rc, mish_q, mish_r = map(sem, ("mish_product", "mish_input", "mish_exp", "mish_square", "mish_reciprocal", "mish_ratio", "mish_ready"))
        msg_hi, msg_lo, agg_g = sem("message_high"), sem("message_low"), sem("aggregate_product")
        node_g, node_r = sem("node_product"), sem("node_result")
        q_loaded, quant_r, q_turned, qT_a, qT_v = [sem("quant_raw_loaded0"), sem("quant_raw_loaded1")], sem("quantized"), sem("quantized_turned"), sem("quantizedT_act"), sem("quantizedT_dve")
        pq_r, pqT_g, pqT_r, srow_g = sem("score_parts_ready"), sem("score_parts_turned"), sem("score_partsT_ready"), sem("score_row_product")
        rel_g, rel_r, rel_w = sem("relation_product"), sem("relation_staged"), sem("relation_written")
        gathered = [sem(f"messages_gathered{i}") for i in range(RING)]
        m_used = sem("scaled_messages_used")
        sk_d, sk_a, sk_p = sem("sinkhorn_dve"), sem("sinkhorn_act"), sem("sinkhorn_turned")
        mish_ln, mish_min, exp2_r, brel_loaded, scaled_r, gelu_r, coef_r, quant_s = map(sem, ("mish_log", "mish_clamped", "score_exp_ready", "relation_bias_loaded", "scaled_ready", "gelu_ready", "coef_ready", "quantize_step"))
        mask_r, pos_g = sem("mask_ready"), sem("position_product")
        weighed, wdeg_r, chosen_r = map(sem, ("weighed_ready", "edge_weights_split", "chosen_ready"))
        out_done = sem("out_written")
        row_used = sem("rows_used")

        def wslot(s, k):
            return wring[:, s, :].rearrange("p (k n) -> p k n", k=k)

        def sm(i):
            return small[:, i, :].rearrange("p (t e) -> p t e", t=NT)

        def node_rows(w, c):
            return w[c * 2 * P:(c + 1) * 2 * P, :].rearrange("(k p) n -> p k n", p=P)

        ROWS = [["L0_gnn_bv", "bwa", "bwb", "L0_gnn_gamma", "L0_gnn_beta"],
                ["L1_gnn_b1", "L1_gnn_b2", "L1_gnn_b4", "L1_gnn_gamma", "L1_gnn_beta"],
                ["L2_gnn_Wb", "L2_gnn_at", "L2_gnn_as"],
                ["L3_gnn_b_self", "L3_gnn_ln1_g", "L3_gnn_ln1_b", "L3_gnn_ln2_g", "L3_gnn_ln2_b", "L3_gnn_b_ffn2"]]
        rows_before = [16 * sum(len(r) for r in ROWS[:i + 1]) for i in range(4)]

        def row(layer, name, w=1):
            r = ROWS[layer].index(name)
            return rows[:, r:r + w, :].rearrange("p a b -> p (a b)")

        owner, arrivals, plan, cursor = {}, [0] * SLOTS, [], [0]

        def stream(src, k, freed_by):
            s = cursor[0] % SLOTS
            cursor[0] += 1
            arrivals[s] += 1
            plan.append((s, src, k, owner.get(s)))
            owner[s] = freed_by
            return s, 16 * arrivals[s]

        def reserve(n, uses, freed_by):
            base = [(cursor[0] + i) % SLOTS for i in range(n)]
            cursor[0] += n
            before = [owner[s] for s in base if s in owner], {s: 16 * arrivals[s] for s in base}
            for s in base:
                arrivals[s] += uses
                owner[s] = freed_by
            return base, *before

        W = {}
        for c in range(2):
            W["wv", c] = stream(node_rows(a["L0_gnn_Wv"], c), 2, (value_g, NT))
        for k in range(8):
            W["ww", k] = stream(a["L0_gnn_Ww"][k * P:(k + 1) * P, :].unsqueeze(1), 1, (table_g, 6 if k < 4 else 12))
        f0, f0_before, f0_base = reserve(6, 2 * EXPERTS, (down_g, UP1))
        plan.append("layer0")
        for c in range(4):
            W["w1", c] = stream(node_rows(a["L1_gnn_W1"], c), 2, (table_g, 12 + (3 if c < 2 else 6)))
        for c in range(2):
            W["w2", c] = stream(node_rows(a["L1_gnn_W2"], c), 2, (agg_g, NT))
        plan.append("edges1")
        for c in range(4):
            W["w3", c] = stream(node_rows(a["L1_gnn_W3"], c), 2, (mish_g, MISH + KT))
        for c in range(2):
            W["w4", c] = stream(node_rows(a["L1_gnn_W4"], c), 2, (node_g, NT))
        plan.append("ffn1")
        for c in range(2):
            W["ws", c] = stream(node_rows(a["L2_gnn_Ws"], c), 2, (value_g, 2 * NT))
        f2, f2_before, f2_base = reserve(4, EXPERTS // 2, (down_g, UP3))
        plan.append("ffn2")
        for r in range(4):
            for c in range(2):
                W["wr", r, c] = stream(node_rows(a["L3_gnn_W_rel"][r], c), 2, (rel_g, NT * (r + 1)))
        for c in range(2):
            W["wself", c] = stream(node_rows(a["L3_gnn_W_self"], c), 2, (node_g, 2 * NT))
        for k in range(4):
            W["wf1", k] = stream(a["L3_gnn_W_ffn1"][k * P:(k + 1) * P, :].unsqueeze(1), 1, (node_g, 2 * NT + 8))
        for c in range(4):
            W["wf2", c] = stream(node_rows(a["L3_gnn_W_ffn2"], c), 2, (node_g, 3 * NT + 8))
        f3, f3_before, f3_base = reserve(4, EXPERTS // 2, None)
        plan.append("ffn3")

        def mish_tile(n):
            if n < 4:
                return "z", 0, n
            b, q = divmod(n - 4, 8)
            if b == NB - 1:
                return "m", b, q
            return ("m", b, q - 2) if 2 <= q < 6 else ("z", b + 1, q if q < 2 else q - 4)


        block = ctx.enter_context(nc.Block())

        @block.sync
        def _(sp):
            sp.dma_start(x[:, :, :], a["x"].rearrange("(t p) d -> p t d", p=P)).then_inc(x_loaded, 16)
            for dst, name in ((srcc, "src_c"), (dstc, "dst_c"), (typc, "typ_c"), (ewc, "ew_c")):
                sp.dma_start(dst[:, :], a[name]).then_inc(edges_loaded, 16)

            def load_index(at):
                sp.dma_start(eidx[:, 0, :], a["src"][bass.ds(at, BLK)].partition_broadcast(P)).then_inc(ix_loaded, 16)
                sp.dma_start(eidx[:, 1, :], a["dst"][bass.ds(at, BLK)].partition_broadcast(P)).then_inc(ix_loaded, 16)

            def layer0():
                load_index(0)
                with sp.Fori(1, NB) as b:
                    sp.wait_ge(oh_ready, b)
                    load_index(b * BLK)
                sp.wait_ge(written, 16 * ET)
                sp.wait_ge(count_g, NB)
                for t in range(NT):
                    sp.dma_start(big[:, t, :], table0.rearrange("(t p n) h -> t p (n h)", t=NT, p=P)[t]).then_inc(big_loaded, 16)
                for wait in f0_before:
                    sp.wait_ge(*wait)

                def load(e, j):
                    for q, lo in ((0, 2 * j * P), (1, FF0 + 2 * j * P)):
                        s = f0[(3 * j + q) % 6]
                        sp.dma_start(wslot(s, KT), a["L0_ffn_W1"][e, :, lo:lo + 2 * P].rearrange("(k p) n -> p k n", p=P)).then_inc(arrive[s], 16)
                    s = f0[(3 * j + 2) % 6]
                    sp.dma_start(wslot(s, 2), a["L0_ffn_W2"][e, 2 * j * P:(2 * j + 2) * P, :].rearrange("(k p) n -> p k n", p=P)).then_inc(arrive[s], 16)

                for j in range(JT0 // 2):
                    if j >= 2:
                        sp.wait_ge(down_g, 2 * (j - 1))
                    load(0, j)
                with sp.Fori(1, EXPERTS) as e:
                    for j in range(JT0 // 2):
                        sp.wait_ge(down_g, e * JT0 + 2 * (j - 1))
                        load(e, j)

            def edges1():
                sp.wait_ge(oh_ready, NB)
                sp.wait_ge(added, ADD1)
                load_index(0)
                for u in range(2):
                    sp.dma_start(attr[:, u, :], a["attrT"][:, u * BLK:(u + 1) * BLK]).then_inc(at_loaded[u], 16)
                sp.wait_ge(oh_ready, NB + 1)
                load_index(BLK)
                with sp.Fori(1, NB // 2) as i:
                    for u in range(2):
                        sp.wait_ge(oh_ready, i * 2 + (NB + u))
                        load_index(i * (2 * BLK) + u * BLK)
                        sp.wait_ge(mish_g, i * 16 + 4 + 8 * (u - 2))
                        sp.dma_start(attr[:, u, :], a["attrT"][:, bass.ds(i * (2 * BLK) + u * BLK, BLK)]).then_inc(at_loaded[u], 16)

            def ffn1():
                def load(u, j):
                    sp.dma_start(qraw[:, u, 0, :], a["L1_ffn_w_gate"][bass.ds(j * P, P), :]).then_inc(q_loaded[u], 16)
                    sp.dma_start(qraw[:, u, 1, :], a["L1_ffn_w_up"][bass.ds(j * P, P), :]).then_inc(q_loaded[u], 16)
                    sp.dma_start(qraw[:, u, 2, :].rearrange("p (g n) -> p g n", g=4),
                                 a["L1_ffn_w_down"][:, bass.ds(j * P, P)].rearrange("(g p) n -> p g n", p=P)).then_inc(q_loaded[u], 16)

                sp.wait_ge(node_g, NT)
                load(0, 0)
                load(1, 1)
                with sp.Fori(1, JT1 // 2) as i:
                    for u in range(2):
                        sp.wait_ge(quant_r, i * 2 + (u - 1))
                        load(u, i * 2 + u)
                sp.wait_ge(quant_r, JT1 - 2)
                load(0, JT1 - 1)

            def ffn2():
                def load(e, v):
                    s1, s2 = f2[2 * v], f2[2 * v + 1]
                    sp.dma_start(wslot(s1, KT), a["L2_ffn_W1"][e].rearrange("(k p) n -> p k n", p=P)).then_inc(arrive[s1], 16)
                    sp.dma_start(wslot(s2, 2), a["L2_ffn_W2"][e].rearrange("(k p) n -> p k n", p=P)).then_inc(arrive[s2], 16)

                for wait in f2_before:
                    sp.wait_ge(*wait)
                load(0, 0)
                load(1, 1)
                with sp.Fori(1, EXPERTS // 2) as i:
                    for v in range(2):
                        sp.wait_ge(down_g, i * (2 * JT2) + (UP2 + JT2 * (v - 1)))
                        load(i * 2 + v, v)

            def ffn3():
                def load(e, v):
                    for c in range(2):
                        s = f3[2 * v + c]
                        sp.dma_start(wslot(s, 2), node_rows(a["L3_ffn_experts"][e], c)).then_inc(arrive[s], 16)

                for wait in f3_before:
                    sp.wait_ge(*wait)
                load(0, 0)
                load(1, 1)
                with sp.Fori(1, EXPERTS // 2) as i:
                    for v in range(2):
                        sp.wait_ge(down_g, i * 2 + (UP3 + v - 1))
                        load(i * 2 + v, v)

            parts = {"layer0": layer0, "edges1": edges1, "ffn1": ffn1, "ffn2": ffn2, "ffn3": ffn3}
            for item in plan:
                if isinstance(item, str):
                    parts[item]()
                    continue
                s, src, k, before = item
                if before is not None:
                    sp.wait_ge(*before)
                sp.dma_start(wslot(s, k), src).then_inc(arrive[s], 16)
            sp.wait_ge(added, ADDED)
            sp.dma_start(out.rearrange("(t p) d -> p t d", p=P), x[:, :, :]).then_inc(out_done, 16)
            sp.wait_ge(out_done, 16)

        @block.gpsimd
        def _(pool):
            step = Steps(pool, pool_s)
            step(pool.memset(big[:, 0, :], NONE), none_ready)
            for tile, value in ((ident, 0.0), (zeros, 0.0), (ones, 1.0), (upper, 1.0), (half, -0.5), (two, 2.0), (sel8, 0.0), (low8, 1.0)):
                step(pool.memset(tile[:], value))
            step(pool.affine_select(out=ident[:, :], in_=ident[:, :], compare_op=ALU.not_equal, fill=1.0, base=0,
                                    pattern=[[-1, P]], channel_multiplier=1))
            step(pool.affine_select(out=upper[:, :], in_=upper[:, :], compare_op=ALU.is_gt, fill=0.0, base=0,
                                    pattern=[[1, P]], channel_multiplier=-1))
            step(pool.affine_select(out=sel8[:, :, :], in_=sel8[:, :, :], compare_op=ALU.not_equal, fill=1.0, base=0,
                                    pattern=[[-1, 8], [0, P]], channel_multiplier=1))
            step(pool.affine_select(out=low8[:, :, :], in_=low8[:, :, :], compare_op=ALU.is_gt, fill=0.0, base=0,
                                    pattern=[[1, 8], [-1, 8]], channel_multiplier=0))
            step(pool.iota(nodeid[:, :], pattern=[[P, NT]], base=0, channel_multiplier=1, allow_small_or_imprecise_dtypes=True))
            step(pool.iota(iota[:, :], pattern=[[1, NODES]], base=0, channel_multiplier=0, allow_small_or_imprecise_dtypes=True), consts_ready)
            done = [0]

            def deviations(n):
                for _ in range(n):
                    done[0] += 1
                    pool.wait_ge(var_ready, done[0])
                    step(pool.tensor_tensor(rstd[:, :], varp[:, :], half[:, :], ALU.pow), rstd_ready)

            deviations(1)
            pool.wait_ge(pairs_r, 1)
            pool.wait_ge(filled, 16 * NT)
            for b in range(NB):
                pool.wait_ge(logit_r, b + 1)
                for s in range(SUB):
                    e = b * SUB + s
                    if e:
                        pool.wait_ge(written, 16 * e)
                    pool.indirect_dma_start(out=table0, out_offset=bass.IndirectOffsetOnAxis(ap=pair[:, e:e + 1], axis=0),
                                            in_=logit[:, e, :], in_offset=None).then_inc(written, 16)
            deviations(3)

            def ratio(n, at):
                pool.wait_ge(mish_sq, at + n + 1)
                pool.wait_ge(mish_rc, at + n + 1)
                pool.tensor_tensor(mr[:, n % 4, :], mr[:, n % 4, :], mt[:, n % 4, :], ALU.mult).then_inc(mish_q, 1)

            for n in range(4):
                ratio(n, 0)
            with pool.Fori(0, NB - 1) as i:
                for q in range(8):
                    ratio(4 + q, i * 8)
            for n in range(MISH - 4, MISH + 4):
                ratio(n, 0)
            deviations(5)
            pool.wait_ge(rel_w, 16 * 4 * NT)
            for e in range(ET):
                if e >= RING:
                    pool.wait_ge(msg_lo, 4 * NB + e - RING + 1)
                pool.indirect_dma_start(out=gather[:, e % RING, :], out_offset=None, in_=table3,
                                        in_offset=bass.IndirectOffsetOnAxis(ap=rrow[:, e:e + 1], axis=0)).then_inc(gathered[e % RING], 16)
            deviations(3)

        @block.scalar
        def _(act):
            step = Steps(act, act_s)
            for r, name in enumerate(ROWS[0]):
                act.dma_start(rows[:, r, :], a[name].partition_broadcast(P)).then_inc(rows_loaded, 16)
            act.wait_ge(none_ready, 1)
            for t in range(NT):
                act.dma_start(table0.rearrange("(t p n) h -> t p (n h)", t=NT, p=P)[t], big[:, 0, :]).then_inc(filled, 16)
            smalls = ((ba[:, :], a["L0_gnn_ba"].partition_broadcast(P)), (wa[:, :], a["L0_gnn_Wa"]),
                      (ab[:, :], a["L2_gnn_a_b"].partition_broadcast(P)), (b1e0[:, :, :], a["L0_ffn_b1"]),
                      (b1e2[:, :, :], a["L2_ffn_b1"]), (b2e[:, 0, :], a["L0_ffn_b2"]), (b2e[:, 1, :], a["L2_ffn_b2"]),
                      (b3c[:, :], a["L1_gnn_b3"]), (bf1[:, :], a["L3_gnn_b_ffn1"]),
                      (gatew[:, 0, :, :], a["L0_ffn_Wg"].rearrange("(k p) e -> p k e", p=P)),
                      (gatew[:, 1, :, :], a["L2_ffn_Wr"].rearrange("(k p) e -> p k e", p=P)),
                      (gatew[:, 2, :, :], a["L3_ffn_gate_w"].rearrange("(k p) e -> p k e", p=P)),
                      (br[:, 0, :], a["L0_ffn_bg"].partition_broadcast(P)), (br[:, 1, :], a["L2_ffn_br"].partition_broadcast(P)),
                      (w1c[:, :], a["L1_gnn_W1"][2 * DIM:2 * DIM + 64, :]))
            assert len(smalls) == N_SMALL
            for dst, src in smalls:
                act.dma_start(dst, src).then_inc(small_loaded, 16)

            def load_rows(layer, uses):
                act.wait_ge(row_used, uses)
                for r, name in enumerate(ROWS[layer]):
                    act.dma_start(rows[:, r, :], a[name].partition_broadcast(P)).then_inc(rows_loaded, 16)

            turns = [0]

            def turn(dst):
                for k in (0, 2):
                    act.wait_ge(turned, KT * turns[0] + k + 1)
                    step(act.activation(dst[:, k, :], bank[k][:, 0:NODES], ACT.Copy), xT_a)
                turns[0] += 1

            def split_tables(first, n, tabs, cols):
                for g in range(n):
                    act.wait_ge(tab_sum, first + g + 1)
                    which, r = divmod(g, n // 2)
                    t, c = divmod(r, cols)
                    step(act.activation(tabs[:, which, 0, t, c * 512:c * 512 + 512], tmp[:, g % 2, :], ACT.Copy), tab_hi)

            act.wait_ge(consts_ready, 1)
            turn(xT)
            split_tables(0, 12, tabs0, 2)

            def relu(n, at):
                act.wait_ge(z_g, at + n + 1)
                act.activation(relu4[:, n % 4, :], bank[n % 4][:, :], ACT.Relu, scale=0.99).then_inc(relu_r, 1)

            for n in range(8):
                relu(n, 0)
            with act.Fori(0, 5) as i:
                for c in range(8, 24):
                    relu(c, i * 16)
            for n in range(88, 96):
                relu(n, 0)
            act.wait_ge(big_loaded, 16 * NT)
            act.wait_ge(max_r, 1)
            for h in range(HEADS):
                if h >= 2:
                    act.wait_ge(e_turned, NT * (h - 1))
                for t in range(NT):
                    step(act.activation(eh[:, h % 2, t, :], big[:, t, :].rearrange("p (n h) -> p h n", h=HEADS)[:, h, :],
                                        ACT.Exp, bias=mneg[:, t, h:h + 1], accum_out=den[:, t, h:h + 1]), e_ready)

            def elu(first):
                for t in range(NT):
                    act.wait_ge(elu_in, first + t + 1)
                    step(act.activation(tmp[:, t % 2, :], tmp[:, t % 2, :], ACT.Exp), elu_ex)

            elu(0)
            load_rows(1, 1)
            turn(xT)
            act.wait_ge(small_loaded, 16 * N_SMALL)
            act.wait_ge(route_d, 1)
            step(act.activation(small[:, 1, :], small[:, 1, :], ACT.Exp), route_a)
            with act.Fori(0, EXPERTS) as e:
                for j in range(JT0):
                    act.wait_ge(up_g, e * JT0 + j + 1)
                    act.activation(silu2[:, j % 2, :], bank[j % 2][:, 0:NODES], ACT.Silu,
                                   bias=b1e0[:, bass.ds(e, 1), j]).then_inc(silu_r, 1)
            turn(xT)
            split_tables(12, 6, tabs1, 1)

            def mish_high(n, at, at_m):
                kind, b, s = mish_tile(n)
                if kind == "m":
                    act.wait_ge(mish_r, at + n + 1)
                    act.activation(mh[:, s, :], mz[:, n % 4, :], ACT.Copy).then_inc(msg_hi, 1)

            def mish_reciprocal(n, at, width=512):
                act.wait_ge(mish_sq, at + n + 1)
                act.activation(mr[:, n % 4, 0:width], mt[:, n % 4, 0:width], ACT.Ln, bias=two[:, 0:1]).then_inc(mish_ln, 1)
                act.wait_ge(mish_ln, at + n + 1)
                act.activation(mr[:, n % 4, 0:width], mr[:, n % 4, 0:width], ACT.Exp, scale=-1.0).then_inc(mish_rc, 1)

            def mish_exp(n, at, width=512):
                act.wait_ge(mish_in, at + n + 1)
                act.activation(mt[:, n % 4, 0:width], mz[:, n % 4, 0:width], ACT.Exp).then_inc(mish_ex, 1)

            def mish_step(n, at, first=0):
                if n - 3 >= first:
                    mish_high(n - 3, at, at)
                if first <= n - 1 < MISH:
                    mish_reciprocal(n - 1, at)
                if n < MISH:
                    mish_exp(n, at)

            for n in range(12):
                mish_step(n, 0)
            with act.Fori(0, 5) as i:
                for c in range(12, 28):
                    mish_step(c, i * 16)
            mish_high(MISH - 7, 0, 0)
            mish_reciprocal(MISH - 5, 0)
            for n in range(MISH - 4, MISH + 3):
                mish_step(n, 0, MISH - 4)
            turn(yT)
            for m in range(KT):
                mish_exp(MISH + m, 0, NODES)
                mish_reciprocal(MISH + m, 0, NODES)
            load_rows(2, 2)
            turn(xT)

            def turn_quant(j, u, at):
                for c in range(2):
                    act.wait_ge(q_turned, at * 3 + 3 * j + c + 1)
                    act.activation(qT[:, u, c, :], bank[c][:, :], ACT.Copy).then_inc(qT_a, 1)

            def hidden1(j, u, at):
                act.wait_ge(up_g, at + UP1 + j + 1)
                act.activation(silu2[:, u, :], bank[3][:, 0:NODES], ACT.Silu).then_inc(silu_r, 1)

            turn_quant(0, 0, 0)
            hidden1(0, 0, 0)
            turn_quant(1, 1, 0)
            with act.Fori(0, 4) as i:
                for j in (1, 2):
                    hidden1(j, j % 2, i * 2)
                    turn_quant(j + 1, (j + 1) % 2, i * 2)
            hidden1(9, 1, 0)
            turn_quant(10, 0, 0)
            hidden1(10, 0, 0)
            turn(xT)
            for h in range(HEADS):
                for t in range(NT):
                    n = h * NT + t
                    act.wait_ge(score_r, n + 1)
                    step(act.activation(srow[:, t, :], srow[:, t, :], ACT.Exp, bias=mneg[:, t, h:h + 1]), exp2_r)
            load_rows(3, 3)
            for r in range(4):
                act.dma_start(brel[:, r, :], a["L3_gnn_b_rel"][r, :].partition_broadcast(P)).then_inc(brel_loaded, 16)
            turn(xT)
            act.wait_ge(route_d, 2)
            step(act.activation(small[:, 1, :], small[:, 1, :], ACT.Exp), route_a)
            with act.Fori(0, EXPERTS // 2) as i:
                for v in range(2):
                    for j in range(JT2):
                        act.wait_ge(up_g, i * (2 * JT2) + (UP2 + v * JT2 + j + 1))
                        act.activation(act2[:, j % 2, :], bank[j % 2][:, 0:NODES], ACT.Gelu,
                                       bias=b1e2[:, bass.ds(i * 2 + v, 1), j]).then_inc(hid_r, 1)
            turn(xT)
            for n in range(4 * NT):
                act.wait_ge(rel_r, n + 1)
                r, t = divmod(n, NT)
                act.dma_start(table3.rearrange("(t p r) d -> t r p d", t=NT, p=P)[t, r], stage[:, n, :]).then_inc(rel_w, 16)

            def scaled_high(n, at):
                act.wait_ge(scaled_r, at + n + 1)
                act.activation(mh[:, n % 4, :], msg4[:, n % 4, :], ACT.Copy).then_inc(msg_hi, 1)

            for n in range(8):
                scaled_high(n, 0)
            with act.Fori(0, 4) as i:
                for c in range(8, 16):
                    scaled_high(c, i * 8)
            for n in range(40, 48):
                scaled_high(n, 0)
            turn(yT)
            for m in range(8):
                act.wait_ge(node_g, 2 * NT + m + 1)
                step(act.activation(hidT[:, m, :], bank[m % 4][:, 0:NODES], ACT.Gelu, bias=bf1[:, m:m + 1]), gelu_r)
            turn(xT)
            act.wait_ge(sk_d, 1)
            step(act.activation(sink[:, 0, :], sink[:, 0, :], ACT.Ln), sk_a)
            with act.Fori(0, SINKHORN) as i:
                step.enter(i, {sk_a: 4})
                act.wait_ge(sk_d, i * 8 + 3)
                step(act.activation(sink[:, 1, :], sink[:, 0, :], ACT.Exp, bias=sinks[:, 0:1], accum_out=sinks[:, 1:2]), sk_a)
                step(act.activation(sinks[:, 2:3], sinks[:, 1:2], ACT.Ln), sk_a)
                act.wait_ge(sk_d, i * 8 + 6)
                step(act.activation(sinka[:, 2, :, :], sinka[:, 1, :, :], ACT.Exp), sk_a)
                act.wait_ge(sk_d, i * 8 + 7)
                step(act.activation(small1[:, 1, :], small1[:, 0, :], ACT.Ln), sk_a)
            step.leave(SINKHORN)
            act.wait_ge(sk_d, 1 + 8 * SINKHORN)
            step(act.activation(sink[:, 0, :], sink[:, 0, :], ACT.Exp), sk_a)

        @block.vector
        def _(dve):
            step = Steps(dve, dve_s)
            turns = [0]
            norms = [0]

            def norm(src, dst, signal=None, after=None):
                for t in range(NT):
                    step(dve.bn_stats(stats[:, :], src[:, t, :]))
                    step(dve.bn_aggr(mv[:, t, :], stats[:, :]))
                norms[0] += 1
                step(dve.tensor_scalar(varp[:, :], mv[:, :, 1], EPS, None, ALU.add), var_ready)
                dve.wait_ge(rstd_ready, norms[0])
                for t in range(NT):
                    step(dve.tensor_scalar(dst[:, t, :], src[:, t, :], mv[:, t, 0:1], rstd[:, t:t + 1], ALU.subtract, ALU.mult), signal)
                    if after is not None:
                        after(t)

            def turn(dst):
                for k in (1, 3):
                    dve.wait_ge(turned, KT * turns[0] + k + 1)
                    step(dve.tensor_copy(dst[:, k, :], bank[k][:, 0:NODES]), xT_v)
                turns[0] += 1

            def tables(first, n, tabs, cols, bias):
                def low(g):
                    which, r = divmod(g, n // 2)
                    t, c = divmod(r, cols)
                    dve.wait_ge(tab_hi, first + g + 1)
                    step(dve.tensor_tensor(tabs[:, which, 1, t, c * 512:c * 512 + 512], tmp[:, g % 2, :],
                                           tabs[:, which, 0, t, c * 512:c * 512 + 512], ALU.subtract), tab_lo)

                for g in range(n):
                    dve.wait_ge(table_g, first + g + 1)
                    which, r = divmod(g, n // 2)
                    if which == 0:
                        step(dve.tensor_tensor(tmp[:, g % 2, :], bank[g % 4][:, :], bias(r % cols), ALU.add), tab_sum)
                    else:
                        step(dve.tensor_copy(tmp[:, g % 2, :], bank[g % 4][:, :]), tab_sum)
                    if g:
                        low(g - 1)
                low(n - 1)

            def onehots(par, at_ix):
                dve.wait_ge(ix_loaded, at_ix)
                for w in range(2):
                    for t in range(NT):
                        last = dve.tensor_scalar(onehot[:, par, w, t, :], eidx[:, w, :], nodeid[:, t:t + 1], None, ALU.is_equal)
                        if (w, t) == (1, NT - 1):
                            last.then_inc(oh_ready, 1)
                        
            dve.wait_ge(x_loaded, 16)
            norm(x, xn, nodes_ready)
            dve.wait_ge(edges_loaded, 64)
            step(dve.tensor_copy(srcf[:, :], srcc[:, :]))
            step(dve.tensor_copy(dstf[:, :], dstc[:, :]))
            step(dve.scalar_tensor_tensor(pair[:, :], srcf[:, :], float(NODES), dstf[:, :], ALU.mult, ALU.add), pairs_r)
            step(dve.scalar_tensor_tensor(rrow[:, :], srcc[:, :], 4.0, typc[:, :], ALU.mult, ALU.add))
            turn(xT)
            dve.wait_ge(rows_loaded, rows_before[0])

            def values(first, layer, name):
                for t in range(NT):
                    dve.wait_ge(value_g, first + t + 1)
                    step(dve.tensor_tensor(vn[:, t, :], bank[4 + t][:, :], row(layer, name), ALU.add), v_ready)

            values(0, 0, "L0_gnn_bv")
            tables(0, 12, tabs0, 2, lambda c: rows[:, 1 + c, :])
            dve.wait_ge(small_loaded, 16 * N_SMALL)

            def edge_onehots(b, at):
                for s in range(SUB):
                    for w, f in ((0, srcf), (1, dstf)):
                        last = dve.tensor_scalar(ebf[:, s, w, :], iota[:, :], f[:, bass.ds(at + s, 1)], None, ALU.is_equal)
                last.then_inc(em_ready, 1)

            def leaky(n, at):
                dve.wait_ge(relu_r, at + n + 1)
                dve.scalar_tensor_tensor(leaky4[:, n % 4, :], bank[n % 4][:, :], 0.01, relu4[:, n % 4, :], ALU.mult, ALU.add).then_inc(leaky_r, 1)

            def logits(b, par, at, at_e):
                dve.wait_ge(logit_g, at + b + 1)
                dve.tensor_scalar(logit[:, bass.ds(at_e, SUB), :], bank[4][:, 32 * par:32 * par + 32].rearrange("p (s h) -> p s h", s=SUB),
                                  ba[:, 0:1], None, ALU.add).then_inc(logit_r, 1)

            def block0(b, par, i2, i16):
                for h in range(HEADS):
                    leaky(b * 8 + h, i16)
                    if h == 0 and b < NB - 1:
                        onehots(1 - par, (i2 + (b + 2)) * 32)
                    if h == 1:
                        if b >= 1:
                            logits(b - 1, 1 - par, i2, (i2 + (b - 1)) * SUB)
                            dve.wait_ge(count_g, i2 + b)
                        edge_onehots(b, (i2 + b) * SUB)

            onehots(0, 32)
            block0(0, 0, 0, 0)
            with dve.Fori(0, 5) as i:
                for u in range(2):
                    block0(1 + u, 1 - u, i * 2, i * 16)
            block0(NB - 1, 1, 0, 0)
            logits(NB - 1, 1, 0, (NB - 1) * SUB)
            dve.wait_ge(count_g, NB)
            for t in range(NT):
                step(dve.tensor_copy(count[:, t, :], bank[5 + t][:, 0:NODES]))
            dve.wait_ge(big_loaded, 16 * NT)
            for t in range(NT):
                step(dve.tensor_reduce(mneg[:, t, :], big[:, t, :].rearrange("p (n h) -> p h n", h=HEADS), AX.X, ALU.max))
            step(dve.tensor_scalar(mneg[:, :, :], mneg[:, :, :], -1e30, -1.0, ALU.max, ALU.mult), max_r)

            def turned_weights(h):
                for d in range(NT):
                    dve.wait_ge(e_turned, turned_heads[0] * NT + d + 1)
                    step(dve.tensor_copy(eT[:, h % 2, d, :], bank[d][:, 0:NODES]), eT_ready)
                turned_heads[0] += 1

            turned_heads = [0]
            for h in range(HEADS):
                turned_weights(h)
            step(dve.tensor_scalar(den[:, :, :], den[:, :, :], 1e-30, None, ALU.max))
            step(dve.reciprocal(den[:, :, :], den[:, :, :]))
            dve.wait_ge(y_g, HEADS)

            def per_head(ap, t):
                return ap[:, t, :].unsqueeze(2).to_broadcast([P, HEADS, HD])

            def heads(ap):
                return ap.rearrange("p (h d) -> p h d", h=HEADS)

            for t in range(NT):
                step(dve.tensor_tensor(heads(y[:, t, :]), heads(bank[5 + t][:, :]), per_head(den, t), ALU.mult))
                step(dve.tensor_scalar(tmp[:, t % 2, :], y[:, t, :], 0.0, None, ALU.min), elu_in)
                dve.wait_ge(elu_ex, t + 1)
                step(dve.scalar_tensor_tensor(y[:, t, :], y[:, t, :], 0.0, tmp[:, t % 2, :], ALU.max, ALU.add))
                step(dve.scalar_tensor_tensor(y[:, t, :], y[:, t, :], -1.0, xn[:, t, :], ALU.add, ALU.add))

            def affine(src, layer, gain, shift, add, signal=None):
                def after(t):
                    step(dve.tensor_tensor(src[:, t, :], src[:, t, :], row(layer, gain), ALU.mult))
                    step(dve.tensor_tensor(src[:, t, :], src[:, t, :], row(layer, shift), ALU.add), signal)
                    if add:
                        step(dve.tensor_tensor(x[:, t, :], x[:, t, :], src[:, t, :], ALU.add))
                norm(src, src, None, after)

            affine(y, 0, "L0_gnn_gamma", "L0_gnn_beta", True)
            step(dve.tensor_copy(stats[:, 0:1], stats[:, 1:2]), row_used)

            def across(ap):
                return ap.unsqueeze(2).to_broadcast([P, NT, 8])

            def top2():
                v = small[:, 0, :]
                others = sm(0).unsqueeze(2).to_broadcast([P, NT, 8, 8])
                own = sm(0).unsqueeze(3).to_broadcast([P, NT, 8, 8])
                g = cmp8[:, 0, :, :].rearrange("p (t e) f -> p t e f", t=NT)
                q = cmp8[:, 1, :, :].rearrange("p (t e) f -> p t e f", t=NT)
                step(dve.tensor_tensor(g, others, own, ALU.is_gt))
                step(dve.tensor_tensor(q, others, own, ALU.is_equal))
                step(dve.tensor_tensor(q, q, low8[:, :, :].unsqueeze(1).to_broadcast([P, NT, 8, 8]), ALU.mult))
                step(dve.tensor_tensor(cmp8[:, 0, :, :], cmp8[:, 0, :, :], cmp8[:, 1, :, :], ALU.add))
                step(dve.tensor_reduce(small[:, 2, :], cmp8[:, 0, :, :], AX.X, ALU.add))
                step(dve.tensor_scalar(small[:, 2, :], small[:, 2, :], 2.0, None, ALU.is_lt))

            def logits_in(n, layer):
                dve.wait_ge(route_g, n)
                step(dve.tensor_tensor(sm(0), bank[7][:, 0:NT * 8].rearrange("p (t e) -> p t e", t=NT),
                                       br[:, layer, :].unsqueeze(1).to_broadcast([P, NT, 8]), ALU.add))
                step(dve.tensor_reduce(small1[:, 0, :], sm(0), AX.X, ALU.max))
                step(dve.tensor_tensor(sm(1), sm(0), across(small1[:, 0, :]), ALU.subtract), route_d)

            def normalized(dst, src, eps):
                step(dve.tensor_reduce(small1[:, 1, :], src, AX.X, ALU.add))
                if eps:
                    step(dve.tensor_scalar(small1[:, 1, :], small1[:, 1, :], eps, None, ALU.add))
                step(dve.reciprocal(small1[:, 1, :], small1[:, 1, :]))
                step(dve.tensor_tensor(dst, src, across(small1[:, 1, :]), ALU.mult))

            def expert_bias(n):
                dve.wait_ge(coefT_g, n)
                step(dve.tensor_copy(coefT[:, :], bank[7][0:8, 0:NODES]), coefT_r)
                for t in range(NT):
                    dve.wait_ge(b2_g, NT * (n - 1) + t + 1)
                    step(dve.tensor_tensor(x[:, t, :], x[:, t, :], bank[4 + t][:, :], ALU.add), added)

            norm(x, xn, nodes_ready)
            turn(xT)
            logits_in(1, 0)
            top2()
            dve.wait_ge(route_a, 1)
            step(dve.tensor_tensor(sm(1), sm(1), sm(2), ALU.mult))
            normalized(coef[:, :, :], sm(1), 0.0)
            step(dve.tensor_copy(stats[:, 0:1], stats[:, 1:2]), coef_r)
            expert_bias(1)

            def add_expert(e, banks, at_down, at_added):
                dve.wait_ge(down_g, at_down)
                for t in range(NT):
                    dve.scalar_tensor_tensor(x[:, t, :], bank[banks + t][:, :], coef[:, t, bass.ds(e, 1)], x[:, t, :],
                                             ALU.mult, ALU.add).then_inc(added, 1)
                dve.wait_ge(added, at_added)

            with dve.Fori(0, EXPERTS) as e:
                for j in range(JT0):
                    dve.wait_ge(silu_r, e * JT0 + j + 1)
                    dve.scalar_tensor_tensor(act2[:, j % 2, :], bank[2 + j % 2][:, 0:NODES], b1e0[:, bass.ds(e, 1), JT0 + j],
                                             silu2[:, j % 2, :], ALU.add, ALU.mult).then_inc(hid_r, 1)
                add_expert(e, 4, e * JT0 + JT0, e * NT + (ADD0 + NT))

            step.skip(added, EXPERTS * NT)
            norm(x, xn, nodes_ready)
            turn(xT)
            dve.wait_ge(rows_loaded, rows_before[1])
            tables(12, 6, tabs1, 1, lambda c: row(1, "L1_gnn_b1"))

            def message_onehots(at):
                for s in range(SUB):
                    last = dve.tensor_scalar(em[:, s, :], iota[:, :], dstf[:, bass.ds(at + s, 1)], None, ALU.is_equal)
                last.then_inc(em_ready, 1)

            def mish_out(n, at):
                kind, b, s = mish_tile(n) if n < MISH else ("u", 0, n - MISH)
                width = 512 if n < MISH else NODES
                dst = {"z": hT[:, b % 2, s, :], "m": mz[:, n % 4, :], "u": hidT[:, s, :]}[kind]
                dve.wait_ge(mish_q, at + n + 1)
                dve.tensor_tensor(dst, mz[:, n % 4, 0:width], mr[:, n % 4, 0:width], ALU.mult).then_inc(mish_r, 1)

            def mish_square(n, at, width=512):
                dve.wait_ge(mish_ex, at + n + 1)
                dve.tensor_scalar(mt[:, n % 4, 0:width], mt[:, n % 4, 0:width], 1e9, None, ALU.min).then_inc(mish_min, 1)
                dve.wait_ge(mish_min, at + n + 1)
                dve.scalar_tensor_tensor(mt[:, n % 4, 0:width], mt[:, n % 4, 0:width], 2.0, mt[:, n % 4, 0:width], ALU.add, ALU.mult).then_inc(mish_sq, 1)

            def message_low(n, at, at4):
                kind, b, s = mish_tile(n)
                if kind == "m":
                    dve.wait_ge(msg_hi, at4 + (4 * b + s + 1))
                    dve.tensor_tensor(ml[:, s, :], mz[:, n % 4, :], mh[:, s, :], ALU.subtract).then_inc(msg_lo, 1)

            def mish_input(n, at):
                kind, b, s = mish_tile(n) if n < MISH else ("u", 0, n - MISH)
                dve.wait_ge(mish_g, at + n + 1)
                if n >= 4:
                    dve.wait_ge(mish_r, at + n - 3)
                if kind == "z":
                    ins = dve.tensor_copy(mz[:, n % 4, :], bank[n % 4][:, :])
                elif kind == "m":
                    ins = dve.tensor_tensor(mz[:, n % 4, :], bank[n % 4][:, :], row(1, "L1_gnn_b2"), ALU.add)
                else:
                    ins = dve.tensor_scalar(mz[:, n % 4, 0:NODES], bank[n % 4][:, 0:NODES], b3c[:, s:s + 1], None, ALU.add)
                ins.then_inc(mish_in, 1)

            def mish_step(n, at, at4, first=0):
                if n - 3 >= first:
                    mish_out(n - 3, at)
                if first <= n - 1 < MISH:
                    mish_square(n - 1, at)
                if n - 3 >= first:
                    message_low(n - 3, at, at4)
                if n < MISH:
                    mish_input(n, at)

            def mish_drain():
                mish_out(MISH - 7, 0)
                mish_square(MISH - 5, 0)
                message_low(MISH - 7, 0, 0)
                for n in (MISH - 6, MISH - 5):
                    mish_out(n, 0)

            def block1(b, i2, at):
                if b == NB - 1:
                    mish_drain()
                for q in range(8 if b < NB - 1 else 4):
                    mish_step(4 + 8 * b + q, at, i2 * 4, MISH - 4 if b == NB - 1 else 0)
                    if q == 1 and b < NB - 2:
                        onehots(b % 2, (i2 + (NB + b + 3)) * 32)
                    if q == (2 if b < NB - 1 else 1):
                        message_onehots((i2 + b) * SUB)

            onehots(0, (NB + 1) * 32)
            onehots(1, (NB + 2) * 32)
            for n in range(4):
                mish_step(n, 0, 0)
            block1(0, 0, 0)
            with dve.Fori(0, 4) as i:
                for u in range(2):
                    block1(1 + u, i * 2, i * 16)
            for b in (NB - 3, NB - 2, NB - 1):
                block1(b, 0, 0)
            for n in range(MISH, MISH + 3):
                mish_step(n, 0, 0, MISH - 4)
            for t in range(NT):
                dve.wait_ge(agg_g, NT)
                step(dve.tensor_copy(y[:, t, :], bank[4 + t][:, :]), nodes_ready)
            turn(yT)
            for m in range(KT):
                mish_input(MISH + m, 0)
                mish_square(MISH + m, 0, NODES)
                mish_out(MISH + m, 0)
            for t in range(NT):
                dve.wait_ge(node_g, t + 1)
                step(dve.tensor_tensor(y[:, t, :], bank[4 + t][:, :], row(1, "L1_gnn_b4"), ALU.add))
                step(dve.tensor_tensor(y[:, t, :], y[:, t, :], xn[:, t, :], ALU.add))
            affine(y, 1, "L1_gnn_gamma", "L1_gnn_beta", True)
            step(dve.tensor_copy(stats[:, 0:1], stats[:, 1:2]), row_used)

            norm(x, xn, nodes_ready)

            turn(xT)

            def quant(j, u, i):
                raw = qraw[:, u, :, :].rearrange("p c (g n) -> p (c g) n", g=4)
                va = qa.rearrange("p (g n) -> p g n", g=12)
                vb = qb.rearrange("p (g n) -> p g n", g=12)
                base = (i * 2 + j) * 4 if i is not None else j * 4

                def link(ins, k):
                    ins.then_inc(quant_s, 1)
                    dve.wait_ge(quant_s, base + k)

                if i is None:
                    dve.wait_ge(q_loaded[u], 48 * (j // 2 + 1))
                else:
                    dve.wait_ge(q_loaded[u], i * 48 + 48 * (j // 2 + 1))
                link(dve.tensor_reduce(qs[:, :, 0], raw, AX.X, ALU.add, apply_absolute_value=True), 1)
                link(dve.tensor_scalar(qs[:, :, 0], qs[:, :, 0], 1.0 / 128, EPS, ALU.mult, ALU.add), 2)
                dve.tensor_scalar(qs[:, :, 1], qs[:, :, 0], 0.5, None, ALU.mult)
                link(dve.tensor_scalar(qs[:, :, 2], qs[:, :, 0], -0.5, None, ALU.mult), 3)
                for g in range(12):
                    dve.tensor_scalar(va[:, g, :], raw[:, g, :], qs[:, g, 1:2], qs[:, g, 0:1], ALU.is_gt, ALU.mult)
                    last = dve.tensor_scalar(vb[:, g, :], raw[:, g, :], qs[:, g, 2:3], qs[:, g, 0:1], ALU.is_lt, ALU.mult)
                link(last, 4)
                dve.tensor_tensor(qa, qa, qb, ALU.subtract).then_inc(quant_r, 1)

            def turn_quant(j, u, at):
                dve.wait_ge(q_turned, at * 3 + 3 * j + 3)
                dve.tensor_copy(qT[:, u, 2, :], bank[2][:, :]).then_inc(qT_v, 1)

            def hidden1(j, u, at):
                dve.wait_ge(silu_r, at + UP1 + j + 1)
                dve.tensor_tensor(act2[:, u, :], bank[4][:, 0:NODES], silu2[:, u, :], ALU.mult).then_inc(hid_r, 1)

            quant(0, 0, None)
            turn_quant(0, 0, 0)
            quant(1, 1, None)
            hidden1(0, 0, 0)
            turn_quant(1, 1, 0)
            quant(2, 0, None)
            with dve.Fori(0, 4) as i:
                for j in (1, 2):
                    hidden1(j, j % 2, i * 2)
                    turn_quant(j + 1, (j + 1) % 2, i * 2)
                    quant(j + 2, j % 2, i)
            hidden1(9, 1, 0)
            turn_quant(10, 0, 0)
            hidden1(10, 0, 0)
            dve.wait_ge(down_g, UP2)
            for t in range(NT):
                step(dve.tensor_tensor(x[:, t, :], x[:, t, :], bank[5 + t][:, :], ALU.add), added)

            norm(x, xn, nodes_ready)
            turn(xT)
            dve.wait_ge(rows_loaded, rows_before[2])
            values(NT, 2, "L2_gnn_Wb")
            for k, name in enumerate(("L2_gnn_at", "L2_gnn_as")):
                for t in range(NT):
                    step(dve.tensor_tensor(prod, vn[:, t, :], row(2, name), ALU.mult))
                    step(dve.tensor_reduce(pq[:, k, t, :], heads(prod), AX.X, ALU.add))
            step(dve.tensor_tensor(pq[:, 1, :, :], pq[:, 1, :, :], ab[:, :].unsqueeze(1).to_broadcast([P, NT, HEADS]), ALU.add), pq_r)
            step(dve.tensor_copy(stats[:, 0:1], stats[:, 1:2]), row_used)
            for t in range(NT):
                step(dve.tensor_scalar(negm[:, t, :], count[:, t, :], 0.0, -1e30, ALU.is_equal, ALU.mult))
            dve.wait_ge(pqT_g, 1)
            step(dve.tensor_copy(qT2, bank[3][0:8, 0:NODES]), pqT_r)

            def score(h, t):
                dve.wait_ge(srow_g, h + 1)
                step(dve.scalar_tensor_tensor(srow[:, t, :], bank[3 + h % 2][:, 0:NODES], pq[:, 0, t, h:h + 1], negm[:, t, :], ALU.add, ALU.add))
                step(dve.scalar_tensor_tensor(srow[:, t, :], srow[:, t, :], 0.2, srow[:, t, :], ALU.mult, ALU.max))
                step(dve.tensor_reduce(small1[:, 0, 0:1], srow[:, t, :], AX.X, ALU.max))
                step(dve.tensor_scalar(mneg[:, t, h:h + 1], small1[:, 0, 0:1], -1.0, None, ALU.mult), score_r)

            def weigh(h, t):
                dve.wait_ge(exp2_r, h * NT + t + 1)
                if h >= 2:
                    dve.wait_ge(e_turned, NT * (HEADS + h - 1))
                step(dve.tensor_tensor_reduce(eh[:, h % 2, t, :], srow[:, t, :], count[:, t, :], 1.0, 0.0,
                                              ALU.mult, ALU.add, den[:, t, h:h + 1]), weighed)

            for h in range(HEADS):
                for t in range(NT):
                    score(h, t)
                    if t:
                        weigh(h, t - 1)
                weigh(h, NT - 1)
                if h:
                    turned_weights(h - 1)
            turned_weights(HEADS - 1)
            step(dve.tensor_scalar(den[:, :, :], den[:, :, :], 1e-30, None, ALU.max))
            step(dve.reciprocal(den[:, :, :], den[:, :, :]))
            dve.wait_ge(y_g, 2 * HEADS)
            for t in range(NT):
                step(dve.tensor_tensor(heads(y[:, t, :]), heads(bank[5 + t][:, :]), per_head(den, t), ALU.mult))
                step(dve.tensor_tensor(x[:, t, :], x[:, t, :], y[:, t, :], ALU.add))

            norm(x, xn, nodes_ready)
            turn(xT)
            logits_in(2, 1)
            top2()
            step(dve.tensor_copy(stats[:, 0:1], stats[:, 1:2]), mask_r)
            dve.wait_ge(route_a, 2)
            normalized(sm(1), sm(1), 0.0)
            step(dve.tensor_tensor(sm(3), sm(1), sm(2), ALU.mult))
            normalized(sm(3), sm(3), 1e-9)
            dve.wait_ge(pos_g, 1)
            step(dve.tensor_scalar(small[:, 4, :], bank[7][:, 32:32 + NT * 8], float(CAP), None, ALU.is_lt))
            step(dve.tensor_tensor(sm(3), sm(3), sm(4), ALU.mult))
            normalized(coef[:, :, :], sm(3), 1e-9)
            step(dve.tensor_copy(stats[:, 0:1], stats[:, 1:2]), coef_r)
            expert_bias(2)
            with dve.Fori(0, EXPERTS // 2) as i:
                for v in range(2):
                    add_expert(i * 2 + v, 4, i * (2 * JT2) + (UP2 + JT2 * (v + 1)), i * (2 * NT) + (ADD2 + NT * (v + 1)))
            step.skip(added, EXPERTS * NT)

            norm(x, xn, nodes_ready)
            turn(xT)
            step(dve.tensor_copy(wdeg[:, :, 0], ewc[:, :]))
            step(dve.tensor_tensor(wdeg[:, :, 1], ewc[:, :], wdeg[:, :, 0], ALU.subtract), wdeg_r)
            dve.wait_ge(brel_loaded, 64)
            dve.wait_ge(rows_loaded, rows_before[3])
            for n in range(4 * NT):
                dve.wait_ge(rel_g, n + 1)
                step(dve.tensor_tensor(stage[:, n, :], bank[n % 4][:, :], brel[:, n // NT, :], ALU.add), rel_r)
            for t in range(NT):
                dve.wait_ge(node_g, NT + t + 1)
                step(dve.tensor_tensor(y[:, t, :], bank[4 + t][:, :], row(3, "L3_gnn_b_self"), ALU.add))
                step(dve.tensor_tensor(y[:, t, :], y[:, t, :], xn[:, t, :], ALU.add))

            def scaled_low(n, at):
                dve.wait_ge(msg_hi, at + (4 * NB + n + 1))
                dve.tensor_tensor(ml[:, n % 4, :], msg4[:, n % 4, :], mh[:, n % 4, :], ALU.subtract).then_inc(msg_lo, 1)

            def scaled(n, at, turn_value):
                if n >= 4:
                    dve.wait_ge(m_used, at + n - 3)
                dve.wait_ge(gathered[n % RING], turn_value)
                dve.tensor_scalar(msg4[:, n % 4, :], gather[:, n % RING, :], ewc[:, bass.ds(at + n, 1)], None, ALU.mult).then_inc(scaled_r, 1)
                dve.tensor_scalar(em[:, n % 4, :], iota[:, :], dstf[:, bass.ds(at + n, 1)], None, ALU.is_equal).then_inc(em_ready, 1)

            for n in range(RING):
                scaled(n, 0, 16)
                if n:
                    scaled_low(n - 1, 0)
            with dve.Fori(0, 4) as i:
                for c in range(RING, 2 * RING):
                    scaled(c, i * RING, i * 16 + 32)
                    scaled_low(c - 1, i * RING)
            for n in range(5 * RING, 6 * RING):
                scaled(n, 0, 96)
                scaled_low(n - 1, 0)
            scaled_low(ET - 1, 0)
            dve.wait_ge(agg_g, 2 * NT + 1)
            step(dve.tensor_reduce(small1[:, 0, :], bank[3][:, 0:2 * NT].rearrange("p (t c) -> p t c", c=2), AX.X, ALU.add))
            step(dve.tensor_scalar(small1[:, 0, :], small1[:, 0, :], 1.0, None, ALU.max))
            step(dve.reciprocal(small1[:, 0, :], small1[:, 0, :]))
            for t in range(NT):
                step(dve.scalar_tensor_tensor(y[:, t, :], bank[t][:, :], small1[:, 0, t:t + 1], y[:, t, :], ALU.mult, ALU.add))
            affine(y, 3, "L3_gnn_ln1_g", "L3_gnn_ln1_b", False, nodes_ready)
            turn(yT)
            for t in range(NT):
                dve.wait_ge(node_g, 2 * NT + 8 + t + 1)
                step(dve.tensor_tensor(y[:, t, :], y[:, t, :], bank[4 + t][:, :], ALU.add))
                step(dve.tensor_tensor(y[:, t, :], y[:, t, :], row(3, "L3_gnn_b_ffn2"), ALU.add))
            affine(y, 3, "L3_gnn_ln2_g", "L3_gnn_ln2_b", True)

            norm(x, xn, nodes_ready)
            turn(xT)
            dve.wait_ge(route_g, 3)
            step(dve.tensor_scalar(sink[:, 0, :], bank[7][0:8, 0:NODES], 1e-10, None, ALU.max), sk_d)
            with dve.Fori(0, SINKHORN) as i:
                step.enter(i, {sk_d: 8})
                dve.wait_ge(sk_a, i * 4 + 1)
                step(dve.tensor_reduce(sinks[:, 3:4], sink[:, 0, :], AX.X, ALU.max), sk_d)
                step(dve.tensor_scalar(sinks[:, 0:1], sinks[:, 3:4], -1.0, None, ALU.mult), sk_d)
                dve.wait_ge(sk_a, i * 4 + 3)
                step(dve.tensor_scalar(sink[:, 0, :], sink[:, 0, :], sinks[:, 3:4], sinks[:, 2:3], ALU.subtract, ALU.subtract), sk_d)
                dve.wait_ge(sk_p, i * 2 + 1)
                turned_gates = bank[0][:, 0:NT * 8].rearrange("p (t e) -> p t e", t=NT)
                step(dve.tensor_reduce(small1[:, 2, :], turned_gates, AX.X, ALU.max), sk_d)
                step(dve.tensor_tensor(sinka[:, 1, :, :], turned_gates, across(small1[:, 2, :]), ALU.subtract), sk_d)
                dve.wait_ge(sk_a, i * 4 + 4)
                step(dve.tensor_reduce(small1[:, 0, :], sinka[:, 2, :, :], AX.X, ALU.add), sk_d)
                dve.wait_ge(sk_a, i * 4 + 5)
                step(dve.tensor_tensor(sinka[:, 0, :, :], sinka[:, 1, :, :], across(small1[:, 1, :]), ALU.subtract), sk_d)
                dve.wait_ge(sk_p, i * 2 + 2)
                step(dve.tensor_copy(sink[:, 0, :], bank[1][0:8, 0:NODES]), sk_d)
            step.leave(SINKHORN)
            dve.wait_ge(sk_a, 4 * SINKHORN + 2)
            for k in range(TOP // 8):
                src = sink[:, 0 if k == 0 else 1 + (k - 1) % 2, :]
                step(dve.max(sinks[:, 0:8], src))
                step(dve.match_replace(sink[:, 1 + k % 2, :], sinks[:, 0:8], src, -1.0))
            step(dve.tensor_scalar(sink[:, 3, :], sink[:, 1 + (TOP // 8 - 1) % 2, :], -1.0, None, ALU.is_equal))
            step(dve.scalar_tensor_tensor(sink[:, 4, :], sink[:, 0, :], 0.5, sink[:, 3, :], ALU.is_gt, ALU.mult), chosen_r)
            dve.wait_ge(sk_p, 2 * SINKHORN + 1)
            chosen = bank[7][:, 0:2 * NT * 8].rearrange("p (c t e) -> p c t e", c=2, t=NT)
            step(dve.tensor_reduce(small1[:, 0, :], chosen[:, 0, :, :], AX.X, ALU.add))
            step(dve.tensor_scalar(small1[:, 0, :], small1[:, 0, :], 1.0, None, ALU.add))
            step(dve.reciprocal(small1[:, 0, :], small1[:, 0, :]))
            step(dve.tensor_tensor(coef[:, :, :], chosen[:, 1, :, :], across(small1[:, 0, :]), ALU.mult))
            with dve.Fori(0, EXPERTS // 2) as i:
                for v in range(2):
                    add_expert(i * 2 + v, 3 * v, i * 2 + (UP3 + v + 1), i * (2 * NT) + (ADD3 + NT * (v + 1)))

        @block.tensor
        def _(pe):
            turns = [0]

            def turn(src):
                pe.wait_ge(nodes_ready, NT * (turns[0] + 1))
                for k in range(KT):
                    for t in range(NT):
                        last = pe.transpose(bank[k][:, t * P:(t + 1) * P], src[:, t, k * P:(k + 1) * P], ident[:, :])
                    last.then_inc(turned, 1)
                turns[0] += 1
                pe.wait_ge(xT_a, 2 * turns[0])
                pe.wait_ge(xT_v, 2 * turns[0])

            def arrived(*key):
                s, value = W[key]
                pe.wait_ge(arrive[s], value)

            def weight(name, k):
                return wslot(W[(*name, k // 2)][0], 2)[:, k % 2, :]

            def product(out, lhs, rhs, n, signal):
                for k in range(n):
                    last = pe.matmul(out, lhs(k), rhs(k), start=(k == 0), stop=(k == n - 1))
                last.then_inc(signal, 1)

            def tile(ap, k, t):
                return ap[:, k, t * P:(t + 1) * P]

            def values(name, signal):
                arrived(*name, 0)
                arrived(*name, 1)
                for t in range(NT):
                    product(bank[4 + t][:, :], lambda k: tile(xT, k, t), lambda k: weight(name, k), KT, signal)

            def router(which):
                for t in range(NT):
                    for k in range(KT):
                        last = pe.matmul(bank[7][:, t * 8:t * 8 + 8], tile(xT, k, t), gatew[:, which, k, :],
                                         start=(k == 0), stop=(k == KT - 1))
                last.then_inc(route_g, 1)

            def expert_bias(n, layer):
                pe.wait_ge(coef_r, n)
                for t in range(NT):
                    last = pe.transpose(bank[7][0:8, t * P:(t + 1) * P], coef[:, t, :], ident[:, :])
                last.then_inc(coefT_g, 1)
                pe.wait_ge(coefT_r, n)
                for t in range(NT):
                    pe.matmul(bank[4 + t][:, :], coefT[:, t * P:(t + 1) * P], b2e[:, layer, :], start=True, stop=True).then_inc(b2_g, 1)

            pe.wait_ge(consts_ready, 1)
            turn(xn)
            values(("wv",), value_g)
            for g in range(12):
                which, r = divmod(g, 6)
                t, c = divmod(r, 2)
                if r == 0:
                    for k in range(4):
                        arrived("ww", 4 * which + k)
                if g >= 4:
                    pe.wait_ge(tab_sum, g - 3)
                product(bank[g % 4][:, :], lambda k: tile(xT, k, t),
                        lambda k: wring[:, W["ww", 4 * which + k][0], c * 512:c * 512 + 512], KT, table_g)
            pe.wait_ge(tab_lo, 12)
            pe.wait_ge(tab_hi, 12)
            pe.wait_ge(small_loaded, 16 * N_SMALL)
            pe.wait_ge(v_ready, NT)

            def z0(n, par, at):
                h = n % 8
                for w in range(2):
                    for t in range(NT):
                        for p in range(2):
                            last = pe.matmul(bank[n % 4][:, :], tabs0[:, w, p, t, h * P:(h + 1) * P], onehot[:, par, w, t, :],
                                             start=(w, t, p) == (0, 0, 0), stop=(w, t, p) == (1, NT - 1, 1))
                last.then_inc(z_g, 1)

            def logit_parts(n, par, at):
                h = n % 8
                pe.wait_ge(leaky_r, at + n + 1)
                for s in range(SUB):
                    last = pe.matmul(bank[4][:, 32 * par + s * 8 + h:32 * par + s * 8 + h + 1],
                                     leaky4[:, n % 4, s * P:(s + 1) * P], wa[:, :], start=True, stop=True)
                if h == 7:
                    last.then_inc(logit_g, 1)

            def count0(b, at):
                pe.wait_ge(em_ready, at + b + 1)
                for s in range(SUB):
                    for t in range(NT):
                        last = pe.matmul(bank[5 + t][:, 0:NODES], ebf[:, s, 1, t * P:(t + 1) * P], ebf[:, s, 0, :],
                                         start=(b, s) == (0, 0), stop=(b, s) == (NB - 1, SUB - 1), skip_group_check=True)
                last.then_inc(count_g, 1)

            def block0(b, par, i2, i16):
                pe.wait_ge(oh_ready, i2 + b + 1)
                for h in range(HEADS):
                    n = b * 8 + h
                    z0(n, par, i16)
                    if n >= 2:
                        if h == 2 and b:
                            pe.wait_ge(logit_r, i2 + b)
                        logit_parts(n - 2, par if h >= 2 else 1 - par, i16)
                    if h == 4:
                        count0(b, i2)

            block0(0, 0, 0, 0)
            with pe.Fori(0, 5) as i:
                for u in range(2):
                    block0(1 + u, 1 - u, i * 2, i * 16)
            block0(NB - 1, 1, 0, 0)
            logit_parts(NB * 8 - 2, 1, 0)
            logit_parts(NB * 8 - 1, 1, 0)

            def attend(first, ready, ready_first):
                def turn_head(h):
                    pe.wait_ge(ready, ready_first + NT * (h + 1))
                    if h:
                        pe.wait_ge(eT_ready, (first + h) * NT)
                    for d in range(NT):
                        for t in range(NT):
                            last = pe.transpose(bank[d][:, t * P:(t + 1) * P], eh[:, h % 2, t, d * P:(d + 1) * P], ident[:, :])
                        last.then_inc(e_turned, 1)

                def weighted(h):
                    pe.wait_ge(eT_ready, (first + h + 1) * NT)
                    for t in range(NT):
                        for d in range(NT):
                            last = pe.matmul(bank[5 + t][:, h * HD:(h + 1) * HD], eT[:, h % 2, d, t * P:(t + 1) * P],
                                             vn[:, d, h * HD:(h + 1) * HD], start=(d == 0), stop=(d == NT - 1))
                    last.then_inc(y_g, 1)
                return turn_head, weighted

            turn_head, weighted = attend(0, e_ready, 0)
            for h in range(HEADS):
                turn_head(h)
                if h:
                    weighted(h - 1)
            weighted(HEADS - 1)

            turn(xn)
            router(0)
            expert_bias(1, 0)

            def up0(e, j):
                jj = j // 2
                for q in range(2):
                    s = f0[(3 * jj + q) % 6]
                    if j % 2 == 0:
                        pe.wait_ge(arrive[s], e * 32 + (f0_base[s] + 16 * (jj // 2 + 1)))
                    product_in(bank[2 * q + j % 2][:, 0:NODES], s, j % 2, 2 * P)
                last_product[0].then_inc(up_g, 1)

            last_product = [None]

            def product_in(out, s, c, n):
                for k in range(KT):
                    last_product[0] = pe.matmul(out, wslot(s, KT)[:, k, c * P:(c + 1) * P], xT[:, k, :], start=(k == 0), stop=(k == KT - 1))

            def down(hid_value, j, jn, rhs, banks, j0=0):
                pe.wait_ge(hid_r, hid_value)
                for t in range(NT):
                    last = pe.matmul(bank[banks + t][:, :], act2[:, j % 2, t * P:(t + 1) * P], rhs,
                                     start=(j == 0), stop=(j == jn - 1), skip_group_check=True)
                last.then_inc(down_g, 1)

            def down0(e, j):
                jj = j // 2
                s = f0[(3 * jj + 2) % 6]
                if j % 2 == 0:
                    pe.wait_ge(arrive[s], e * 32 + (f0_base[s] + 16 * (jj // 2 + 1)))
                if j == 0:
                    pe.wait_ge(added, e * NT + ADD0)
                down(e * JT0 + j + 1, j, JT0, wslot(s, 2)[:, j % 2, :], 4)

            with pe.Fori(0, EXPERTS) as e:
                for j in range(JT0):
                    up0(e, j)
                    if j:
                        down0(e, j - 1)
                down0(e, JT0 - 1)

            turn(xn)
            for g in range(6):
                which, t = divmod(g, NT)
                if t == 0:
                    arrived("w1", 2 * which)
                    arrived("w1", 2 * which + 1)
                if g >= 4:
                    pe.wait_ge(tab_sum, 12 + g - 3)
                product(bank[g % 4][:, :], lambda k: tile(xT, k, t), lambda k: weight(("w1",), 4 * which + k), KT, table_g)
            pe.wait_ge(tab_lo, 18)
            pe.wait_ge(tab_hi, 18)
            arrived("w2", 0)
            arrived("w2", 1)

            def z1(n, b, f, at, at_b):
                for w in range(2):
                    for t in range(NT):
                        for p in range(2):
                            pe.matmul(bank[n % 4][:, :], tabs1[:, w, p, t, f * P:(f + 1) * P], onehot[:, b % 2, w, t, :],
                                      start=(w, t, p) == (0, 0, 0), stop=False)
                if f == 0:
                    pe.wait_ge(at_loaded[b % 2], at_b)
                pe.matmul(bank[n % 4][:, :], w1c[:, f * P:(f + 1) * P], attr[:, b % 2, :], start=False, stop=True).then_inc(mish_g, 1)

            def message(n, b, s):
                product(bank[n % 4][:, :], lambda k: hT[:, b % 2, k, s * P:(s + 1) * P], lambda k: weight(("w2",), k), KT, mish_g)

            def mish_product(n, at, i2):
                kind, b, s = mish_tile(n)
                if n >= 4:
                    pe.wait_ge(mish_in, at + n - 3)
                if kind == "z":
                    if s == 0:
                        pe.wait_ge(oh_ready, i2 + (NB + b + 1))
                    z1(n, b, s, at, i2 * 8 + 16 * (b // 2 + 1))
                else:
                    if s == 0:
                        pe.wait_ge(mish_r, at + (8 * b + 4))
                    message(n, b, s)

            def aggregate(b, i2):
                pe.wait_ge(em_ready, i2 + (NB + b + 1))
                pe.wait_ge(msg_lo, i2 * 4 + (4 * b + 4))
                for s in range(SUB):
                    for t in range(NT):
                        for p, part in enumerate((mh, ml)):
                            last = pe.matmul(bank[4 + t][:, :], em[:, s, t * P:(t + 1) * P], part[:, s, :],
                                             start=(b, s, p) == (0, 0, 0), stop=(b, s, p) == (NB - 1, SUB - 1, 1), skip_group_check=True)
                            if b == NB - 1 and s == SUB - 1 and p == 1:
                                last.then_inc(agg_g, 1)

            def block1(b, i2, at):
                for q in range(8 if b < NB - 1 else 4):
                    mish_product(4 + 8 * b + q, at, i2)
                aggregate(b, i2)

            for n in range(4):
                mish_product(n, 0, 0)
            block1(0, 0, 0)
            with pe.Fori(0, 5) as i:
                for u in range(2):
                    block1(1 + u, i * 2, i * 16)
            block1(NB - 1, 0, 0)
            turn(y)
            for c in range(4):
                arrived("w3", c)
            for m in range(KT):
                product(bank[m][:, 0:NODES], lambda k: weight(("w3",), k)[:, m * P:(m + 1) * P],
                        lambda k: xT[:, k, :] if k < KT else yT[:, k - KT, :], 2 * KT, mish_g)
            arrived("w4", 0)
            arrived("w4", 1)
            pe.wait_ge(mish_r, MISH + KT)
            for t in range(NT):
                product(bank[4 + t][:, :], lambda k: tile(hidT, k, t), lambda k: weight(("w4",), k), KT, node_g)

            turn(xn)

            def turn_quant(j, u, at):
                pe.wait_ge(quant_r, at + j + 1)
                for c in range(3):
                    for g in range(4):
                        last = pe.transpose(bank[c][:, g * P:(g + 1) * P], qa[:, (4 * c + g) * P:(4 * c + g + 1) * P], ident[:, :])
                    last.then_inc(q_turned, 1)

            def up1(j, u, at):
                pe.wait_ge(qT_a, at * 2 + 2 * j + 2)
                pe.wait_ge(qT_v, at + j + 1)
                for c in range(2):
                    for k in range(KT):
                        last = pe.matmul(bank[3 + c][:, 0:NODES], qT[:, u, c, k * P:(k + 1) * P], xT[:, k, :], start=(k == 0), stop=(k == KT - 1))
                last.then_inc(up_g, 1)

            def step1(j, at):
                up1(j, j % 2, at)
                if j < JT1 - 1:
                    turn_quant(j + 1, (j + 1) % 2, at)
                pe.wait_ge(hid_r, at + UP1 + j + 1)
                for t in range(NT):
                    last = pe.matmul(bank[5 + t][:, :], act2[:, j % 2, t * P:(t + 1) * P], qT[:, j % 2, 2, :],
                                     start=(j == 0), stop=(j == JT1 - 1), skip_group_check=True)
                last.then_inc(down_g, 1)

            turn_quant(0, 0, 0)
            step1(0, 0)
            with pe.Fori(0, 4) as i:
                for j in (1, 2):
                    step1(j, i * 2)
            step1(9, 0)
            step1(10, 0)

            turn(xn)
            values(("ws",), value_g)
            pe.wait_ge(pq_r, 1)
            for t in range(NT):
                last = pe.transpose(bank[3][0:8, t * P:(t + 1) * P], pq[:, 1, t, :], ident[:, :])
            last.then_inc(pqT_g, 1)
            pe.wait_ge(pqT_r, 1)

            def source_row(h):
                if h >= 2:
                    pe.wait_ge(score_r, NT * (h - 1))
                pe.matmul(bank[3 + h % 2][:, 0:NODES], sel8[:, h, :], qT2, start=True, stop=True).then_inc(srow_g, 1)

            turn_head, weighted = attend(HEADS, weighed, 0)
            source_row(0)
            source_row(1)
            for h in range(HEADS):
                turn_head(h)
                if h + 2 < HEADS:
                    source_row(h + 2)
                if h:
                    weighted(h - 1)
            weighted(HEADS - 1)

            turn(xn)
            router(1)
            pe.wait_ge(mask_r, 1)
            for t in range(NT):
                for k in range(t + 1):
                    last = pe.matmul(bank[7][:, 32 + t * 8:40 + t * 8], (upper if k == t else ones)[:, :], sm(2)[:, k, :],
                                     start=(k == 0), stop=(k == t))
            last.then_inc(pos_g, 1)
            expert_bias(2, 1)

            def up2(v, j, at):
                s = f2[2 * v]
                if j == 0:
                    pe.wait_ge(arrive[s], at * 8 + (f2_base[s] + 16))
                product_in(bank[j % 2][:, 0:NODES], s, j, 2 * P)
                last_product[0].then_inc(up_g, 1)

            def down2(v, j, at):
                s = f2[2 * v + 1]
                if j == 0:
                    pe.wait_ge(arrive[s], at * 8 + (f2_base[s] + 16))
                    pe.wait_ge(added, at * NT + (ADD2 + NT * v))
                down(at * JT2 + (UP2 + JT2 * v + j + 1), j, JT2, wslot(s, 2)[:, j, :], 4)

            with pe.Fori(0, EXPERTS // 2) as i:
                for v in range(2):
                    up2(v, 0, i * 2)
                    up2(v, 1, i * 2)
                    down2(v, 0, i * 2)
                    down2(v, 1, i * 2)

            turn(xn)
            for r in range(4):
                arrived("wr", r, 0)
                arrived("wr", r, 1)
                for t in range(NT):
                    n = r * NT + t
                    if n >= 4:
                        pe.wait_ge(rel_r, n - 3)
                    product(bank[n % 4][:, :], lambda k: tile(xT, k, t), lambda k: weight(("wr", r), k), KT, rel_g)
            values(("wself",), node_g)
            pe.wait_ge(wdeg_r, 1)
            pe.wait_ge(rel_r, 4 * NT)
            pe.matmul(bank[3][:, 0:2 * NT], zeros[:, :], zeros[:, 0:2 * NT], start=True, stop=False, skip_group_check=True)

            def sum3(n, at):
                pe.wait_ge(em_ready, at + (2 * NB + n + 1))
                pe.wait_ge(msg_lo, at + (4 * NB + n + 1))
                for t in range(NT):
                    lhs = em[:, n % 4, t * P:(t + 1) * P]
                    for p, part in enumerate((mh, ml)):
                        last = pe.matmul(bank[t][:, :], lhs, part[:, n % 4, :], start=(n, p) == (0, 0), stop=(n, p) == (ET - 1, 1), skip_group_check=True)
                        if (n, p) == (ET - 1, 1):
                            last.then_inc(agg_g, 1)
                    last = pe.matmul(bank[3][:, 2 * t:2 * t + 2], lhs, wdeg[:, bass.ds(at + n, 1), :].rearrange("p a b -> p (a b)"),
                                     start=False, stop=(n, t) == (ET - 1, NT - 1), skip_group_check=True)
                last.then_inc(agg_g if n == ET - 1 else m_used, 1)

            for n in range(RING):
                sum3(n, 0)
            with pe.Fori(0, 4) as i:
                for c in range(RING, 2 * RING):
                    sum3(c, i * RING)
            for n in range(5 * RING, 6 * RING):
                sum3(n, 0)
            turn(y)
            for k in range(4):
                arrived("wf1", k)
            for m in range(8):
                if m >= 4:
                    pe.wait_ge(gelu_r, m - 3)
                product(bank[m % 4][:, 0:NODES], lambda k: wring[:, W["wf1", k][0], m * P:(m + 1) * P], lambda k: yT[:, k, :], KT, node_g)
            for c in range(4):
                arrived("wf2", c)
            pe.wait_ge(gelu_r, 8)
            for t in range(NT):
                product(bank[4 + t][:, :], lambda k: tile(hidT, k, t), lambda k: weight(("wf2",), k), 8, node_g)

            turn(xn)
            for k in range(KT):
                last = pe.matmul(bank[7][0:8, 0:NODES], gatew[:, 2, k, :], xT[:, k, :], start=(k == 0), stop=(k == KT - 1))
            last.then_inc(route_g, 1)
            with pe.Fori(0, SINKHORN) as i:
                pe.wait_ge(sk_d, i * 8 + 4)
                for t in range(NT):
                    last = pe.matmul(bank[0][:, t * 8:t * 8 + 8], sink[:, 0, t * P:(t + 1) * P], ident[0:8, 0:8], start=True, stop=True)
                last.then_inc(sk_p, 1)
                pe.wait_ge(sk_d, i * 8 + 8)
                for t in range(NT):
                    last = pe.transpose(bank[1][0:8, t * P:(t + 1) * P], sinka[:, 0, t, :], ident[:, :])
                last.then_inc(sk_p, 1)
            pe.wait_ge(chosen_r, 1)
            for c in range(2):
                for t in range(NT):
                    last = pe.transpose(bank[7][:, (c * NT + t) * 8:(c * NT + t) * 8 + 8], sink[:, 3 + c, t * P:(t + 1) * P], ident[0:8, 0:8])
            last.then_inc(sk_p, 1)

            def expert3(v, at):
                for c in range(2):
                    s = f3[2 * v + c]
                    pe.wait_ge(arrive[s], at * 8 + (f3_base[s] + 16))
                pe.wait_ge(added, at * NT + (ADD3 + NT * (v - 1)))
                for t in range(NT):
                    for k in range(KT):
                        last = pe.matmul(bank[3 * v + t][:, :], tile(xT, k, t), wslot(f3[2 * v + k // 2], 2)[:, k % 2, :],
                                         start=(k == 0), stop=(k == KT - 1))
                last.then_inc(down_g, 1)

            with pe.Fori(0, EXPERTS // 2) as i:
                for v in range(2):
                    expert3(v, i * 2)


def kernel(**inputs):
    import numpy as np
    import concourse.bacc as bacc
    from concourse.bass_utils import run_bass_kernel_spmd

    given = {k: np.ascontiguousarray(v) for k, v in inputs.items()}
    sent = dict(given)
    for name, new in (("src", "src_c"), ("dst", "dst_c"), ("edge_type_4", "typ_c"), ("edge_weight", "ew_c")):
        sent[new] = given[name].reshape(ET, P).T
    sent["attrT"] = given["edge_attr_64"].T
    sent["bwa"], sent["bwb"] = given["L0_gnn_bw"][:512], given["L0_gnn_bw"][512:]
    sent["L0_ffn_b1"] = given["L0_ffn_b1"].reshape(EXPERTS, 2 * JT0, P).transpose(2, 0, 1)
    sent["L2_ffn_b1"] = given["L2_ffn_b1"].reshape(EXPERTS, JT2, P).transpose(2, 0, 1)
    sent["L1_gnn_b3"] = given["L1_gnn_b3"].reshape(KT, P).T
    sent["L3_gnn_b_ffn1"] = given["L3_gnn_b_ffn1"].reshape(8, P).T
    sent["L2_gnn_Ws"] = given["L2_gnn_Ws"].transpose(1, 0, 2).reshape(DIM, DIM)
    sent["L2_gnn_Wb"] = given["L2_gnn_Wb"].reshape(DIM)
    sent["L2_gnn_at"] = given["L2_gnn_a_w"][:, :HD].reshape(DIM)
    sent["L2_gnn_as"] = given["L2_gnn_a_w"][:, HD:].reshape(DIM)
    sent["L3_ffn_gate_w"] = given["L3_ffn_gate_w"][0]
    for name in ("edge_attr_64", "edge_type_4", "edge_weight", "L0_gnn_bw", "L2_gnn_a_w"):
        del sent[name]

    nc = bacc.Bacc("TRN2", target_bir_lowering=False, num_devices=1)
    arrays, a = {}, {}
    for name, value in sent.items():
        value = np.ascontiguousarray(value)
        arrays[f"in_{name}"] = value
        a[name] = nc.dram_tensor(f"in_{name}", value.shape, mybir.dt.from_np(value.dtype), kind="ExternalInput").ap()
    out = nc.dram_tensor("out", (NODES, DIM), F32, kind="ExternalOutput").ap()
    table0 = nc.dram_tensor("pair_logits", (NODES * NODES, HEADS), F32, kind="Internal").ap()
    table3 = nc.dram_tensor("relation_rows", (NODES * 4, DIM), F32, kind="Internal").ap()
    build(nc, a, out, table0, table3)
    return run_bass_kernel_spmd(nc, [arrays], core_ids=[0]).results[0]["out"]
```

```python
from contextlib import ExitStack

import concourse.bass as bass
from concourse import mybir

F32 = mybir.dt.float32
F32R = mybir.dt.float32r
BF16 = mybir.dt.bfloat16
I32 = mybir.dt.int32
ALU = mybir.AluOpType
ACT = mybir.ActivationFunctionType
AX = mybir.AxisListType

P = 128
NODES, DIM, EDGES = 384, 512, 6144
NT, KT = NODES // P, DIM // P
ET = EDGES // P
BLK = 512
NB, SUB = EDGES // BLK, BLK // P
HEADS, HD = 8, 64
EPS = 1e-5
NONE = -3e38
FF0, FF1 = 1024, 1408
JT0, JT1, JT2 = FF0 // P, FF1 // P, 2
EXPERTS = 8
CAP = 120
TOP = NODES // EXPERTS
SINKHORN = 8
SLOTS, SW = 6, 1024
SE = P
RING = 8

MISH = 4 + 8 * (NB - 1) + 4
N_SMALL = 15

UP0, UP1 = 0, EXPERTS * JT0
UP2 = UP1 + JT1
UP3 = UP2 + EXPERTS * JT2
ADD1 = 1
ADD2 = ADD1 + NT
ADD3 = ADD2 + 1
ADDED = ADD3 + EXPERTS * NT


class Steps:

    def __init__(self, engine, own):
        self.engine, self.own, self.base, self.local, self.per, self.i = engine, own, {}, {}, {}, None

    def __call__(self, instruction, sem=None):
        sem = sem or self.own
        instruction.then_inc(sem, 1)
        key = sem.name
        self.local[key] = self.local.get(key, 0) + 1
        value = self.base.get(key, 0) + self.local[key]
        if self.i is not None:
            value = self.i * self.per[key] + value
        self.engine.wait_ge(sem, value)

    def fold(self):
        for key, n in self.local.items():
            self.base[key] = self.base.get(key, 0) + n
        self.local = {}

    def skip(self, sem, n):
        self.base[sem.name] = self.base.get(sem.name, 0) + n

    def enter(self, i, per):
        self.fold()
        self.i, self.per = i, {s.name: n for s, n in per.items()}

    def leave(self, iterations):
        for key, n in self.local.items():
            assert n == self.per[key], (key, n, self.per[key])
            self.base[key] = self.base.get(key, 0) + iterations * n
        self.local, self.i = {}, None


def build(nc, a, out, table0, table3):
    with ExitStack() as ctx:
        def sb(name, shape, dt=F32, within=None):
            return (within or ctx).enter_context(nc.sbuf_tensor(name, shape, dt))

        def sem(name):
            return ctx.enter_context(nc.semaphore(name))

        bank = [ctx.enter_context(nc.psum_tensor(f"bank{i}", [P, 512], F32)) for i in range(8)]

        x = sb("x", [P, NT, DIM])
        xn = sb("xn", [P, NT, DIM])
        xT = sb("xT", [P, KT, NODES])
        hold = sb("hold", [P, 3, NT * DIM])
        y = hold[:, 0, :].rearrange("p (t d) -> p t d", t=NT)
        vn = hold[:, 1, :].rearrange("p (t d) -> p t d", t=NT)
        yT = hold[:, 2, :].rearrange("p (k n) -> p k n", k=KT)
        hT = hold[:, :, :].rearrange("p a b -> p (a b)")[:, 0:4096].rearrange("p (a f n) -> p a f n", a=2, f=KT)
        tmp = sb("tmp", [P, 2, DIM])
        wring = sb("wring", [P, SLOTS, SW])
        rows = sb("rows", [P, 6, DIM])
        count = sb("count", [P, NT, NODES])
        stats = sb("stats", [P, 6])
        mv = sb("mv", [P, NT, 2])
        varp = sb("varp", [P, NT])
        rstd = sb("rstd", [P, NT])
        half = sb("half", [P, NT])
        two = sb("two", [P, 1])
        ident = sb("ident", [P, P])
        zeros = sb("zeros", [P, P])
        ones = sb("ones", [P, P])
        upper = sb("upper", [P, P])
        nodeid = sb("nodeid", [P, NT])
        iota = sb("iota", [P, NODES])
        sel8 = sb("sel8", [8, 8, P])
        low8 = sb("low8", [P, 8, 8])
        srcc = sb("srcc", [P, ET], I32)
        dstc = sb("dstc", [P, ET], I32)
        typc = sb("typc", [P, ET], I32)
        ewc = sb("ewc", [P, ET])
        srcf = sb("srcf", [P, ET])
        dstf = sb("dstf", [P, ET])
        pair = sb("pair", [P, ET], I32)
        rrow = sb("rrow", [P, ET], I32)
        logit = sb("logit", [P, ET, HEADS])
        ba = sb("ba", [P, 1])
        wa = sb("wa", [P, 1])
        ab = sb("ab", [P, 8])
        b1e0 = sb("b1e0", [P, EXPERTS, 2 * JT0])
        b1e2 = sb("b1e2", [P, EXPERTS, JT2])
        b2e = sb("b2e", [8, 2, DIM])
        b3c = sb("b3c", [P, KT])
        bf1 = sb("bf1", [P, 8])
        gatew = sb("gatew", [P, 3, KT, 8])
        br = sb("br", [P, 2, 8])
        w1c = sb("w1c", [64, DIM])
        small = sb("small", [P, 8, NT * 8])
        small1 = sb("small1", [P, 4, NT])
        cmp8 = sb("cmp8", [P, 2, NT * 8, 8])
        coef = sb("coef", [P, NT, 8])
        coefT = sb("coefT", [8, NODES])
        mneg = sb("mneg", [P, NT, HEADS])
        den = sb("den", [P, NT, HEADS])
        pq = sb("pq", [P, 2, NT, HEADS])
        crowd = sb("crowd", [P, EXPERTS], I32)
        eidx = sb("eidx", [P, 2, BLK], I32)

        with ExitStack() as third:
            eh = sb("eh", [P, 2, NT, NODES], within=third)
            eT = sb("eT", [P, 2, NT, NODES], within=third)
            sink = sb("sink", [8, 5, NODES], within=third)
            sinks = sb("sinks", [8, 8], within=third)
            sinka = sb("sinka", [P, 6, NT, 8], within=third)
        with ExitStack() as third:
            more = sb("more", [P, 6, SW], within=third)
            sb("beside_xsplit", [P, 3 * SW], within=third)
            cplace = sb("cplace", [P, NT, EXPERTS * SE], within=third)
        with ExitStack() as second:
            tabs1 = sb("tabs1", [P, 2, 2, NT, 512], F32R, within=second)
            em = sb("em", [P, SUB, NODES], F32R, within=second)
            mh = sb("mh", [P, SUB, DIM], F32R, within=second)
            ml = sb("ml", [P, SUB, DIM], F32R, within=second)
        tabs0 = sb("tabs0", [P, 2, 2, NT, 1024], F32R)
        tabsf = tabs0[:, :, :, :, :].rearrange("p a b t n -> p (a b t n)")
        xsplit = tabsf[:, 6144:9216].rearrange("p (c t n) -> p c t n", c=2, t=NT)
        with ExitStack() as second:
            big = sb("big", [P, NT, NODES * HEADS], within=second)
            wdeg = sb("wdeg", [P, ET, 2], F32R, within=second)
        onehot = sb("onehot", [P, 2, 2, NT, BLK], F32R)
        work = sb("work", [P, 3, 4, 512])
        attr = sb("attr", [64, 2, BLK])
        relu4, leaky4 = work[:, 0, :, :], work[:, 1, :, :]
        ebf = work[:, 2, :, :].rearrange("p a b -> p (a b)")[:, 0:1536].bitcast(BF16).rearrange(
            "p (s c n) -> p s c n", s=SUB, c=2)
        mz, mt, mr = work[:, 0, :, :], work[:, 1, :, :], work[:, 2, :, :]
        bigf = big[:, :, :].rearrange("p a b -> p (a b)")
        silu2 = bigf[:, 0:768].rearrange("p (a n) -> p a n", a=2)
        act2 = bigf[:, 768:1536].rearrange("p (a n) -> p a n", a=2)
        qraw = bigf[:, 1536:4608].rearrange("p (a c n) -> p a c n", a=2, c=3)
        qa = bigf[:, 4608:6144]
        qb = bigf[:, 6144:7680]
        qs = cmp8[:, 0, 0:12, 0:3]
        gather = bigf[:, 0:4096].rearrange("p (a n) -> p a n", a=RING)
        stage = bigf[:, 0:6144].rearrange("p (a n) -> p a n", a=4 * NT)
        brel = bigf[:, 7168:9216].rearrange("p (a n) -> p a n", a=4)
        hidT = bigf[:, 0:3072].rearrange("p (f n) -> p f n", f=8)
        msg4 = bigf[:, 4096:6144].rearrange("p (a n) -> p a n", a=4)
        negm = bigf[:, 0:1152].rearrange("p (t n) -> p t n", t=NT)
        srow = bigf[:, 1152:2304].rearrange("p (a n) -> p a n", a=3)
        qT2 = bigf[0:8, 2304:2688]
        prod = bigf[:, 3072:3584]
        cplaceT = bigf[:, 5632:8704].rearrange("p (e n) -> p e n", e=EXPERTS)
        holdf = hold[:, :, :].rearrange("p a b -> p (a b)")
        cp2 = holdf[:, 2048:2048 + 2 * NODES].rearrange("p (a n) -> p a n", a=2)
        cpl = holdf[:, 2816:2816 + 2 * NODES].rearrange("p (t n) -> p t n", t=NT)
        qT = hold[:, :, :].rearrange("p a b -> p (a b)")[:, 0:3072].rearrange("p (a c n) -> p a c n", a=2, c=3)

        dve_s, act_s, pool_s = sem("dve_step"), sem("act_step"), sem("pool_step")
        arrive = [sem(f"slot{i}_loaded") for i in range(SLOTS)]
        x_loaded, edges_loaded, small_loaded, rows_loaded = map(sem, ("x_loaded", "edges_loaded", "small_loaded", "rows_loaded"))
        consts_ready, none_ready = sem("consts_ready"), sem("none_ready")
        var_ready, rstd_ready = sem("variance_ready"), sem("deviation_ready")
        nodes_ready, turned, xT_a, xT_v = sem("nodes_ready"), sem("nodes_turned"), sem("xT_act_half"), sem("xT_dve_half")
        value_g, v_ready = sem("value_product"), sem("value_ready")
        table_g, tab_sum, tab_hi, tab_lo = sem("table_product"), sem("table_sum"), sem("table_high"), sem("table_low")
        ix_loaded, at_loaded = sem("block_index_loaded"), [sem("attr_loaded0"), sem("attr_loaded1")]
        oh_ready, em_ready = sem("onehot_ready"), sem("edge_onehot_ready")
        z_g, relu_r, leaky_r, logit_g, logit_r = map(sem, ("z_product", "relu_ready", "leaky_ready", "logit_product", "logit_ready"))
        count_g = sem("count_product")
        pairs_r, filled, written, big_loaded = map(sem, ("pair_rows_ready", "table0_filled", "table0_written", "pair_logits_loaded"))
        max_r, score_r, e_ready, e_turned, eT_ready, y_g = map(sem, ("row_max_ready", "score_ready", "weight_ready", "weight_turned", "weightT_ready", "attention_product"))
        elu_in, elu_ex = sem("elu_input"), sem("elu_exp")
        route_g, route_d, route_a, coefT_g, coefT_r, b2_g = map(sem, ("router_product", "router_dve", "router_act", "coef_turned", "coefT_ready", "expert_bias_product"))
        up_g, silu_r, hid_r, down_g, added = map(sem, ("up_product", "silu_ready", "hidden_ready", "down_product", "down_added"))
        mish_g, mish_in, mish_ex, mish_sq, mish_rc, mish_q, mish_r = map(sem, ("mish_product", "mish_input", "mish_exp", "mish_square", "mish_reciprocal", "mish_ratio", "mish_ready"))
        msg_hi, msg_lo, agg_g = sem("message_high"), sem("message_low"), sem("aggregate_product")
        node_g, node_r = sem("node_product"), sem("node_result")
        q_loaded, quant_r, q_turned, qT_a, qT_v = [sem("quant_raw_loaded0"), sem("quant_raw_loaded1")], sem("quantized"), sem("quantized_turned"), sem("quantizedT_act"), sem("quantizedT_dve")
        pq_r, pqT_g, pqT_r, srow_g = sem("score_parts_ready"), sem("score_parts_turned"), sem("score_partsT_ready"), sem("score_row_product")
        rel_g, rel_r, rel_w = sem("relation_product"), sem("relation_staged"), sem("relation_written")
        gathered = [sem(f"messages_gathered{i}") for i in range(RING)]
        m_used = sem("scaled_messages_used")
        sk_d, sk_a, sk_p = sem("sinkhorn_dve"), sem("sinkhorn_act"), sem("sinkhorn_turned")
        mish_ln, mish_min, exp2_r, brel_loaded, scaled_r, gelu_r, coef_r, quant_s = map(sem, ("mish_log", "mish_clamped", "score_exp_ready", "relation_bias_loaded", "scaled_ready", "gelu_ready", "coef_ready", "quantize_step"))
        mask_r, pos_g = sem("mask_ready"), sem("position_product")
        weighed, wdeg_r, chosen_r = map(sem, ("weighed_ready", "edge_weights_split", "chosen_ready"))
        out_done = sem("out_written")
        more_loaded = [sem(f"more{i}_loaded") for i in range(6)]
        expert_added = sem("expert_added")

        class Routed:

            def __init__(self, layer, width):
                self.width, self.groups = width, EXPERTS * width // 512
                self.place = tabsf[:, 0:NT * EXPERTS * width].rearrange("p (t n) -> p t n", t=NT)
                n = EXPERTS * width
                self.xgT = [bigf[:, 1536 + k * n:1536 + (k + 1) * n] for k in range(3)] + [holdf[:, 0:n]]
                self.sem = {name: sem(f"r{layer}_{name}") for name in (
                    "split_high", "split_low", "place_ready", "gather_product", "gathered_act", "gathered_dve",
                    "cplace_ready", "cplace_turned", "cplaceT_act", "cplaceT_dve", "cplace_copied",
                    "expert_out", "combined")}

        routed0, routed2 = Routed(0, 2 * SE), Routed(2, SE)
        row_used = sem("rows_used")

        def wslot(s, k):
            return wring[:, s, :].rearrange("p (k n) -> p k n", k=k)

        def sm(i):
            return small[:, i, :].rearrange("p (t e) -> p t e", t=NT)

        def node_rows(w, c):
            return w[c * 2 * P:(c + 1) * 2 * P, :].rearrange("(k p) n -> p k n", p=P)

        ROWS = [["L0_gnn_bv", "bwa", "bwb", "L0_gnn_gamma", "L0_gnn_beta"],
                ["L1_gnn_b1", "L1_gnn_b2", "L1_gnn_b4", "L1_gnn_gamma", "L1_gnn_beta"],
                ["L2_gnn_Wb", "L2_gnn_at", "L2_gnn_as"],
                ["L3_gnn_b_self", "L3_gnn_ln1_g", "L3_gnn_ln1_b", "L3_gnn_ln2_g", "L3_gnn_ln2_b", "L3_gnn_b_ffn2"]]
        rows_before = [16 * sum(len(r) for r in ROWS[:i + 1]) for i in range(4)]

        def row(layer, name, w=1):
            r = ROWS[layer].index(name)
            return rows[:, r:r + w, :].rearrange("p a b -> p (a b)")

        owner, arrivals, plan, cursor = {}, [0] * SLOTS, [], [0]

        def stream(src, k, freed_by):
            s = cursor[0] % SLOTS
            cursor[0] += 1
            arrivals[s] += 1
            plan.append((s, src, k, owner.get(s)))
            owner[s] = freed_by
            return s, 16 * arrivals[s]

        def reserve(n, uses, freed_by):
            base = [(cursor[0] + i) % SLOTS for i in range(n)]
            cursor[0] += n
            before = [owner[s] for s in base if s in owner], {s: 16 * arrivals[s] for s in base}
            for s in base:
                arrivals[s] += uses
                owner[s] = freed_by
            return base, *before

        W = {}
        for c in range(2):
            W["wv", c] = stream(node_rows(a["L0_gnn_Wv"], c), 2, (value_g, NT))
        for k in range(8):
            W["ww", k] = stream(a["L0_gnn_Ww"][k * P:(k + 1) * P, :].unsqueeze(1), 1, (table_g, 6 if k < 4 else 12))
        f0, f0_before, f0_base = reserve(6, EXPERTS, (down_g, UP1))
        slots0 = [(wring[:, s, :], arrive[s], f0_base[s]) for s in f0] + [(more[:, i, :], more_loaded[i], 0) for i in range(6)]
        plan.append("layer0")
        for c in range(4):
            W["w1", c] = stream(node_rows(a["L1_gnn_W1"], c), 2, (table_g, 12 + (3 if c < 2 else 6)))
        for c in range(2):
            W["w2", c] = stream(node_rows(a["L1_gnn_W2"], c), 2, (agg_g, NT))
        plan.append("edges1")
        for c in range(4):
            W["w3", c] = stream(node_rows(a["L1_gnn_W3"], c), 2, (mish_g, MISH + KT))
        for c in range(2):
            W["w4", c] = stream(node_rows(a["L1_gnn_W4"], c), 2, (node_g, NT))
        plan.append("ffn1")
        for c in range(2):
            W["ws", c] = stream(node_rows(a["L2_gnn_Ws"], c), 2, (value_g, 2 * NT))
        f2, f2_before, f2_base = reserve(4, EXPERTS // 2, (down_g, UP3))
        plan.append("ffn2")
        for r in range(4):
            for c in range(2):
                W["wr", r, c] = stream(node_rows(a["L3_gnn_W_rel"][r], c), 2, (rel_g, NT * (r + 1)))
        for c in range(2):
            W["wself", c] = stream(node_rows(a["L3_gnn_W_self"], c), 2, (node_g, 2 * NT))
        for k in range(4):
            W["wf1", k] = stream(a["L3_gnn_W_ffn1"][k * P:(k + 1) * P, :].unsqueeze(1), 1, (node_g, 2 * NT + 8))
        for c in range(4):
            W["wf2", c] = stream(node_rows(a["L3_gnn_W_ffn2"], c), 2, (node_g, 3 * NT + 8))
        f3, f3_before, f3_base = reserve(4, EXPERTS // 2, None)
        plan.append("ffn3")

        def mish_tile(n):
            if n < 4:
                return "z", 0, n
            b, q = divmod(n - 4, 8)
            if b == NB - 1:
                return "m", b, q
            return ("m", b, q - 3) if 3 <= q < 7 else ("z", b + 1, min(q, 3))


        block = ctx.enter_context(nc.Block())

        @block.sync
        def _(sp):
            sp.dma_start(x[:, :, :], a["x"].rearrange("(t p) d -> p t d", p=P)).then_inc(x_loaded, 16)
            for dst, name in ((srcc, "src_c"), (dstc, "dst_c"), (typc, "typ_c"), (ewc, "ew_c")):
                sp.dma_start(dst[:, :], a[name]).then_inc(edges_loaded, 16)

            def load_index(at):
                sp.dma_start(eidx[:, 0, :], a["src"][bass.ds(at, BLK)].partition_broadcast(P)).then_inc(ix_loaded, 16)
                sp.dma_start(eidx[:, 1, :], a["dst"][bass.ds(at, BLK)].partition_broadcast(P)).then_inc(ix_loaded, 16)

            def layer0():
                load_index(0)
                with sp.Fori(1, NB) as b:
                    sp.wait_ge(oh_ready, b)
                    load_index(b * BLK)
                sp.wait_ge(written, 16 * ET)
                sp.wait_ge(count_g, NB)
                for t in range(NT):
                    sp.dma_start(big[:, t, :], table0.rearrange("(t p n) h -> t p (n h)", t=NT, p=P)[t]).then_inc(big_loaded, 16)
                for wait in f0_before:
                    sp.wait_ge(*wait)

                def load(e, j):
                    for q, lo in ((0, 2 * j * P), (1, FF0 + 2 * j * P)):
                        slot, loaded, _ = slots0[3 * j + q]
                        sp.dma_start(slot.rearrange("p (k n) -> p k n", k=KT), a["L0_ffn_W1"][e, :, lo:lo + 2 * P].rearrange("(k p) n -> p k n", p=P)).then_inc(loaded, 16)
                    slot, loaded, _ = slots0[3 * j + 2]
                    sp.dma_start(slot.rearrange("p (k n) -> p k n", k=2), a["L0_ffn_W2"][e, 2 * j * P:(2 * j + 2) * P, :].rearrange("(k p) n -> p k n", p=P)).then_inc(loaded, 16)

                for j in range(JT0 // 2):
                    if j == 2:
                        sp.wait_ge(routed0.sem["gather_product"], KT * routed0.groups)
                    load(0, j)
                with sp.Fori(1, EXPERTS) as e:
                    for j in range(JT0 // 2):
                        sp.wait_ge(down_g, e * JT0 + (2 * (j + 1) - JT0))
                        load(e, j)

            def edges1():
                sp.wait_ge(oh_ready, NB)
                sp.wait_ge(added, ADD1)
                load_index(0)
                for u in range(2):
                    sp.dma_start(attr[:, u, :], a["attrT"][:, u * BLK:(u + 1) * BLK]).then_inc(at_loaded[u], 16)
                sp.wait_ge(oh_ready, NB + 1)
                load_index(BLK)
                with sp.Fori(1, NB // 2) as i:
                    for u in range(2):
                        sp.wait_ge(oh_ready, i * 2 + (NB + u))
                        load_index(i * (2 * BLK) + u * BLK)
                        sp.wait_ge(mish_g, i * 16 + 4 + 8 * (u - 2))
                        sp.dma_start(attr[:, u, :], a["attrT"][:, bass.ds(i * (2 * BLK) + u * BLK, BLK)]).then_inc(at_loaded[u], 16)

            def ffn1():
                def load(u, j):
                    sp.dma_start(qraw[:, u, 0, :], a["L1_ffn_w_gate"][bass.ds(j * P, P), :]).then_inc(q_loaded[u], 16)
                    sp.dma_start(qraw[:, u, 1, :], a["L1_ffn_w_up"][bass.ds(j * P, P), :]).then_inc(q_loaded[u], 16)
                    sp.dma_start(qraw[:, u, 2, :].rearrange("p (g n) -> p g n", g=4),
                                 a["L1_ffn_w_down"][:, bass.ds(j * P, P)].rearrange("(g p) n -> p g n", p=P)).then_inc(q_loaded[u], 16)

                sp.wait_ge(node_g, NT)
                load(0, 0)
                load(1, 1)
                with sp.Fori(1, JT1 // 2) as i:
                    for u in range(2):
                        sp.wait_ge(quant_r, i * 2 + (u - 1))
                        load(u, i * 2 + u)
                sp.wait_ge(quant_r, JT1 - 2)
                load(0, JT1 - 1)

            def ffn2():
                def load(e, v):
                    s1, s2 = f2[2 * v], f2[2 * v + 1]
                    sp.dma_start(wslot(s1, KT), a["L2_ffn_W1"][e].rearrange("(k p) n -> p k n", p=P)).then_inc(arrive[s1], 16)
                    sp.dma_start(wslot(s2, 2), a["L2_ffn_W2"][e].rearrange("(k p) n -> p k n", p=P)).then_inc(arrive[s2], 16)

                for wait in f2_before:
                    sp.wait_ge(*wait)
                load(0, 0)
                load(1, 1)
                with sp.Fori(1, EXPERTS // 2) as i:
                    for v in range(2):
                        sp.wait_ge(down_g, i * (2 * JT2) + (UP2 + JT2 * (v - 1)))
                        load(i * 2 + v, v)

            def ffn3():
                def load(e, v):
                    for c in range(2):
                        s = f3[2 * v + c]
                        sp.dma_start(wslot(s, 2), node_rows(a["L3_ffn_experts"][e], c)).then_inc(arrive[s], 16)

                for wait in f3_before:
                    sp.wait_ge(*wait)
                load(0, 0)
                load(1, 1)
                with sp.Fori(1, EXPERTS // 2) as i:
                    for v in range(2):
                        sp.wait_ge(down_g, i * 2 + (UP3 + v - 1))
                        load(i * 2 + v, v)

            parts = {"layer0": layer0, "edges1": edges1, "ffn1": ffn1, "ffn2": ffn2, "ffn3": ffn3}
            for item in plan:
                if isinstance(item, str):
                    parts[item]()
                    continue
                s, src, k, before = item
                if before is not None:
                    sp.wait_ge(*before)
                sp.dma_start(wslot(s, k), src).then_inc(arrive[s], 16)
            sp.wait_ge(added, ADDED)
            sp.dma_start(out.rearrange("(t p) d -> p t d", p=P), x[:, :, :]).then_inc(out_done, 16)
            sp.wait_ge(out_done, 16)

        @block.gpsimd
        def _(pool):
            step = Steps(pool, pool_s)
            step(pool.memset(big[:, 0, :], NONE), none_ready)
            for tile, value in ((ident, 0.0), (zeros, 0.0), (ones, 1.0), (upper, 1.0), (half, -0.5), (two, 2.0), (sel8, 0.0), (low8, 1.0)):
                step(pool.memset(tile[:], value))
            step(pool.affine_select(out=ident[:, :], in_=ident[:, :], compare_op=ALU.not_equal, fill=1.0, base=0,
                                    pattern=[[-1, P]], channel_multiplier=1))
            step(pool.affine_select(out=upper[:, :], in_=upper[:, :], compare_op=ALU.is_gt, fill=0.0, base=0,
                                    pattern=[[1, P]], channel_multiplier=-1))
            step(pool.affine_select(out=sel8[:, :, :], in_=sel8[:, :, :], compare_op=ALU.not_equal, fill=1.0, base=0,
                                    pattern=[[-1, 8], [0, P]], channel_multiplier=1))
            step(pool.affine_select(out=low8[:, :, :], in_=low8[:, :, :], compare_op=ALU.is_gt, fill=0.0, base=0,
                                    pattern=[[1, 8], [-1, 8]], channel_multiplier=0))
            step(pool.iota(nodeid[:, :], pattern=[[P, NT]], base=0, channel_multiplier=1, allow_small_or_imprecise_dtypes=True))
            step(pool.iota(iota[:, :], pattern=[[1, NODES]], base=0, channel_multiplier=0, allow_small_or_imprecise_dtypes=True), consts_ready)
            done = [0]

            def deviations(n):
                for _ in range(n):
                    done[0] += 1
                    pool.wait_ge(var_ready, done[0])
                    step(pool.tensor_tensor(rstd[:, :], varp[:, :], half[:, :], ALU.pow), rstd_ready)

            deviations(1)
            pool.wait_ge(pairs_r, 1)
            pool.wait_ge(filled, 16 * NT)
            for b in range(NB):
                pool.wait_ge(logit_r, b + 1)
                for s in range(SUB):
                    e = b * SUB + s
                    if e:
                        pool.wait_ge(written, 16 * e)
                    pool.indirect_dma_start(out=table0, out_offset=bass.IndirectOffsetOnAxis(ap=pair[:, e:e + 1], axis=0),
                                            in_=logit[:, e, :], in_offset=None).then_inc(written, 16)
            deviations(3)

            def ratio(n, at):
                pool.wait_ge(mish_sq, at + n + 1)
                pool.wait_ge(mish_rc, at + n + 1)
                pool.tensor_tensor(mr[:, n % 4, :], mr[:, n % 4, :], mt[:, n % 4, :], ALU.mult).then_inc(mish_q, 1)

            for n in range(4):
                ratio(n, 0)
            with pool.Fori(0, NB - 1) as i:
                for q in range(8):
                    ratio(4 + q, i * 8)
            for n in range(MISH - 4, MISH + 4):
                ratio(n, 0)
            deviations(5)
            pool.wait_ge(rel_w, 16 * 4 * NT)
            for e in range(ET):
                if e >= RING:
                    pool.wait_ge(msg_lo, 4 * NB + e - RING + 1)
                pool.indirect_dma_start(out=gather[:, e % RING, :], out_offset=None, in_=table3,
                                        in_offset=bass.IndirectOffsetOnAxis(ap=rrow[:, e:e + 1], axis=0)).then_inc(gathered[e % RING], 16)
            deviations(3)

        @block.scalar
        def _(act):
            step = Steps(act, act_s)
            for r, name in enumerate(ROWS[0]):
                act.dma_start(rows[:, r, :], a[name].partition_broadcast(P)).then_inc(rows_loaded, 16)
            act.wait_ge(none_ready, 1)
            for t in range(NT):
                act.dma_start(table0.rearrange("(t p n) h -> t p (n h)", t=NT, p=P)[t], big[:, 0, :]).then_inc(filled, 16)
            smalls = ((ba[:, :], a["L0_gnn_ba"].partition_broadcast(P)), (wa[:, :], a["L0_gnn_Wa"]),
                      (ab[:, :], a["L2_gnn_a_b"].partition_broadcast(P)), (b1e0[:, :, :], a["L0_ffn_b1"]),
                      (b1e2[:, :, :], a["L2_ffn_b1"]), (b2e[:, 0, :], a["L0_ffn_b2"]), (b2e[:, 1, :], a["L2_ffn_b2"]),
                      (b3c[:, :], a["L1_gnn_b3"]), (bf1[:, :], a["L3_gnn_b_ffn1"]),
                      (gatew[:, 0, :, :], a["L0_ffn_Wg"].rearrange("(k p) e -> p k e", p=P)),
                      (gatew[:, 1, :, :], a["L2_ffn_Wr"].rearrange("(k p) e -> p k e", p=P)),
                      (gatew[:, 2, :, :], a["L3_ffn_gate_w"].rearrange("(k p) e -> p k e", p=P)),
                      (br[:, 0, :], a["L0_ffn_bg"].partition_broadcast(P)), (br[:, 1, :], a["L2_ffn_br"].partition_broadcast(P)),
                      (w1c[:, :], a["L1_gnn_W1"][2 * DIM:2 * DIM + 64, :]))
            assert len(smalls) == N_SMALL
            for dst, src in smalls:
                act.dma_start(dst, src).then_inc(small_loaded, 16)

            def load_rows(layer, uses):
                act.wait_ge(row_used, uses)
                for r, name in enumerate(ROWS[layer]):
                    act.dma_start(rows[:, r, :], a[name].partition_broadcast(P)).then_inc(rows_loaded, 16)

            turns = [0]

            def turn(dst):
                for k in (0, 2):
                    act.wait_ge(turned, KT * turns[0] + k + 1)
                    step(act.activation(dst[:, k, :], bank[k][:, 0:NODES], ACT.Copy), xT_a)
                turns[0] += 1

            def split_tables(first, n, tabs, cols):
                for g in range(n):
                    act.wait_ge(tab_sum, first + g + 1)
                    which, r = divmod(g, n // 2)
                    t, c = divmod(r, cols)
                    step(act.activation(tabs[:, which, 0, t, c * 512:c * 512 + 512], tmp[:, g % 2, :], ACT.Copy), tab_hi)

            act.wait_ge(consts_ready, 1)
            turn(xT)
            split_tables(0, 12, tabs0, 2)

            def relu(n, at):
                act.wait_ge(z_g, at + n + 1)
                act.activation(relu4[:, n % 4, :], bank[n % 4][:, :], ACT.Relu, scale=0.99).then_inc(relu_r, 1)

            for n in range(8):
                relu(n, 0)
            with act.Fori(0, 5) as i:
                for c in range(8, 24):
                    relu(c, i * 16)
            for n in range(88, 96):
                relu(n, 0)
            act.wait_ge(big_loaded, 16 * NT)
            act.wait_ge(max_r, 1)
            for h in range(HEADS):
                if h >= 2:
                    act.wait_ge(e_turned, NT * (h - 1))
                for t in range(NT):
                    step(act.activation(eh[:, h % 2, t, :], big[:, t, :].rearrange("p (n h) -> p h n", h=HEADS)[:, h, :],
                                        ACT.Exp, bias=mneg[:, t, h:h + 1], accum_out=den[:, t, h:h + 1]), e_ready)

            def elu(first):
                for t in range(NT):
                    act.wait_ge(elu_in, first + t + 1)
                    step(act.activation(tmp[:, t % 2, :], tmp[:, t % 2, :], ACT.Exp), elu_ex)

            elu(0)
            load_rows(1, 1)
            turn(xT)
            act.wait_ge(small_loaded, 16 * N_SMALL)
            act.wait_ge(route_d, 1)
            step(act.activation(small[:, 1, :], small[:, 1, :], ACT.Exp), route_a)

            def gather_nodes(r):
                s = r.sem
                for t in range(NT):
                    act.activation(xsplit[:, 0, t, :], xn[:, t, :], ACT.Copy).then_inc(s["split_high"], 1)
                for g in range(r.groups):
                    for k in (0, 2):
                        act.wait_ge(s["gather_product"], 4 * g + k + 1)
                        act.activation(r.xgT[k][:, g * 512:g * 512 + 512], bank[4 * (g % 2) + k][:, :], ACT.Copy).then_inc(s["gathered_act"], 1)

            gather_nodes(routed0)
            with act.Fori(0, EXPERTS) as e:
                def expert0(width):
                    for j in range(JT0):
                        act.wait_ge(up_g, e * JT0 + j + 1)
                        act.activation(silu2[:, j % 2, 0:width], bank[j % 2][:, 0:width], ACT.Silu,
                                       bias=b1e0[:, bass.ds(e, 1), j]).then_inc(silu_r, 1)
                    act.wait_ge(down_g, e * JT0 + JT0)
                    if width == 2 * SE:
                        act.activation(tmp[:, 1, :], bank[3][:, :], ACT.Copy)
                    act.activation(tmp[:, 0, :], bank[7][:, :], ACT.Copy).then_inc(routed0.sem["expert_out"], 1)

                chosen_by = act.value_load(crowd[0:1, bass.ds(e, 1)], min_val=0, max_val=NODES)
                with act.If(chosen_by <= SE):
                    expert0(SE)
                with act.Else():
                    with act.If(chosen_by <= 2 * SE):
                        expert0(2 * SE)
                    with act.Else():
                        expert0(NODES)
            turn(xT)
            split_tables(12, 6, tabs1, 1)

            def mish_high(n, at, at_m):
                kind, b, s = mish_tile(n)
                if kind == "m":
                    act.wait_ge(mish_r, at + n + 1)
                    act.activation(mh[:, s, :], mz[:, n % 4, :], ACT.Copy).then_inc(msg_hi, 1)

            def mish_reciprocal(n, at, width=512):
                act.wait_ge(mish_sq, at + n + 1)
                act.activation(mr[:, n % 4, 0:width], mt[:, n % 4, 0:width], ACT.Ln, bias=two[:, 0:1]).then_inc(mish_ln, 1)
                act.wait_ge(mish_ln, at + n + 1)
                act.activation(mr[:, n % 4, 0:width], mr[:, n % 4, 0:width], ACT.Exp, scale=-1.0).then_inc(mish_rc, 1)

            def mish_exp(n, at, width=512):
                act.wait_ge(mish_in, at + n + 1)
                act.activation(mt[:, n % 4, 0:width], mz[:, n % 4, 0:width], ACT.Exp).then_inc(mish_ex, 1)

            def mish_step(n, at, first=0):
                if n - 4 >= first:
                    mish_high(n - 4, at, at)
                if first <= n - 1 < MISH:
                    mish_reciprocal(n - 1, at)
                if n < MISH:
                    mish_exp(n, at)

            nc.scalar.preload_act_table_set("natural_log_exp_and_others")
            for n in range(12):
                mish_step(n, 0)
            with act.Fori(0, 5) as i:
                for c in range(12, 28):
                    mish_step(c, i * 16)
            mish_high(MISH - 8, 0, 0)
            mish_reciprocal(MISH - 5, 0)
            for n in (MISH - 7, MISH - 6, MISH - 5):
                mish_high(n, 0, 0)
            for n in range(MISH - 4, MISH + 4):
                mish_step(n, 0, MISH - 4)
            turn(yT)
            for m in range(KT):
                mish_exp(MISH + m, 0, NODES)
                mish_reciprocal(MISH + m, 0, NODES)
            load_rows(2, 2)
            turn(xT)

            def turn_quant(j, u, at):
                for c in range(2):
                    act.wait_ge(q_turned, at * 3 + 3 * j + c + 1)
                    act.activation(qT[:, u, c, :], bank[c][:, :], ACT.Copy).then_inc(qT_a, 1)

            def hidden1(j, u, at):
                act.wait_ge(up_g, at + UP1 + j + 1)
                act.activation(silu2[:, u, :], bank[3][:, 0:NODES], ACT.Silu).then_inc(silu_r, 1)

            turn_quant(0, 0, 0)
            hidden1(0, 0, 0)
            turn_quant(1, 1, 0)
            with act.Fori(0, 4) as i:
                for j in (1, 2):
                    hidden1(j, j % 2, i * 2)
                    turn_quant(j + 1, (j + 1) % 2, i * 2)
            hidden1(9, 1, 0)
            turn_quant(10, 0, 0)
            hidden1(10, 0, 0)
            turn(xT)
            for h in range(HEADS):
                for t in range(NT):
                    n = h * NT + t
                    act.wait_ge(score_r, n + 1)
                    step(act.activation(srow[:, t, :], srow[:, t, :], ACT.Exp, bias=mneg[:, t, h:h + 1]), exp2_r)
            load_rows(3, 3)
            turn(xT)
            act.wait_ge(route_d, 2)
            step(act.activation(small[:, 1, :], small[:, 1, :], ACT.Exp), route_a)
            def experts2():
                s = routed2.sem
                for e in range(0, EXPERTS, 2):
                    act.wait_ge(s["cplace_turned"], e + 1)
                    act.activation(cplaceT[:, e, :], bank[e % 4][:, 0:NODES], ACT.Copy).then_inc(s["cplaceT_act"], 1)

                def expert_out(c, i2):
                    act.wait_ge(down_g, i2 * JT2 + (UP2 + (c + 1) * JT2))
                    if c >= 2:
                        act.wait_ge(s["combined"], i2 + c - 1)
                    act.activation(tmp[:, c % 2, :], bank[3 + c % 2][:, :], ACT.Copy).then_inc(s["expert_out"], 1)

                def body(c, i2):
                    for j in range(JT2):
                        act.wait_ge(up_g, i2 * JT2 + (UP2 + c * JT2 + j + 1))
                        act.activation(act2[:, j % 2, 0:SE], bank[j % 2][:, 0:SE], ACT.Gelu,
                                       bias=b1e2[:, bass.ds(i2 + c, 1), j]).then_inc(hid_r, 1)
                        if j == 0 and c:
                            expert_out(c - 1, i2)

                for c in range(3):
                    body(c, 0)
                with act.Fori(0, 2) as i:
                    body(3, i * 2)
                    body(4, i * 2)
                body(7, 0)
                expert_out(7, 0)

            gather_nodes(routed2)
            experts2()
            act.wait_ge(routed2.sem["combined"], EXPERTS)
            for r in range(4):
                act.dma_start(brel[:, r, :], a["L3_gnn_b_rel"][r, :].partition_broadcast(P)).then_inc(brel_loaded, 16)
            turn(xT)
            for n in range(4 * NT):
                act.wait_ge(rel_r, n + 1)
                r, t = divmod(n, NT)
                act.dma_start(table3.rearrange("(t p r) d -> t r p d", t=NT, p=P)[t, r], stage[:, n, :]).then_inc(rel_w, 16)

            def scaled_high(n, at):
                act.wait_ge(scaled_r, at + n + 1)
                act.activation(mh[:, n % 4, :], msg4[:, n % 4, :], ACT.Copy).then_inc(msg_hi, 1)

            for n in range(8):
                scaled_high(n, 0)
            with act.Fori(0, 4) as i:
                for c in range(8, 16):
                    scaled_high(c, i * 8)
            for n in range(40, 48):
                scaled_high(n, 0)
            turn(yT)
            for m in range(8):
                act.wait_ge(node_g, 2 * NT + m + 1)
                step(act.activation(hidT[:, m, :], bank[m % 4][:, 0:NODES], ACT.Gelu, bias=bf1[:, m:m + 1]), gelu_r)
            turn(xT)
            act.wait_ge(sk_d, 1)
            step(act.activation(sink[:, 0, :], sink[:, 0, :], ACT.Ln), sk_a)
            with act.Fori(0, SINKHORN) as i:
                step.enter(i, {sk_a: 4})
                act.wait_ge(sk_d, i * 8 + 3)
                step(act.activation(sink[:, 1, :], sink[:, 0, :], ACT.Exp, bias=sinks[:, 0:1], accum_out=sinks[:, 1:2]), sk_a)
                step(act.activation(sinks[:, 2:3], sinks[:, 1:2], ACT.Ln), sk_a)
                act.wait_ge(sk_d, i * 8 + 6)
                step(act.activation(sinka[:, 2, :, :], sinka[:, 1, :, :], ACT.Exp), sk_a)
                act.wait_ge(sk_d, i * 8 + 7)
                step(act.activation(small1[:, 1, :], small1[:, 0, :], ACT.Ln), sk_a)
            step.leave(SINKHORN)
            act.wait_ge(sk_d, 1 + 8 * SINKHORN)
            step(act.activation(sink[:, 0, :], sink[:, 0, :], ACT.Exp), sk_a)

        @block.vector
        def _(dve):
            step = Steps(dve, dve_s)
            turns = [0]
            norms = [0]

            def norm(src, dst, signal=None, after=None):
                for t in range(NT):
                    step(dve.bn_stats(stats[:, :], src[:, t, :]))
                    step(dve.bn_aggr(mv[:, t, :], stats[:, :]))
                norms[0] += 1
                step(dve.tensor_scalar(varp[:, :], mv[:, :, 1], EPS, None, ALU.add), var_ready)
                dve.wait_ge(rstd_ready, norms[0])
                for t in range(NT):
                    step(dve.tensor_scalar(dst[:, t, :], src[:, t, :], mv[:, t, 0:1], rstd[:, t:t + 1], ALU.subtract, ALU.mult), signal)
                    if after is not None:
                        after(t)

            def turn(dst):
                for k in (1, 3):
                    dve.wait_ge(turned, KT * turns[0] + k + 1)
                    step(dve.tensor_copy(dst[:, k, :], bank[k][:, 0:NODES]), xT_v)
                turns[0] += 1

            def tables(first, n, tabs, cols, bias):
                def low(g):
                    which, r = divmod(g, n // 2)
                    t, c = divmod(r, cols)
                    dve.wait_ge(tab_hi, first + g + 1)
                    step(dve.tensor_tensor(tabs[:, which, 1, t, c * 512:c * 512 + 512], tmp[:, g % 2, :],
                                           tabs[:, which, 0, t, c * 512:c * 512 + 512], ALU.subtract), tab_lo)

                for g in range(n):
                    dve.wait_ge(table_g, first + g + 1)
                    which, r = divmod(g, n // 2)
                    if which == 0:
                        step(dve.tensor_tensor(tmp[:, g % 2, :], bank[g % 4][:, :], bias(r % cols), ALU.add), tab_sum)
                    else:
                        step(dve.tensor_copy(tmp[:, g % 2, :], bank[g % 4][:, :]), tab_sum)
                    if g:
                        low(g - 1)
                low(n - 1)

            def onehots(par, at_ix, which=(0, 1)):
                if 0 in which:
                    dve.wait_ge(ix_loaded, at_ix)
                for w in which:
                    for t in range(NT):
                        last = dve.tensor_scalar(onehot[:, par, w, t, :], eidx[:, w, :], nodeid[:, t:t + 1], None, ALU.is_equal)
                        if (w, t) == (1, NT - 1):
                            last.then_inc(oh_ready, 1)
                        
            dve.wait_ge(x_loaded, 16)
            norm(x, xn, nodes_ready)
            dve.wait_ge(edges_loaded, 64)
            step(dve.tensor_copy(srcf[:, :], srcc[:, :]))
            step(dve.tensor_copy(dstf[:, :], dstc[:, :]))
            step(dve.scalar_tensor_tensor(pair[:, :], srcf[:, :], float(NODES), dstf[:, :], ALU.mult, ALU.add), pairs_r)
            step(dve.scalar_tensor_tensor(rrow[:, :], srcc[:, :], 4.0, typc[:, :], ALU.mult, ALU.add))
            turn(xT)
            dve.wait_ge(rows_loaded, rows_before[0])

            def values(first, layer, name):
                for t in range(NT):
                    dve.wait_ge(value_g, first + t + 1)
                    step(dve.tensor_tensor(vn[:, t, :], bank[4 + t][:, :], row(layer, name), ALU.add), v_ready)

            values(0, 0, "L0_gnn_bv")
            tables(0, 12, tabs0, 2, lambda c: rows[:, 1 + c, :])
            dve.wait_ge(small_loaded, 16 * N_SMALL)

            def edge_onehots(b, at):
                for s in range(SUB):
                    for w, f in ((0, srcf), (1, dstf)):
                        last = dve.tensor_scalar(ebf[:, s, w, :], iota[:, :], f[:, bass.ds(at + s, 1)], None, ALU.is_equal)
                last.then_inc(em_ready, 1)

            def leaky(n, at):
                dve.wait_ge(relu_r, at + n + 1)
                dve.scalar_tensor_tensor(leaky4[:, n % 4, :], bank[n % 4][:, :], 0.01, relu4[:, n % 4, :], ALU.mult, ALU.add).then_inc(leaky_r, 1)

            def logits(b, par, at, at_e):
                dve.wait_ge(logit_g, at + b + 1)
                dve.tensor_scalar(logit[:, bass.ds(at_e, SUB), :], bank[4][:, 32 * par:32 * par + 32].rearrange("p (s h) -> p s h", s=SUB),
                                  ba[:, 0:1], None, ALU.add).then_inc(logit_r, 1)

            def block0(b, par, i2, i16):
                for h in range(HEADS):
                    leaky(b * 8 + h, i16)
                    if h == 0 and b < NB - 1:
                        onehots(1 - par, (i2 + (b + 2)) * 32)
                    if h == 1:
                        if b >= 1:
                            logits(b - 1, 1 - par, i2, (i2 + (b - 1)) * SUB)
                            dve.wait_ge(count_g, i2 + b)
                        edge_onehots(b, (i2 + b) * SUB)

            onehots(0, 32)
            block0(0, 0, 0, 0)
            with dve.Fori(0, 5) as i:
                for u in range(2):
                    block0(1 + u, 1 - u, i * 2, i * 16)
            block0(NB - 1, 1, 0, 0)
            logits(NB - 1, 1, 0, (NB - 1) * SUB)
            dve.wait_ge(count_g, NB)
            for t in range(NT):
                step(dve.tensor_copy(count[:, t, :], bank[5 + t][:, 0:NODES]))
            dve.wait_ge(big_loaded, 16 * NT)
            for t in range(NT):
                step(dve.tensor_reduce(mneg[:, t, :], big[:, t, :].rearrange("p (n h) -> p h n", h=HEADS), AX.X, ALU.max))
            step(dve.tensor_scalar(mneg[:, :, :], mneg[:, :, :], -1e30, -1.0, ALU.max, ALU.mult), max_r)

            def turned_weights(h):
                for d in range(NT):
                    dve.wait_ge(e_turned, turned_heads[0] * NT + d + 1)
                    step(dve.tensor_copy(eT[:, h % 2, d, :], bank[d][:, 0:NODES]), eT_ready)
                turned_heads[0] += 1

            turned_heads = [0]
            for h in range(HEADS):
                turned_weights(h)
            step(dve.tensor_scalar(den[:, :, :], den[:, :, :], 1e-30, None, ALU.max))
            step(dve.reciprocal(den[:, :, :], den[:, :, :]))
            dve.wait_ge(y_g, HEADS)

            def per_head(ap, t):
                return ap[:, t, :].unsqueeze(2).to_broadcast([P, HEADS, HD])

            def heads(ap):
                return ap.rearrange("p (h d) -> p h d", h=HEADS)

            for t in range(NT):
                step(dve.tensor_tensor(heads(y[:, t, :]), heads(bank[5 + t][:, :]), per_head(den, t), ALU.mult))
                step(dve.tensor_scalar(tmp[:, t % 2, :], y[:, t, :], 0.0, None, ALU.min), elu_in)
                dve.wait_ge(elu_ex, t + 1)
                step(dve.scalar_tensor_tensor(y[:, t, :], y[:, t, :], 0.0, tmp[:, t % 2, :], ALU.max, ALU.add))
                step(dve.scalar_tensor_tensor(y[:, t, :], y[:, t, :], -1.0, xn[:, t, :], ALU.add, ALU.add))

            def affine(src, layer, gain, shift, add, signal=None):
                def after(t):
                    step(dve.tensor_tensor(src[:, t, :], src[:, t, :], row(layer, gain), ALU.mult))
                    step(dve.tensor_tensor(src[:, t, :], src[:, t, :], row(layer, shift), ALU.add), signal)
                    if add:
                        step(dve.tensor_tensor(x[:, t, :], x[:, t, :], src[:, t, :], ALU.add))
                norm(src, src, None, after)

            affine(y, 0, "L0_gnn_gamma", "L0_gnn_beta", True)
            step(dve.tensor_copy(stats[:, 0:1], stats[:, 1:2]), row_used)

            def across(ap):
                return ap.unsqueeze(2).to_broadcast([P, NT, 8])

            def top2():
                v = small[:, 0, :]
                others = sm(0).unsqueeze(2).to_broadcast([P, NT, 8, 8])
                own = sm(0).unsqueeze(3).to_broadcast([P, NT, 8, 8])
                g = cmp8[:, 0, :, :].rearrange("p (t e) f -> p t e f", t=NT)
                q = cmp8[:, 1, :, :].rearrange("p (t e) f -> p t e f", t=NT)
                step(dve.tensor_tensor(g, others, own, ALU.is_gt))
                step(dve.tensor_tensor(q, others, own, ALU.is_equal))
                step(dve.tensor_tensor(q, q, low8[:, :, :].unsqueeze(1).to_broadcast([P, NT, 8, 8]), ALU.mult))
                step(dve.tensor_tensor(cmp8[:, 0, :, :], cmp8[:, 0, :, :], cmp8[:, 1, :, :], ALU.add))
                step(dve.tensor_reduce(small[:, 2, :], cmp8[:, 0, :, :], AX.X, ALU.add))
                step(dve.tensor_scalar(small[:, 2, :], small[:, 2, :], 2.0, None, ALU.is_lt))

            def logits_in(n, layer):
                dve.wait_ge(route_g, n)
                step(dve.tensor_tensor(sm(0), bank[7][:, 0:NT * 8].rearrange("p (t e) -> p t e", t=NT),
                                       br[:, layer, :].unsqueeze(1).to_broadcast([P, NT, 8]), ALU.add))
                step(dve.tensor_reduce(small1[:, 0, :], sm(0), AX.X, ALU.max))
                step(dve.tensor_tensor(sm(1), sm(0), across(small1[:, 0, :]), ALU.subtract), route_d)

            def normalized(dst, src, eps):
                step(dve.tensor_reduce(small1[:, 1, :], src, AX.X, ALU.add))
                if eps:
                    step(dve.tensor_scalar(small1[:, 1, :], small1[:, 1, :], eps, None, ALU.add))
                step(dve.reciprocal(small1[:, 1, :], small1[:, 1, :]))
                step(dve.tensor_tensor(dst, src, across(small1[:, 1, :]), ALU.mult))

            def places(n, mask):
                step(dve.scalar_tensor_tensor(sm(5), sm(4), 1.0, mask, ALU.add, ALU.mult))
                step(dve.tensor_scalar(sm(5), sm(5), -1.0, None, ALU.add))
                step(dve.tensor_copy(stats[:, 0:1], stats[:, 1:2]), coef_r)
                dve.wait_ge(coefT_g, n)
                step(dve.tensor_copy(coefT[:, :], bank[7][0:8, 0:NODES]), coefT_r)

            def gather_nodes(r):
                s, w = r.sem, r.width
                for g in range(r.groups):
                    for e in range(g * 512 // w, (g + 1) * 512 // w):
                        for t in range(NT):
                            last = dve.tensor_scalar(r.place[:, t, e * w:(e + 1) * w], iota[:, 0:w], small[:, 5, t * 8 + e:t * 8 + e + 1], None, ALU.is_equal)
                    last.then_inc(s["place_ready"], 1)
                    if g == 0:
                        for t in range(NT):
                            dve.wait_ge(s["split_high"], t + 1)
                            dve.tensor_tensor(xsplit[:, 1, t, :], xn[:, t, :], xsplit[:, 0, t, :], ALU.subtract).then_inc(s["split_low"], 1)

            def take_gathered(r, g):
                s = r.sem
                for k in (1, 3):
                    dve.wait_ge(s["gather_product"], 4 * g + k + 1)
                    dve.tensor_copy(r.xgT[k][:, g * 512:g * 512 + 512], bank[4 * (g % 2) + k][:, :]).then_inc(s["gathered_dve"], 1)

            def experts2():
                s = routed2.sem
                for e in range(EXPERTS):
                    for t in range(NT):
                        last = dve.tensor_scalar(cplace[:, t, e * SE:(e + 1) * SE], iota[:, 0:SE], small[:, 5, t * 8 + e:t * 8 + e + 1],
                                                 coef[:, t, e:e + 1], ALU.is_equal, ALU.mult)
                    last.then_inc(s["cplace_ready"], 1)
                for g in range(routed2.groups):
                    take_gathered(routed2, g)
                for e in range(1, EXPERTS, 2):
                    dve.wait_ge(s["cplace_turned"], e + 1)
                    dve.tensor_copy(cplaceT[:, e, :], bank[e % 4][:, 0:NODES]).then_inc(s["cplaceT_dve"], 1)
                dve.wait_ge(s["cplaceT_act"], 4)
                dve.wait_ge(s["cplaceT_dve"], 4)
                for e in range(EXPERTS):
                    if e >= 2:
                        dve.wait_ge(s["combined"], e - 1)
                    dve.tensor_copy(cp2[:, e % 2, :], cplaceT[:, e, :]).then_inc(s["cplace_copied"], 1)
                dve.wait_ge(s["combined"], EXPERTS)
                for t in range(NT):
                    step(dve.tensor_tensor(x[:, t, :], x[:, t, :], bank[5 + t][:, :], ALU.add))

            norm(x, xn, nodes_ready)
            turn(xT)
            logits_in(1, 0)
            top2()
            step(dve.tensor_copy(stats[:, 0:1], stats[:, 1:2]), mask_r)
            dve.wait_ge(route_a, 1)
            step(dve.tensor_tensor(sm(1), sm(1), sm(2), ALU.mult))
            normalized(coef[:, :, :], sm(1), 0.0)
            dve.wait_ge(pos_g, 1)
            step(dve.tensor_copy(small[:, 4, :], bank[7][:, 32:32 + NT * 8]))
            step(dve.tensor_copy(crowd[:, :], bank[7][:, 64:72]))
            places(1, sm(2))

            def add_expert(e, banks, at_down, at_added):
                dve.wait_ge(down_g, at_down)
                for t in range(NT):
                    dve.scalar_tensor_tensor(x[:, t, :], bank[banks + t][:, :], coef[:, t, bass.ds(e, 1)], x[:, t, :],
                                             ALU.mult, ALU.add).then_inc(added, 1)
                dve.wait_ge(added, at_added)

            for t in range(NT):
                dve.wait_ge(b2_g, t + 1)
                dve.tensor_tensor(x[:, t, :], x[:, t, :], bank[4 + t][:, :], ALU.add).then_inc(expert_added, 1)
            gather_nodes(routed0)
            for g in range(routed0.groups):
                take_gathered(routed0, g)
            with dve.Fori(0, EXPERTS) as e:
                def expert0(width):
                    s = routed0.sem
                    w = min(width, 2 * SE)
                    dve.wait_ge(expert_added, e * NT + NT)
                    for t in range(NT):
                        last = dve.tensor_scalar(cpl[:, t, 0:w], iota[:, 0:w], sm(5)[:, t, bass.ds(e, 1)], coef[:, t, bass.ds(e, 1)],
                                                 ALU.is_equal, ALU.mult)
                    last.then_inc(s["cplace_ready"], 1)
                    dve.wait_ge(s["cplace_turned"], e + 1)
                    if width == 2 * SE:
                        dve.tensor_copy(cp2[:, 1, :], bank[3][:, 0:NODES])
                    dve.tensor_copy(cp2[:, 0, :], bank[7][:, 0:NODES]).then_inc(s["cplace_copied"], 1)
                    for j in range(JT0):
                        dve.wait_ge(silu_r, e * JT0 + j + 1)
                        up = bank[2 + j % 2][:, 0:NODES] if width == NODES else bank[j % 2][:, width:2 * width]
                        dve.scalar_tensor_tensor(act2[:, j % 2, 0:width], up, b1e0[:, bass.ds(e, 1), JT0 + j],
                                                 silu2[:, j % 2, 0:width], ALU.add, ALU.mult).then_inc(hid_r, 1)
                    dve.wait_ge(s["combined"], e + 1)
                    for t in range(NT):
                        if width == NODES:
                            ins = dve.scalar_tensor_tensor(x[:, t, :], bank[4 + t][:, :], coef[:, t, bass.ds(e, 1)], x[:, t, :], ALU.mult, ALU.add)
                        else:
                            ins = dve.tensor_tensor(x[:, t, :], x[:, t, :], bank[4 + t][:, :], ALU.add)
                        ins.then_inc(expert_added, 1)

                chosen_by = dve.value_load(crowd[0:1, bass.ds(e, 1)], min_val=0, max_val=NODES)
                with dve.If(chosen_by <= SE):
                    expert0(SE)
                with dve.Else():
                    with dve.If(chosen_by <= 2 * SE):
                        expert0(2 * SE)
                    with dve.Else():
                        expert0(NODES)
            dve.wait_ge(expert_added, NT + EXPERTS * NT)
            step(dve.tensor_copy(stats[:, 0:1], stats[:, 1:2]), added)

            norm(x, xn, nodes_ready)
            turn(xT)
            dve.wait_ge(rows_loaded, rows_before[1])
            tables(12, 6, tabs1, 1, lambda c: row(1, "L1_gnn_b1"))

            def message_onehots(at):
                for s in range(SUB):
                    last = dve.tensor_scalar(em[:, s, :], iota[:, :], dstf[:, bass.ds(at + s, 1)], None, ALU.is_equal)
                last.then_inc(em_ready, 1)

            def mish_out(n, at):
                kind, b, s = mish_tile(n) if n < MISH else ("u", 0, n - MISH)
                width = 512 if n < MISH else NODES
                dst = {"z": hT[:, b % 2, s, :], "m": mz[:, n % 4, :], "u": hidT[:, s, :]}[kind]
                dve.wait_ge(mish_q, at + n + 1)
                dve.tensor_tensor(dst, mz[:, n % 4, 0:width], mr[:, n % 4, 0:width], ALU.mult).then_inc(mish_r, 1)

            def mish_square(n, at, width=512):
                dve.wait_ge(mish_ex, at + n + 1)
                dve.tensor_scalar(mt[:, n % 4, 0:width], mt[:, n % 4, 0:width], 1e9, None, ALU.min).then_inc(mish_min, 1)
                dve.wait_ge(mish_min, at + n + 1)
                dve.scalar_tensor_tensor(mt[:, n % 4, 0:width], mt[:, n % 4, 0:width], 2.0, mt[:, n % 4, 0:width], ALU.add, ALU.mult).then_inc(mish_sq, 1)

            def message_low(n, at, at4):
                kind, b, s = mish_tile(n)
                if kind == "m":
                    dve.wait_ge(msg_hi, at4 + (4 * b + s + 1))
                    dve.tensor_tensor(ml[:, s, :], mz[:, n % 4, :], mh[:, s, :], ALU.subtract).then_inc(msg_lo, 1)

            def mish_input(n, at, at4=0):
                kind, b, s = mish_tile(n) if n < MISH else ("u", 0, n - MISH)
                dve.wait_ge(mish_g, at + n + 1)
                if n >= 4:
                    dve.wait_ge(mish_r, at + n - 3)
                    kind_, b_, s_ = mish_tile(n - 4) if n < MISH else ("u", 0, 0)
                    if kind_ == "m":
                        dve.wait_ge(msg_lo, at4 + (4 * b_ + s_ + 1))
                if kind == "z":
                    ins = dve.tensor_copy(mz[:, n % 4, :], bank[n % 4][:, :])
                elif kind == "m":
                    ins = dve.tensor_tensor(mz[:, n % 4, :], bank[n % 4][:, :], row(1, "L1_gnn_b2"), ALU.add)
                else:
                    ins = dve.tensor_scalar(mz[:, n % 4, 0:NODES], bank[n % 4][:, 0:NODES], b3c[:, s:s + 1], None, ALU.add)
                ins.then_inc(mish_in, 1)

            def mish_step(n, at, at4, first=0):
                if first <= n - 1 < MISH:
                    mish_square(n - 1, at)
                if n - 4 >= first:
                    message_low(n - 4, at, at4)
                if n < MISH:
                    mish_input(n, at, at4)
                if first <= n - 3 < MISH:
                    mish_out(n - 3, at)

            def mish_drain():
                mish_square(MISH - 5, 0)
                message_low(MISH - 8, 0, 0)
                for n in (MISH - 7, MISH - 6, MISH - 5):
                    mish_out(n, 0)
                    message_low(n, 0, 0)

            def block1(b, i2, at):
                if b == NB - 1:
                    mish_drain()
                for q in range(8 if b < NB - 1 else 4):
                    mish_step(4 + 8 * b + q, at, i2 * 4, MISH - 4 if b == NB - 1 else 0)
                    if q in (4, 5) and b < NB - 2:
                        onehots(b % 2, (i2 + (NB + b + 3)) * 32, (q - 4,))
                    if q == (3 if b < NB - 1 else 0):
                        message_onehots((i2 + b) * SUB)

            onehots(0, (NB + 1) * 32)
            onehots(1, (NB + 2) * 32)
            for n in range(4):
                mish_step(n, 0, 0)
            block1(0, 0, 0)
            with dve.Fori(0, 4) as i:
                for u in range(2):
                    block1(1 + u, i * 2, i * 16)
            for b in (NB - 3, NB - 2, NB - 1):
                block1(b, 0, 0)
            for n in range(MISH, MISH + 4):
                mish_step(n, 0, 0, MISH - 4)
            for t in range(NT):
                dve.wait_ge(agg_g, NT)
                step(dve.tensor_copy(y[:, t, :], bank[4 + t][:, :]), nodes_ready)
            turn(yT)
            for m in range(KT):
                mish_input(MISH + m, 0)
                mish_square(MISH + m, 0, NODES)
                mish_out(MISH + m, 0)
            for t in range(NT):
                dve.wait_ge(node_g, t + 1)
                step(dve.tensor_tensor(y[:, t, :], bank[4 + t][:, :], row(1, "L1_gnn_b4"), ALU.add))
                step(dve.tensor_tensor(y[:, t, :], y[:, t, :], xn[:, t, :], ALU.add))
            affine(y, 1, "L1_gnn_gamma", "L1_gnn_beta", True)
            step(dve.tensor_copy(stats[:, 0:1], stats[:, 1:2]), row_used)

            norm(x, xn, nodes_ready)

            turn(xT)

            def quant(j, u, i):
                raw = qraw[:, u, :, :].rearrange("p c (g n) -> p (c g) n", g=4)
                va = qa.rearrange("p (g n) -> p g n", g=12)
                vb = qb.rearrange("p (g n) -> p g n", g=12)
                base = (i * 2 + j) * 4 if i is not None else j * 4

                def link(ins, k):
                    ins.then_inc(quant_s, 1)
                    dve.wait_ge(quant_s, base + k)

                if i is None:
                    dve.wait_ge(q_loaded[u], 48 * (j // 2 + 1))
                else:
                    dve.wait_ge(q_loaded[u], i * 48 + 48 * (j // 2 + 1))
                link(dve.tensor_reduce(qs[:, :, 0], raw, AX.X, ALU.add, apply_absolute_value=True), 1)
                link(dve.tensor_scalar(qs[:, :, 0], qs[:, :, 0], 1.0 / 128, EPS, ALU.mult, ALU.add), 2)
                dve.tensor_scalar(qs[:, :, 1], qs[:, :, 0], 0.5, None, ALU.mult)
                link(dve.tensor_scalar(qs[:, :, 2], qs[:, :, 0], -0.5, None, ALU.mult), 3)
                for g in range(12):
                    dve.tensor_scalar(va[:, g, :], raw[:, g, :], qs[:, g, 1:2], qs[:, g, 0:1], ALU.is_gt, ALU.mult)
                    last = dve.tensor_scalar(vb[:, g, :], raw[:, g, :], qs[:, g, 2:3], qs[:, g, 0:1], ALU.is_lt, ALU.mult)
                link(last, 4)
                dve.tensor_tensor(qa, qa, qb, ALU.subtract).then_inc(quant_r, 1)

            def turn_quant(j, u, at):
                dve.wait_ge(q_turned, at * 3 + 3 * j + 3)
                dve.tensor_copy(qT[:, u, 2, :], bank[2][:, :]).then_inc(qT_v, 1)

            def hidden1(j, u, at):
                dve.wait_ge(silu_r, at + UP1 + j + 1)
                dve.tensor_tensor(act2[:, u, :], bank[4][:, 0:NODES], silu2[:, u, :], ALU.mult).then_inc(hid_r, 1)

            quant(0, 0, None)
            turn_quant(0, 0, 0)
            quant(1, 1, None)
            hidden1(0, 0, 0)
            turn_quant(1, 1, 0)
            quant(2, 0, None)
            with dve.Fori(0, 4) as i:
                for j in (1, 2):
                    hidden1(j, j % 2, i * 2)
                    turn_quant(j + 1, (j + 1) % 2, i * 2)
                    quant(j + 2, j % 2, i)
            hidden1(9, 1, 0)
            turn_quant(10, 0, 0)
            hidden1(10, 0, 0)
            dve.wait_ge(down_g, UP2)
            for t in range(NT):
                step(dve.tensor_tensor(x[:, t, :], x[:, t, :], bank[5 + t][:, :], ALU.add), added)

            norm(x, xn, nodes_ready)
            turn(xT)
            dve.wait_ge(rows_loaded, rows_before[2])
            values(NT, 2, "L2_gnn_Wb")
            for k, name in enumerate(("L2_gnn_at", "L2_gnn_as")):
                for t in range(NT):
                    step(dve.tensor_tensor(prod, vn[:, t, :], row(2, name), ALU.mult))
                    step(dve.tensor_reduce(pq[:, k, t, :], heads(prod), AX.X, ALU.add))
            step(dve.tensor_tensor(pq[:, 1, :, :], pq[:, 1, :, :], ab[:, :].unsqueeze(1).to_broadcast([P, NT, HEADS]), ALU.add), pq_r)
            step(dve.tensor_copy(stats[:, 0:1], stats[:, 1:2]), row_used)
            for t in range(NT):
                step(dve.tensor_scalar(negm[:, t, :], count[:, t, :], 0.0, -1e30, ALU.is_equal, ALU.mult))
            dve.wait_ge(pqT_g, 1)
            step(dve.tensor_copy(qT2, bank[3][0:8, 0:NODES]), pqT_r)

            def score(h, t):
                dve.wait_ge(srow_g, h + 1)
                step(dve.scalar_tensor_tensor(srow[:, t, :], bank[3 + h % 2][:, 0:NODES], pq[:, 0, t, h:h + 1], negm[:, t, :], ALU.add, ALU.add))
                step(dve.scalar_tensor_tensor(srow[:, t, :], srow[:, t, :], 0.2, srow[:, t, :], ALU.mult, ALU.max))
                step(dve.tensor_reduce(small1[:, 0, 0:1], srow[:, t, :], AX.X, ALU.max))
                step(dve.tensor_scalar(mneg[:, t, h:h + 1], small1[:, 0, 0:1], -1.0, None, ALU.mult), score_r)

            def weigh(h, t):
                dve.wait_ge(exp2_r, h * NT + t + 1)
                if h >= 2:
                    dve.wait_ge(e_turned, NT * (HEADS + h - 1))
                step(dve.tensor_tensor_reduce(eh[:, h % 2, t, :], srow[:, t, :], count[:, t, :], 1.0, 0.0,
                                              ALU.mult, ALU.add, den[:, t, h:h + 1]), weighed)

            for h in range(HEADS):
                for t in range(NT):
                    score(h, t)
                    if t:
                        weigh(h, t - 1)
                weigh(h, NT - 1)
                if h:
                    turned_weights(h - 1)
            turned_weights(HEADS - 1)
            step(dve.tensor_scalar(den[:, :, :], den[:, :, :], 1e-30, None, ALU.max))
            step(dve.reciprocal(den[:, :, :], den[:, :, :]))
            dve.wait_ge(y_g, 2 * HEADS)
            for t in range(NT):
                step(dve.tensor_tensor(heads(y[:, t, :]), heads(bank[5 + t][:, :]), per_head(den, t), ALU.mult))
                step(dve.tensor_tensor(x[:, t, :], x[:, t, :], y[:, t, :], ALU.add))

            norm(x, xn, nodes_ready)
            turn(xT)
            logits_in(2, 1)
            top2()
            step(dve.tensor_copy(stats[:, 0:1], stats[:, 1:2]), mask_r)
            dve.wait_ge(route_a, 2)
            normalized(sm(1), sm(1), 0.0)
            step(dve.tensor_tensor(sm(3), sm(1), sm(2), ALU.mult))
            normalized(sm(3), sm(3), 1e-9)
            dve.wait_ge(pos_g, 2)
            step(dve.tensor_copy(small[:, 4, :], bank[7][:, 32:32 + NT * 8]))
            step(dve.scalar_tensor_tensor(small[:, 6, :], small[:, 4, :], float(CAP), small[:, 2, :], ALU.is_lt, ALU.mult))
            step(dve.tensor_tensor(sm(3), sm(3), sm(6), ALU.mult))
            normalized(coef[:, :, :], sm(3), 1e-9)
            places(2, sm(6))
            gather_nodes(routed2)
            experts2()
            step(dve.tensor_copy(stats[:, 0:1], stats[:, 1:2]), added)

            norm(x, xn, nodes_ready)
            turn(xT)
            step(dve.tensor_copy(wdeg[:, :, 0], ewc[:, :]))
            step(dve.tensor_tensor(wdeg[:, :, 1], ewc[:, :], wdeg[:, :, 0], ALU.subtract), wdeg_r)
            dve.wait_ge(brel_loaded, 64)
            dve.wait_ge(rows_loaded, rows_before[3])
            for n in range(4 * NT):
                dve.wait_ge(rel_g, n + 1)
                step(dve.tensor_tensor(stage[:, n, :], bank[n % 4][:, :], brel[:, n // NT, :], ALU.add), rel_r)
            for t in range(NT):
                dve.wait_ge(node_g, NT + t + 1)
                step(dve.tensor_tensor(y[:, t, :], bank[4 + t][:, :], row(3, "L3_gnn_b_self"), ALU.add))
                step(dve.tensor_tensor(y[:, t, :], y[:, t, :], xn[:, t, :], ALU.add))

            def scaled_low(n, at):
                dve.wait_ge(msg_hi, at + (4 * NB + n + 1))
                dve.tensor_tensor(ml[:, n % 4, :], msg4[:, n % 4, :], mh[:, n % 4, :], ALU.subtract).then_inc(msg_lo, 1)

            def scaled(n, at, turn_value):
                if n >= 4:
                    dve.wait_ge(m_used, at + n - 3)
                dve.wait_ge(gathered[n % RING], turn_value)
                dve.tensor_scalar(msg4[:, n % 4, :], gather[:, n % RING, :], ewc[:, bass.ds(at + n, 1)], None, ALU.mult).then_inc(scaled_r, 1)
                dve.tensor_scalar(em[:, n % 4, :], iota[:, :], dstf[:, bass.ds(at + n, 1)], None, ALU.is_equal).then_inc(em_ready, 1)

            for n in range(RING):
                scaled(n, 0, 16)
                if n:
                    scaled_low(n - 1, 0)
            with dve.Fori(0, 4) as i:
                for c in range(RING, 2 * RING):
                    scaled(c, i * RING, i * 16 + 32)
                    scaled_low(c - 1, i * RING)
            for n in range(5 * RING, 6 * RING):
                scaled(n, 0, 96)
                scaled_low(n - 1, 0)
            scaled_low(ET - 1, 0)
            dve.wait_ge(agg_g, 2 * NT + 1)
            step(dve.tensor_reduce(small1[:, 0, :], bank[3][:, 0:2 * NT].rearrange("p (t c) -> p t c", c=2), AX.X, ALU.add))
            step(dve.tensor_scalar(small1[:, 0, :], small1[:, 0, :], 1.0, None, ALU.max))
            step(dve.reciprocal(small1[:, 0, :], small1[:, 0, :]))
            for t in range(NT):
                step(dve.scalar_tensor_tensor(y[:, t, :], bank[t][:, :], small1[:, 0, t:t + 1], y[:, t, :], ALU.mult, ALU.add))
            affine(y, 3, "L3_gnn_ln1_g", "L3_gnn_ln1_b", False, nodes_ready)
            turn(yT)
            for t in range(NT):
                dve.wait_ge(node_g, 2 * NT + 8 + t + 1)
                step(dve.tensor_tensor(y[:, t, :], y[:, t, :], bank[4 + t][:, :], ALU.add))
                step(dve.tensor_tensor(y[:, t, :], y[:, t, :], row(3, "L3_gnn_b_ffn2"), ALU.add))
            affine(y, 3, "L3_gnn_ln2_g", "L3_gnn_ln2_b", True)

            norm(x, xn, nodes_ready)
            turn(xT)
            dve.wait_ge(route_g, 3)
            step(dve.tensor_scalar(sink[:, 0, :], bank[7][0:8, 0:NODES], 1e-10, None, ALU.max), sk_d)
            with dve.Fori(0, SINKHORN) as i:
                step.enter(i, {sk_d: 8})
                dve.wait_ge(sk_a, i * 4 + 1)
                step(dve.tensor_reduce(sinks[:, 3:4], sink[:, 0, :], AX.X, ALU.max), sk_d)
                step(dve.tensor_scalar(sinks[:, 0:1], sinks[:, 3:4], -1.0, None, ALU.mult), sk_d)
                dve.wait_ge(sk_a, i * 4 + 3)
                step(dve.tensor_scalar(sink[:, 0, :], sink[:, 0, :], sinks[:, 3:4], sinks[:, 2:3], ALU.subtract, ALU.subtract), sk_d)
                dve.wait_ge(sk_p, i * 2 + 1)
                turned_gates = bank[0][:, 0:NT * 8].rearrange("p (t e) -> p t e", t=NT)
                step(dve.tensor_reduce(small1[:, 2, :], turned_gates, AX.X, ALU.max), sk_d)
                step(dve.tensor_tensor(sinka[:, 1, :, :], turned_gates, across(small1[:, 2, :]), ALU.subtract), sk_d)
                dve.wait_ge(sk_a, i * 4 + 4)
                step(dve.tensor_reduce(small1[:, 0, :], sinka[:, 2, :, :], AX.X, ALU.add), sk_d)
                dve.wait_ge(sk_a, i * 4 + 5)
                step(dve.tensor_tensor(sinka[:, 0, :, :], sinka[:, 1, :, :], across(small1[:, 1, :]), ALU.subtract), sk_d)
                dve.wait_ge(sk_p, i * 2 + 2)
                step(dve.tensor_copy(sink[:, 0, :], bank[1][0:8, 0:NODES]), sk_d)
            step.leave(SINKHORN)
            dve.wait_ge(sk_a, 4 * SINKHORN + 2)
            for k in range(TOP // 8):
                src = sink[:, 0 if k == 0 else 1 + (k - 1) % 2, :]
                step(dve.max(sinks[:, 0:8], src))
                step(dve.match_replace(sink[:, 1 + k % 2, :], sinks[:, 0:8], src, -1.0))
            step(dve.tensor_scalar(sink[:, 3, :], sink[:, 1 + (TOP // 8 - 1) % 2, :], -1.0, None, ALU.is_equal))
            step(dve.scalar_tensor_tensor(sink[:, 4, :], sink[:, 0, :], 0.5, sink[:, 3, :], ALU.is_gt, ALU.mult), chosen_r)
            dve.wait_ge(sk_p, 2 * SINKHORN + 1)
            chosen = bank[7][:, 0:2 * NT * 8].rearrange("p (c t e) -> p c t e", c=2, t=NT)
            step(dve.tensor_reduce(small1[:, 0, :], chosen[:, 0, :, :], AX.X, ALU.add))
            step(dve.tensor_scalar(small1[:, 0, :], small1[:, 0, :], 1.0, None, ALU.add))
            step(dve.reciprocal(small1[:, 0, :], small1[:, 0, :]))
            step(dve.tensor_tensor(coef[:, :, :], chosen[:, 1, :, :], across(small1[:, 0, :]), ALU.mult))
            with dve.Fori(0, EXPERTS // 2) as i:
                for v in range(2):
                    add_expert(i * 2 + v, 3 * v, i * 2 + (UP3 + v + 1), i * (2 * NT) + (ADD3 + NT * (v + 1)))

        @block.tensor
        def _(pe):
            turns = [0]

            def turn(src):
                pe.wait_ge(nodes_ready, NT * (turns[0] + 1))
                for k in range(KT):
                    for t in range(NT):
                        last = pe.transpose(bank[k][:, t * P:(t + 1) * P], src[:, t, k * P:(k + 1) * P], ident[:, :])
                    last.then_inc(turned, 1)
                turns[0] += 1
                pe.wait_ge(xT_a, 2 * turns[0])
                pe.wait_ge(xT_v, 2 * turns[0])

            def arrived(*key):
                s, value = W[key]
                pe.wait_ge(arrive[s], value)

            def weight(name, k):
                return wslot(W[(*name, k // 2)][0], 2)[:, k % 2, :]

            def product(out, lhs, rhs, n, signal):
                for k in range(n):
                    last = pe.matmul(out, lhs(k), rhs(k), start=(k == 0), stop=(k == n - 1))
                last.then_inc(signal, 1)

            def tile(ap, k, t):
                return ap[:, k, t * P:(t + 1) * P]

            def values(name, signal):
                arrived(*name, 0)
                arrived(*name, 1)
                for t in range(NT):
                    product(bank[4 + t][:, :], lambda k: tile(xT, k, t), lambda k: weight(name, k), KT, signal)

            def router(which):
                for t in range(NT):
                    for k in range(KT):
                        last = pe.matmul(bank[7][:, t * 8:t * 8 + 8], tile(xT, k, t), gatew[:, which, k, :],
                                         start=(k == 0), stop=(k == KT - 1))
                last.then_inc(route_g, 1)

            def positions(n):
                pe.wait_ge(mask_r, n)
                for t in range(NT):
                    for k in range(t + 1):
                        pe.matmul(bank[7][:, 32 + t * 8:40 + t * 8], (upper if k == t else ones)[:, :], sm(2)[:, k, :],
                                  start=(k == 0), stop=(k == t))
                for k in range(NT):
                    last = pe.matmul(bank[7][:, 64:72], ones[:, :], sm(2)[:, k, :], start=(k == 0), stop=(k == NT - 1))
                last.then_inc(pos_g, 1)

            def turn_coef(n):
                pe.wait_ge(coef_r, n)
                for t in range(NT):
                    last = pe.transpose(bank[7][0:8, t * P:(t + 1) * P], coef[:, t, :], ident[:, :])
                last.then_inc(coefT_g, 1)
                pe.wait_ge(coefT_r, n)

            def gather_nodes(r):
                s = r.sem
                pe.wait_ge(s["split_high"], NT)
                pe.wait_ge(s["split_low"], NT)
                for g in range(r.groups):
                    pe.wait_ge(s["place_ready"], g + 1)
                    if g >= 2:
                        pe.wait_ge(s["gathered_act"], 2 * (g - 1))
                        pe.wait_ge(s["gathered_dve"], 2 * (g - 1))
                    for k in range(KT):
                        for t in range(NT):
                            for p in range(2):
                                last = pe.matmul(bank[4 * (g % 2) + k][:, :], xsplit[:, p, t, k * P:(k + 1) * P], r.place[:, t, g * 512:g * 512 + 512],
                                                 start=(t, p) == (0, 0), stop=(t, p) == (NT - 1, 1))
                        last.then_inc(s["gather_product"], 1)

            def experts2():
                s = routed2.sem
                pe.wait_ge(s["gathered_act"], 2)
                pe.wait_ge(s["gathered_dve"], 2)
                for e in range(EXPERTS):
                    pe.wait_ge(s["cplace_ready"], e + 1)
                    if e >= 4:
                        pe.wait_ge(s["cplaceT_dve" if e % 2 else "cplaceT_act"], e // 2 - 1)
                    for t in range(NT):
                        last = pe.transpose(bank[e % 4][:, t * P:(t + 1) * P], cplace[:, t, e * SE:(e + 1) * SE], ident[:, :])
                    last.then_inc(s["cplace_turned"], 1)
                pe.wait_ge(s["gathered_act"], 4)
                pe.wait_ge(s["gathered_dve"], 4)
                for t in range(NT):
                    pe.matmul(bank[5 + t][:, :], coefT[:, t * P:(t + 1) * P], b2e[:, 1, :], start=True, stop=False, skip_group_check=True)
                pe.wait_ge(s["cplaceT_act"], 4)
                pe.wait_ge(s["cplaceT_dve"], 4)

                def loaded(c, i2, part):
                    slot = f2[2 * (c % 2) + part]
                    pe.wait_ge(arrive[slot], i2 * 8 + (16 * (c // 2 + 1) + f2_base[slot]))

                def up(c, i2, j):
                    if j == 0:
                        loaded(c, i2, 0)
                    for k in range(KT):
                        last = pe.matmul(bank[j % 2][:, 0:SE], wslot(f2[2 * (c % 2)], KT)[:, k, j * P:(j + 1) * P],
                                         routed2.xgT[k][:, bass.ds((i2 + c) * SE, SE)], start=(k == 0), stop=(k == KT - 1))
                    last.then_inc(up_g, 1)

                def down(c, i2, j):
                    if j == 0:
                        loaded(c, i2, 1)
                    pe.wait_ge(hid_r, i2 * JT2 + (UP2 + c * JT2 + j + 1))
                    pe.matmul(bank[3 + c % 2][:, :], act2[:, j % 2, 0:SE], wslot(f2[2 * (c % 2) + 1], 2)[:, j, :], start=(j == 0), stop=(j == JT2 - 1),
                              skip_group_check=True).then_inc(down_g, 1)

                def combine(c, i2):
                    pe.wait_ge(s["cplace_copied"], i2 + c + 1)
                    pe.wait_ge(s["expert_out"], i2 + c + 1)
                    for t in range(NT):
                        last = pe.matmul(bank[5 + t][:, :], cp2[:, c % 2, t * P:(t + 1) * P], tmp[:, c % 2, :],
                                         start=False, stop=(c == EXPERTS - 1), skip_group_check=True)
                    last.then_inc(s["combined"], 1)

                def body(c, i2):
                    for j in range(JT2):
                        up(c, i2, j)
                        if j:
                            down(c, i2, j - 1)
                        if j == 1 and c:
                            combine(c - 1, i2)
                    down(c, i2, JT2 - 1)

                for c in range(3):
                    body(c, 0)
                with pe.Fori(0, 2) as i:
                    body(3, i * 2)
                    body(4, i * 2)
                body(7, 0)
                combine(7, 0)

            pe.wait_ge(consts_ready, 1)
            turn(xn)
            values(("wv",), value_g)
            for g in range(12):
                which, r = divmod(g, 6)
                t, c = divmod(r, 2)
                if r == 0:
                    for k in range(4):
                        arrived("ww", 4 * which + k)
                if g >= 4:
                    pe.wait_ge(tab_sum, g - 3)
                product(bank[g % 4][:, :], lambda k: tile(xT, k, t),
                        lambda k: wring[:, W["ww", 4 * which + k][0], c * 512:c * 512 + 512], KT, table_g)
            pe.wait_ge(tab_lo, 12)
            pe.wait_ge(tab_hi, 12)
            pe.wait_ge(small_loaded, 16 * N_SMALL)
            pe.wait_ge(v_ready, NT)

            def z0(n, par, at):
                h = n % 8
                for w in range(2):
                    for t in range(NT):
                        for p in range(2):
                            last = pe.matmul(bank[n % 4][:, :], tabs0[:, w, p, t, h * P:(h + 1) * P], onehot[:, par, w, t, :],
                                             start=(w, t, p) == (0, 0, 0), stop=(w, t, p) == (1, NT - 1, 1))
                last.then_inc(z_g, 1)

            def logit_parts(n, par, at):
                h = n % 8
                pe.wait_ge(leaky_r, at + n + 1)
                for s in range(SUB):
                    last = pe.matmul(bank[4][:, 32 * par + s * 8 + h:32 * par + s * 8 + h + 1],
                                     leaky4[:, n % 4, s * P:(s + 1) * P], wa[:, :], start=True, stop=True)
                if h == 7:
                    last.then_inc(logit_g, 1)

            def count0(b, at):
                pe.wait_ge(em_ready, at + b + 1)
                for s in range(SUB):
                    for t in range(NT):
                        last = pe.matmul(bank[5 + t][:, 0:NODES], ebf[:, s, 1, t * P:(t + 1) * P], ebf[:, s, 0, :],
                                         start=(b, s) == (0, 0), stop=(b, s) == (NB - 1, SUB - 1), skip_group_check=True)
                last.then_inc(count_g, 1)

            def block0(b, par, i2, i16):
                pe.wait_ge(oh_ready, i2 + b + 1)
                for h in range(HEADS):
                    n = b * 8 + h
                    z0(n, par, i16)
                    if n >= 2:
                        if h == 2 and b:
                            pe.wait_ge(logit_r, i2 + b)
                        logit_parts(n - 2, par if h >= 2 else 1 - par, i16)
                    if h == 4:
                        count0(b, i2)

            block0(0, 0, 0, 0)
            with pe.Fori(0, 5) as i:
                for u in range(2):
                    block0(1 + u, 1 - u, i * 2, i * 16)
            block0(NB - 1, 1, 0, 0)
            logit_parts(NB * 8 - 2, 1, 0)
            logit_parts(NB * 8 - 1, 1, 0)

            def attend(first, ready, ready_first):
                def turn_head(h):
                    pe.wait_ge(ready, ready_first + NT * (h + 1))
                    if h:
                        pe.wait_ge(eT_ready, (first + h) * NT)
                    for d in range(NT):
                        for t in range(NT):
                            last = pe.transpose(bank[d][:, t * P:(t + 1) * P], eh[:, h % 2, t, d * P:(d + 1) * P], ident[:, :])
                        last.then_inc(e_turned, 1)

                def weighted(h):
                    pe.wait_ge(eT_ready, (first + h + 1) * NT)
                    for t in range(NT):
                        for d in range(NT):
                            last = pe.matmul(bank[5 + t][:, h * HD:(h + 1) * HD], eT[:, h % 2, d, t * P:(t + 1) * P],
                                             vn[:, d, h * HD:(h + 1) * HD], start=(d == 0), stop=(d == NT - 1))
                    last.then_inc(y_g, 1)
                return turn_head, weighted

            turn_head, weighted = attend(0, e_ready, 0)
            for h in range(HEADS):
                turn_head(h)
                if h:
                    weighted(h - 1)
            weighted(HEADS - 1)

            turn(xn)
            router(0)
            positions(1)
            turn_coef(1)

            for t in range(NT):
                pe.matmul(bank[4 + t][:, :], coefT[:, t * P:(t + 1) * P], b2e[:, 0, :], start=True, stop=True).then_inc(b2_g, 1)
            pe.wait_ge(expert_added, NT)
            gather_nodes(routed0)
            pe.wait_ge(routed0.sem["gathered_act"], 2 * routed0.groups)
            pe.wait_ge(routed0.sem["gathered_dve"], 2 * routed0.groups)
            with pe.Fori(0, EXPERTS) as e:
                def loaded(jj, q):
                    slot, arrived, base = slots0[3 * jj + q]
                    pe.wait_ge(arrived, e * 16 + (base + 16))
                    return slot.rearrange("p (k n) -> p k n", k=KT if q < 2 else 2)

                def expert0(width):
                    s = routed0.sem
                    blocks = (7, 3)[:width // SE]
                    slots = {}

                    def up(j):
                        for q in range(2):
                            if j % 2 == 0:
                                slots[j // 2, q] = loaded(j // 2, q)
                            out = bank[2 * q + j % 2][:, 0:NODES] if width == NODES else bank[j % 2][:, q * width:(q + 1) * width]
                            for k in range(KT):
                                rhs = xT[:, k, :] if width == NODES else routed0.xgT[k][:, bass.ds(e * (2 * SE), width)]
                                last = pe.matmul(out, slots[j // 2, q][:, k, j % 2 * P:(j % 2 + 1) * P], rhs,
                                                 start=(k == 0), stop=(k == KT - 1))
                        last.then_inc(up_g, 1)

                    def down(j):
                        if j % 2 == 0:
                            slots[j // 2, 2] = loaded(j // 2, 2)
                        if j == 0:
                            pe.wait_ge(s["cplace_copied"], e + 1)
                            if width == NODES:
                                pe.wait_ge(expert_added, e * NT + NT)
                        pe.wait_ge(hid_r, e * JT0 + j + 1)
                        for i, b in enumerate((4, 5, 6) if width == NODES else blocks):
                            last = pe.matmul(bank[b][:, :], act2[:, j % 2, i * P:(i + 1) * P], slots[j // 2, 2][:, j % 2, :],
                                             start=(j == 0), stop=(j == JT0 - 1), skip_group_check=True)
                        last.then_inc(down_g, 1)

                    up(0)
                    pe.wait_ge(s["cplace_ready"], e + 1)
                    for i, b in enumerate(blocks if width < NODES else (7,)):
                        for t in range(NT):
                            last = pe.transpose(bank[b][:, t * P:(t + 1) * P], cpl[:, t, i * SE:(i + 1) * SE], ident[:, :])
                    last.then_inc(s["cplace_turned"], 1)
                    for j in range(1, JT0):
                        up(j)
                        down(j - 1)
                    down(JT0 - 1)
                    pe.wait_ge(s["expert_out"], e + 1)
                    if width == NODES:
                        pe.transpose(bank[7][:, 0:P], cpl[:, 0, 0:SE], ident[:, :]).then_inc(s["combined"], 1)
                        return
                    pe.wait_ge(expert_added, e * NT + NT)
                    for t in range(NT):
                        for i in range(len(blocks)):
                            last = pe.matmul(bank[4 + t][:, :], cp2[:, i, t * P:(t + 1) * P], tmp[:, i, :], start=(i == 0), stop=(i == len(blocks) - 1))
                    last.then_inc(s["combined"], 1)

                chosen_by = pe.value_load(crowd[0:1, bass.ds(e, 1)], min_val=0, max_val=NODES)
                with pe.If(chosen_by <= SE):
                    expert0(SE)
                with pe.Else():
                    with pe.If(chosen_by <= 2 * SE):
                        expert0(2 * SE)
                    with pe.Else():
                        expert0(NODES)

            turn(xn)
            for g in range(6):
                which, t = divmod(g, NT)
                if t == 0:
                    arrived("w1", 2 * which)
                    arrived("w1", 2 * which + 1)
                if g >= 4:
                    pe.wait_ge(tab_sum, 12 + g - 3)
                product(bank[g % 4][:, :], lambda k: tile(xT, k, t), lambda k: weight(("w1",), 4 * which + k), KT, table_g)
            pe.wait_ge(tab_lo, 18)
            pe.wait_ge(tab_hi, 18)
            arrived("w2", 0)
            arrived("w2", 1)

            def z1(n, b, f, at, at_b):
                for w in range(2):
                    for t in range(NT):
                        for p in range(2):
                            pe.matmul(bank[n % 4][:, :], tabs1[:, w, p, t, f * P:(f + 1) * P], onehot[:, b % 2, w, t, :],
                                      start=(w, t, p) == (0, 0, 0), stop=False)
                if f == 0:
                    pe.wait_ge(at_loaded[b % 2], at_b)
                pe.matmul(bank[n % 4][:, :], w1c[:, f * P:(f + 1) * P], attr[:, b % 2, :], start=False, stop=True).then_inc(mish_g, 1)

            def message(n, b, s):
                product(bank[n % 4][:, :], lambda k: hT[:, b % 2, k, s * P:(s + 1) * P], lambda k: weight(("w2",), k), KT, mish_g)

            def mish_product(n, at, i2):
                kind, b, s = mish_tile(n)
                if n >= 4:
                    pe.wait_ge(mish_in, at + n - 3)
                if kind == "z":
                    if s == 0:
                        pe.wait_ge(oh_ready, i2 + (NB + b + 1))
                    z1(n, b, s, at, i2 * 8 + 16 * (b // 2 + 1))
                else:
                    if s == 0:
                        pe.wait_ge(mish_r, at + (8 * b + 4))
                    message(n, b, s)

            def aggregate(b, i2):
                pe.wait_ge(em_ready, i2 + (NB + b + 1))
                pe.wait_ge(msg_lo, i2 * 4 + (4 * b + 4))
                for s in range(SUB):
                    for t in range(NT):
                        for p, part in enumerate((mh, ml)):
                            last = pe.matmul(bank[4 + t][:, :], em[:, s, t * P:(t + 1) * P], part[:, s, :],
                                             start=(b, s, p) == (0, 0, 0), stop=(b, s, p) == (NB - 1, SUB - 1, 1), skip_group_check=True)
                            if b == NB - 1 and s == SUB - 1 and p == 1:
                                last.then_inc(agg_g, 1)

            def block1(b, i2, at):
                for q in range(8 if b < NB - 1 else 4):
                    if q == (3 if b < NB - 1 else 0) and b:
                        aggregate(b - 1, i2)
                    mish_product(4 + 8 * b + q, at, i2)

            for n in range(4):
                mish_product(n, 0, 0)
            for b in range(3):
                block1(b, 0, 0)
            with pe.Fori(0, 4) as i:
                for u in range(2):
                    block1(3 + u, i * 2, i * 16)
            block1(NB - 1, 0, 0)
            aggregate(NB - 1, 0)
            turn(y)
            for c in range(4):
                arrived("w3", c)
            for m in range(KT):
                product(bank[m][:, 0:NODES], lambda k: weight(("w3",), k)[:, m * P:(m + 1) * P],
                        lambda k: xT[:, k, :] if k < KT else yT[:, k - KT, :], 2 * KT, mish_g)
            arrived("w4", 0)
            arrived("w4", 1)
            pe.wait_ge(mish_r, MISH + KT)
            for t in range(NT):
                product(bank[4 + t][:, :], lambda k: tile(hidT, k, t), lambda k: weight(("w4",), k), KT, node_g)

            turn(xn)

            def turn_quant(j, u, at):
                pe.wait_ge(quant_r, at + j + 1)
                for c in range(3):
                    for g in range(4):
                        last = pe.transpose(bank[c][:, g * P:(g + 1) * P], qa[:, (4 * c + g) * P:(4 * c + g + 1) * P], ident[:, :])
                    last.then_inc(q_turned, 1)

            def up1(j, u, at):
                pe.wait_ge(qT_a, at * 2 + 2 * j + 2)
                pe.wait_ge(qT_v, at + j + 1)
                for c in range(2):
                    for k in range(KT):
                        last = pe.matmul(bank[3 + c][:, 0:NODES], qT[:, u, c, k * P:(k + 1) * P], xT[:, k, :], start=(k == 0), stop=(k == KT - 1))
                last.then_inc(up_g, 1)

            def step1(j, at):
                up1(j, j % 2, at)
                if j < JT1 - 1:
                    turn_quant(j + 1, (j + 1) % 2, at)
                pe.wait_ge(hid_r, at + UP1 + j + 1)
                for t in range(NT):
                    last = pe.matmul(bank[5 + t][:, :], act2[:, j % 2, t * P:(t + 1) * P], qT[:, j % 2, 2, :],
                                     start=(j == 0), stop=(j == JT1 - 1), skip_group_check=True)
                last.then_inc(down_g, 1)

            turn_quant(0, 0, 0)
            step1(0, 0)
            with pe.Fori(0, 4) as i:
                for j in (1, 2):
                    step1(j, i * 2)
            step1(9, 0)
            step1(10, 0)

            turn(xn)
            values(("ws",), value_g)
            pe.wait_ge(pq_r, 1)
            for t in range(NT):
                last = pe.transpose(bank[3][0:8, t * P:(t + 1) * P], pq[:, 1, t, :], ident[:, :])
            last.then_inc(pqT_g, 1)
            pe.wait_ge(pqT_r, 1)

            def source_row(h):
                if h >= 2:
                    pe.wait_ge(score_r, NT * (h - 1))
                pe.matmul(bank[3 + h % 2][:, 0:NODES], sel8[:, h, :], qT2, start=True, stop=True).then_inc(srow_g, 1)

            turn_head, weighted = attend(HEADS, weighed, 0)
            source_row(0)
            source_row(1)
            for h in range(HEADS):
                turn_head(h)
                if h + 2 < HEADS:
                    source_row(h + 2)
                if h:
                    weighted(h - 1)
            weighted(HEADS - 1)

            turn(xn)
            router(1)
            positions(2)
            turn_coef(2)

            gather_nodes(routed2)
            experts2()

            turn(xn)
            for r in range(4):
                arrived("wr", r, 0)
                arrived("wr", r, 1)
                for t in range(NT):
                    n = r * NT + t
                    if n >= 4:
                        pe.wait_ge(rel_r, n - 3)
                    product(bank[n % 4][:, :], lambda k: tile(xT, k, t), lambda k: weight(("wr", r), k), KT, rel_g)
            values(("wself",), node_g)
            pe.wait_ge(wdeg_r, 1)
            pe.wait_ge(rel_r, 4 * NT)
            pe.matmul(bank[3][:, 0:2 * NT], zeros[:, :], zeros[:, 0:2 * NT], start=True, stop=False, skip_group_check=True)

            def sum3(n, at):
                pe.wait_ge(em_ready, at + (2 * NB + n + 1))
                pe.wait_ge(msg_lo, at + (4 * NB + n + 1))
                for t in range(NT):
                    lhs = em[:, n % 4, t * P:(t + 1) * P]
                    for p, part in enumerate((mh, ml)):
                        last = pe.matmul(bank[t][:, :], lhs, part[:, n % 4, :], start=(n, p) == (0, 0), stop=(n, p) == (ET - 1, 1), skip_group_check=True)
                        if (n, p) == (ET - 1, 1):
                            last.then_inc(agg_g, 1)
                    last = pe.matmul(bank[3][:, 2 * t:2 * t + 2], lhs, wdeg[:, bass.ds(at + n, 1), :].rearrange("p a b -> p (a b)"),
                                     start=False, stop=(n, t) == (ET - 1, NT - 1), skip_group_check=True)
                last.then_inc(agg_g if n == ET - 1 else m_used, 1)

            for n in range(RING):
                sum3(n, 0)
            with pe.Fori(0, 4) as i:
                for c in range(RING, 2 * RING):
                    sum3(c, i * RING)
            for n in range(5 * RING, 6 * RING):
                sum3(n, 0)
            turn(y)
            for k in range(4):
                arrived("wf1", k)
            for m in range(8):
                if m >= 4:
                    pe.wait_ge(gelu_r, m - 3)
                product(bank[m % 4][:, 0:NODES], lambda k: wring[:, W["wf1", k][0], m * P:(m + 1) * P], lambda k: yT[:, k, :], KT, node_g)
            for c in range(4):
                arrived("wf2", c)
            pe.wait_ge(gelu_r, 8)
            for t in range(NT):
                product(bank[4 + t][:, :], lambda k: tile(hidT, k, t), lambda k: weight(("wf2",), k), 8, node_g)

            turn(xn)
            for k in range(KT):
                last = pe.matmul(bank[7][0:8, 0:NODES], gatew[:, 2, k, :], xT[:, k, :], start=(k == 0), stop=(k == KT - 1))
            last.then_inc(route_g, 1)
            with pe.Fori(0, SINKHORN) as i:
                pe.wait_ge(sk_d, i * 8 + 4)
                for t in range(NT):
                    last = pe.matmul(bank[0][:, t * 8:t * 8 + 8], sink[:, 0, t * P:(t + 1) * P], ident[0:8, 0:8], start=True, stop=True)
                last.then_inc(sk_p, 1)
                pe.wait_ge(sk_d, i * 8 + 8)
                for t in range(NT):
                    last = pe.transpose(bank[1][0:8, t * P:(t + 1) * P], sinka[:, 0, t, :], ident[:, :])
                last.then_inc(sk_p, 1)
            pe.wait_ge(chosen_r, 1)
            for c in range(2):
                for t in range(NT):
                    last = pe.transpose(bank[7][:, (c * NT + t) * 8:(c * NT + t) * 8 + 8], sink[:, 3 + c, t * P:(t + 1) * P], ident[0:8, 0:8])
            last.then_inc(sk_p, 1)

            def expert3(v, at):
                for c in range(2):
                    s = f3[2 * v + c]
                    pe.wait_ge(arrive[s], at * 8 + (f3_base[s] + 16))
                pe.wait_ge(added, at * NT + (ADD3 + NT * (v - 1)))
                for t in range(NT):
                    for k in range(KT):
                        last = pe.matmul(bank[3 * v + t][:, :], tile(xT, k, t), wslot(f3[2 * v + k // 2], 2)[:, k % 2, :],
                                         start=(k == 0), stop=(k == KT - 1))
                last.then_inc(down_g, 1)

            with pe.Fori(0, EXPERTS // 2) as i:
                for v in range(2):
                    expert3(v, i * 2)


def kernel(**inputs):
    import numpy as np
    import concourse.bacc as bacc
    from concourse.bass_utils import run_bass_kernel_spmd

    given = {k: np.ascontiguousarray(v) for k, v in inputs.items()}
    sent = dict(given)
    for name, new in (("src", "src_c"), ("dst", "dst_c"), ("edge_type_4", "typ_c"), ("edge_weight", "ew_c")):
        sent[new] = given[name].reshape(ET, P).T
    sent["attrT"] = given["edge_attr_64"].T
    sent["bwa"], sent["bwb"] = given["L0_gnn_bw"][:512], given["L0_gnn_bw"][512:]
    sent["L0_ffn_b1"] = given["L0_ffn_b1"].reshape(EXPERTS, 2 * JT0, P).transpose(2, 0, 1)
    sent["L2_ffn_b1"] = given["L2_ffn_b1"].reshape(EXPERTS, JT2, P).transpose(2, 0, 1)
    sent["L1_gnn_b3"] = given["L1_gnn_b3"].reshape(KT, P).T
    sent["L3_gnn_b_ffn1"] = given["L3_gnn_b_ffn1"].reshape(8, P).T
    sent["L2_gnn_Ws"] = given["L2_gnn_Ws"].transpose(1, 0, 2).reshape(DIM, DIM)
    sent["L2_gnn_Wb"] = given["L2_gnn_Wb"].reshape(DIM)
    sent["L2_gnn_at"] = given["L2_gnn_a_w"][:, :HD].reshape(DIM)
    sent["L2_gnn_as"] = given["L2_gnn_a_w"][:, HD:].reshape(DIM)
    sent["L3_ffn_gate_w"] = given["L3_ffn_gate_w"][0]
    for name in ("edge_attr_64", "edge_type_4", "edge_weight", "L0_gnn_bw", "L2_gnn_a_w"):
        del sent[name]

    nc = bacc.Bacc("TRN2", target_bir_lowering=False, num_devices=1)
    arrays, a = {}, {}
    for name, value in sent.items():
        value = np.ascontiguousarray(value)
        arrays[f"in_{name}"] = value
        a[name] = nc.dram_tensor(f"in_{name}", value.shape, mybir.dt.from_np(value.dtype), kind="ExternalInput").ap()
    out = nc.dram_tensor("out", (NODES, DIM), F32, kind="ExternalOutput").ap()
    table0 = nc.dram_tensor("pair_logits", (NODES * NODES, HEADS), F32, kind="Internal").ap()
    table3 = nc.dram_tensor("relation_rows", (NODES * 4, DIM), F32, kind="Internal").ap()
    build(nc, a, out, table0, table3)
    return run_bass_kernel_spmd(nc, [arrays], core_ids=[0]).results[0]["out"]
```

```python
from contextlib import ExitStack

import concourse.bass as bass
from concourse import mybir

F32 = mybir.dt.float32
F32R = mybir.dt.float32r
BF16 = mybir.dt.bfloat16
I32 = mybir.dt.int32
ALU = mybir.AluOpType
ACT = mybir.ActivationFunctionType
AX = mybir.AxisListType

P = 128
NODES, DIM, EDGES = 384, 512, 6144
NT, KT = NODES // P, DIM // P
ET = EDGES // P
BLK = 512
NB, SUB = EDGES // BLK, BLK // P
HEADS, HD = 8, 64
EPS = 1e-5
NONE = -3e38
FF0, FF1 = 1024, 1408
JT0, JT1, JT2 = FF0 // P, FF1 // P, 2
EXPERTS = 8
CAP = 120
TOP = NODES // EXPERTS
SINKHORN = 8
SLOTS, SW = 6, 1024
SE = P
RING = 8

MISH = 4 + 8 * (NB - 1) + 4
N_SMALL = 14

UP0, UP1 = 0, EXPERTS * JT0
UP2 = UP1 + JT1
UP3 = UP2 + EXPERTS * JT2
ADD1 = 1
ADD2 = ADD1 + NT
ADD3 = ADD2 + 1
ADDED = ADD3 + EXPERTS * NT


class Steps:

    def __init__(self, engine, own):
        self.engine, self.own, self.base, self.local, self.per, self.i = engine, own, {}, {}, {}, None

    def __call__(self, instruction, sem=None):
        sem = sem or self.own
        instruction.then_inc(sem, 1)
        key = sem.name
        self.local[key] = self.local.get(key, 0) + 1
        value = self.base.get(key, 0) + self.local[key]
        if self.i is not None:
            value = self.i * self.per[key] + value
        self.engine.wait_ge(sem, value)

    def fold(self):
        for key, n in self.local.items():
            self.base[key] = self.base.get(key, 0) + n
        self.local = {}

    def skip(self, sem, n):
        self.base[sem.name] = self.base.get(sem.name, 0) + n

    def enter(self, i, per):
        self.fold()
        self.i, self.per = i, {s.name: n for s, n in per.items()}

    def leave(self, iterations):
        for key, n in self.local.items():
            assert n == self.per[key], (key, n, self.per[key])
            self.base[key] = self.base.get(key, 0) + iterations * n
        self.local, self.i = {}, None


def build(nc, a, out, table0, table3):
    with ExitStack() as ctx:
        def sb(name, shape, dt=F32, within=None):
            return (within or ctx).enter_context(nc.sbuf_tensor(name, shape, dt))

        def sem(name):
            return ctx.enter_context(nc.semaphore(name))

        bank = [ctx.enter_context(nc.psum_tensor(f"bank{i}", [P, 512], F32)) for i in range(8)]

        x = sb("x", [P, NT, DIM])
        xn = sb("xn", [P, NT, DIM])
        xT = sb("xT", [P, KT, NODES])
        hold = sb("hold", [P, 3, NT * DIM])
        y = hold[:, 0, :].rearrange("p (t d) -> p t d", t=NT)
        vn = hold[:, 1, :].rearrange("p (t d) -> p t d", t=NT)
        yT = hold[:, 2, :].rearrange("p (k n) -> p k n", k=KT)
        hT = hold[:, :, :].rearrange("p a b -> p (a b)")[:, 0:4096].rearrange("p (a f n) -> p a f n", a=2, f=KT)
        tmp = sb("tmp", [P, 2, DIM])
        wring = sb("wring", [P, SLOTS, SW])
        rows = sb("rows", [P, 6, DIM])
        count = sb("count", [P, NT, NODES])
        stats = sb("stats", [P, 6])
        mv = sb("mv", [P, NT, 2])
        varp = sb("varp", [P, NT])
        rstd = sb("rstd", [P, NT])
        half = sb("half", [P, NT])
        two = sb("two", [P, 1])
        ident = sb("ident", [P, P])
        zeros = sb("zeros", [P, P])
        ones = sb("ones", [P, P])
        upper = sb("upper", [P, P])
        nodeid = sb("nodeid", [P, NT])
        iota = sb("iota", [P, NODES])
        low8 = sb("low8", [P, 8, 8])
        srcc = sb("srcc", [P, ET], I32)
        dstc = sb("dstc", [P, ET], I32)
        typc = sb("typc", [P, ET], I32)
        ewc = sb("ewc", [P, ET])
        srcf = sb("srcf", [P, ET])
        dstf = sb("dstf", [P, ET])
        pair = sb("pair", [P, ET], I32)
        rrow = sb("rrow", [P, ET], I32)
        logit = sb("logit", [P, ET, HEADS])
        ba = sb("ba", [P, 1])
        wa = sb("wa", [P, 1])
        wsel = sb("wsel", [P, HEADS, 2 * HEADS], F32R)
        pairsum = sb("pairsum", [2 * HEADS, HEADS])
        ab = sb("ab", [P, 8])
        b1e0 = sb("b1e0", [P, EXPERTS, 2 * JT0])
        b1e2 = sb("b1e2", [P, EXPERTS, JT2])
        b2e = sb("b2e", [8, 2, DIM])
        b3c = sb("b3c", [P, KT])
        bf1 = sb("bf1", [P, 8])
        gatew = sb("gatew", [P, 3, KT, 8])
        br = sb("br", [P, 2, 8])
        w1hi = sb("w1hi", [P, DIM], F32R)
        small = sb("small", [P, 8, NT * 8])
        small1 = sb("small1", [P, 4, NT])
        cmp8 = sb("cmp8", [P, 2, NT * 8, 8])
        coef = sb("coef", [P, NT, 8])
        coefT = sb("coefT", [8, NODES])
        mneg = sb("mneg", [P, NT, HEADS])
        den = sb("den", [P, NT, HEADS])
        pq = sb("pq", [P, 2, NT, HEADS])
        crowd = sb("crowd", [P, EXPERTS], I32)
        eidx = sb("eidx", [P, 2, BLK], I32)

        with ExitStack() as third:
            eh = sb("eh", [P, 2, NT, NODES], within=third)
            eT = sb("eT", [P, 2, NT, NODES], within=third)
            sink = sb("sink", [8, 5, NODES], within=third)
            sinks = sb("sinks", [8, 8], within=third)
            sinka = sb("sinka", [P, 6, NT, 8], within=third)
            sel8 = sb("sel8", [8, 8, P], within=third)
        with ExitStack() as third:
            more = sb("more", [P, 6, SW], within=third)
            sb("beside_xsplit", [P, 3 * SW], within=third)
            cplace = sb("cplace", [P, NT, EXPERTS * SE], within=third)
        with ExitStack() as second:
            tabs1 = sb("tabs1", [P, 2, 2, NT, 512], F32R, within=second)
            em = sb("em", [P, SUB, NODES], F32R, within=second)
            mh = sb("mh", [P, SUB, DIM], F32R, within=second)
            ml = sb("ml", [P, SUB, DIM], F32R, within=second)
            w1lo = sb("w1lo", [64, DIM], F32R, within=second)
        tabs0 = sb("tabs0", [P, 2, 2, NT, 1024], F32R)
        tabsf = tabs0[:, :, :, :, :].rearrange("p a b t n -> p (a b t n)")
        xsplit = tabsf[:, 6144:9216].rearrange("p (c t n) -> p c t n", c=2, t=NT)
        with ExitStack() as second:
            big = sb("big", [P, NT, NODES * HEADS], within=second)
            wdeg = sb("wdeg", [P, ET, 2], F32R, within=second)
        onehot = sb("onehot", [P, 2, 2, NT, BLK], F32R)
        with ExitStack() as second:
            leak = sb("leak", [P, 2, 2, 512], within=second)
            edge_bits = sb("edge_bits", [P, 3 * 512], within=second)
            lsplit = sb("lsplit", [P, 2, 2, 512], F32R, within=second)
            dots = sb("dots", [2 * HEADS, BLK], within=second)
        work = sb("work", [P, 3, 4, 512])
        attr = sb("attr", [P, BLK])
        attrs = sb("attrs", [P, 2, BLK], F32R)
        ebf = edge_bits[:, :].bitcast(BF16).rearrange("p (s c n) -> p s c n", s=SUB, c=2)
        mz, mt, mr = work[:, 0, :, :], work[:, 1, :, :], work[:, 2, :, :]
        bigf = big[:, :, :].rearrange("p a b -> p (a b)")
        silu2 = bigf[:, 0:768].rearrange("p (a n) -> p a n", a=2)
        act2 = bigf[:, 768:1536].rearrange("p (a n) -> p a n", a=2)
        qraw = bigf[:, 1536:4608].rearrange("p (a c n) -> p a c n", a=2, c=3)
        qa = bigf[:, 4608:7680].rearrange("p (a n) -> p a n", a=2)
        qb = bigf[:, 7680:9216]
        qs = cmp8[:, 0, 0:12, 0:3]
        gather = bigf[:, 0:4096].rearrange("p (a n) -> p a n", a=RING)
        stage = bigf[:, 0:6144].rearrange("p (a n) -> p a n", a=4 * NT)
        brel = bigf[:, 7168:9216].rearrange("p (a n) -> p a n", a=4)
        hidT = bigf[:, 0:3072].rearrange("p (f n) -> p f n", f=8)
        negm = bigf[:, 0:1152].rearrange("p (t n) -> p t n", t=NT)
        srow = bigf[:, 1152:2304].rearrange("p (a n) -> p a n", a=3)
        y3 = [bigf[:, 0:9216].rearrange("p (e n) -> p e n", e=6), hold[:, :, :].rearrange("p a b -> p (a b)")[:, 0:3072].rearrange("p (e n) -> p e n", e=2)]
        diag = xT[:, :, :].rearrange("p k n -> p (k n)")[:, 0:EXPERTS * P].rearrange("p (e n) -> p e n", n=P)
        qT2 = bigf[0:8, 2304:2688]
        prod = bigf[:, 3072:3584]
        cplaceT = bigf[:, 5632:8704].rearrange("p (e n) -> p e n", e=EXPERTS)
        holdf = hold[:, :, :].rearrange("p a b -> p (a b)")
        cp2 = holdf[:, 2048:2048 + 2 * NODES].rearrange("p (a n) -> p a n", a=2)
        cpl = holdf[:, 2816:2816 + 2 * NODES].rearrange("p (t n) -> p t n", t=NT)
        qsum = sb("qsum", [P, 2, 12])
        qT = hold[:, :, :].rearrange("p a b -> p (a b)")[:, 0:3072].rearrange("p (a c n) -> p a c n", a=2, c=3)

        dve_s, act_s, pool_s = sem("dve_step"), sem("act_step"), sem("pool_step")
        arrive = [sem(f"slot{i}_loaded") for i in range(SLOTS)]
        x_loaded, edges_loaded, small_loaded, rows_loaded = map(sem, ("x_or_last_Ww_loaded", "edges_or_biases_loaded", "small_loaded", "rows_loaded"))
        consts_ready, none_ready = sem("consts_ready"), sem("none_ready")
        var_ready, rstd_ready = sem("variance_ready"), sem("deviation_ready")
        nodes_ready, turned, xT_a, xT_v = sem("nodes_ready"), sem("nodes_turned"), sem("xT_act_half"), sem("xT_dve_half")
        value_g, v_ready = sem("value_product"), sem("value_ready")
        table_g, tab_sum, tab_hi, tab_lo = sem("table_product"), sem("table_sum"), sem("table_high"), sem("table_low")
        ix_loaded, at_loaded, at_hi, at_lo = map(sem, ("block_index_loaded", "attr_loaded", "attr_high", "attr_low"))
        oh_ready, em_ready = sem("onehot_ready"), sem("edge_onehot_ready")
        z_g, relu_r, leaky_r, logit_r = map(sem, ("z_product", "relu_ready", "leaky_ready", "logit_ready"))
        count_g = sem("count_product")
        pairs_r, filled, written = map(sem, ("pair_rows_ready", "table0_filled", "table0_written"))
        big_loaded = [sem(f"pair_logits_loaded{t}") for t in range(NT)]
        max_r, score_r, e_ready, e_turned, eT_ready, y_g = map(sem, ("row_max_ready", "score_ready", "weight_ready", "weight_turned", "weightT_ready", "attention_product"))
        elu_in, elu_ex = sem("elu_input"), sem("elu_exp")
        route_g, route_d, route_a, coefT_g, coefT_r, b2_g = map(sem, ("router_product", "router_dve", "router_act", "coef_turned", "coefT_ready", "expert_bias_product"))
        up_g, silu_r, hid_r, down_g, added = map(sem, ("up_product", "silu_ready", "hidden_ready", "down_product", "down_added"))
        mish_g, z_in, m_in, mish_ex, mish_sq, mish_rc, mish_q, mish_r = map(sem, ("mish_product", "z_input", "message_input", "mish_exp", "mish_square", "mish_reciprocal", "mish_ratio", "mish_ready"))
        msg_hi, msg_lo, agg_g = sem("message_high"), sem("message_low"), sem("aggregate_product")
        node_g = sem("node_product")
        q_loaded, quant_r, q_turned, qT_a, qT_v = [sem("quant_raw_loaded0"), sem("quant_raw_loaded1")], sem("quantized"), sem("quantized_turned"), sem("quantizedT_act"), sem("quantizedT_dve")
        pq_r, pqT_g, pqT_r, srow_g = sem("score_parts_ready"), sem("score_parts_turned"), sem("score_partsT_ready"), sem("score_row_product")
        rel_g, rel_r, rel_w = sem("relation_product"), sem("relation_staged"), sem("relation_written")
        gathered = [sem(f"messages_gathered{i}") for i in range(RING)]
        m_used = sem("scaled_messages_used")
        sk_d, sk_a, sk_p = sem("sinkhorn_dve"), sem("sinkhorn_act"), sem("sinkhorn_turned")
        mish_ln, mish_min, exp2_r, gelu_r, coef_r, quant_s = map(sem, ("mish_log", "mish_clamped", "score_exp_ready", "gelu_ready", "coef_ready", "quantize_step"))
        mask_r, pos_g = sem("mask_ready"), sem("position_product")
        weighed, wdeg_r = map(sem, ("weighed_ready", "edge_weights_split"))
        out_done = sem("out_written")
        more_loaded = [sem(f"more{i}_loaded") for i in range(6)]
        expert_added = sem("expert_added")

        class Routed:

            def __init__(self, layer, width):
                self.width, self.groups = width, EXPERTS * width // 512
                self.place = tabsf[:, 0:NT * EXPERTS * width].rearrange("p (t n) -> p t n", t=NT)
                n = EXPERTS * width
                self.xgT = [bigf[:, 1536 + k * n:1536 + (k + 1) * n] for k in range(3)] + [holdf[:, 0:n]]
                self.sem = {name: sem(f"r{layer}_{name}") for name in (
                    "split_high", "split_low", "place_ready", "gather_product", "gathered_act", "gathered_dve",
                    "cplace_ready", "cplace_turned", "cplace_copied", "expert_out", "combined",
                    *(("cplaceT_act", "cplaceT_dve") if layer else ()))}

        routed0, routed2 = Routed(0, 2 * SE), Routed(2, SE)
        row_used = sem("rows_used")
        quant_c, sums_r = sem("quantized_signs"), sem("group_sums")
        sel_ready = sem("selector_ready")
        mish_zq, mish_fix = sem("mish_value"), sem("mish_correction")
        logit_g = sem("logit_product")
        dots_g, dots_r, leaky_hi, leaky_lo, wa_hi, wa_lo = map(sem, ("head_dots", "dots_summed", "leaky_high", "leaky_low", "wa_high", "wa_low"))
        expert3_g, y3_out = sem("expert3_product"), sem("expert3_out")

        def wslot(s, k):
            return wring[:, s, :].rearrange("p (k n) -> p k n", k=k)

        def sm(i):
            return small[:, i, :].rearrange("p (t e) -> p t e", t=NT)

        def node_rows(w, c):
            return w[c * 2 * P:(c + 1) * 2 * P, :].rearrange("(k p) n -> p k n", p=P)

        ROWS = [["L0_gnn_bv", "bwa", "bwb", "L0_gnn_gamma", "L0_gnn_beta"],
                ["L1_gnn_b1", "L1_gnn_b2", "L1_gnn_b4", "L1_gnn_gamma", "L1_gnn_beta"],
                ["L2_gnn_Wb", "L2_gnn_at", "L2_gnn_as"],
                ["L3_gnn_b_self", "L3_gnn_ln1_g", "L3_gnn_ln1_b", "L3_gnn_ln2_g", "L3_gnn_ln2_b", "L3_gnn_b_ffn2"]]
        rows_before = [16 * sum(len(r) for r in ROWS[:i + 1]) for i in range(4)]

        def row(layer, name, w=1):
            r = ROWS[layer].index(name)
            return rows[:, r:r + w, :].rearrange("p a b -> p (a b)")

        owner, arrivals, plan, cursor = {}, [0] * SLOTS, [], [0]

        def stream(src, k, freed_by):
            s = cursor[0] % SLOTS
            cursor[0] += 1
            arrivals[s] += 1
            plan.append((s, src, k, owner.get(s)))
            owner[s] = freed_by
            return s, 16 * arrivals[s]

        def reserve(n, uses, freed_by):
            base = [(cursor[0] + i) % SLOTS for i in range(n)]
            cursor[0] += n
            before = [owner[s] for s in base if s in owner], {s: 16 * arrivals[s] for s in base}
            for s in base:
                arrivals[s] += uses
                owner[s] = freed_by
            return base, *before

        W = {}
        for c in range(2):
            W["wv", c] = stream(node_rows(a["L0_gnn_Wv"], c), 2, (value_g, NT))
        for k in range(6):
            W["ww", k] = stream(a["L0_gnn_Ww"][k * P:(k + 1) * P, :].unsqueeze(1), 1, (table_g, 6 if k < 4 else 12))
        late_ww = {6: hold[:, 0, 0:SW], 7: hold[:, 2, 0:SW]}
        f0, f0_before, f0_base = reserve(6, EXPERTS, (down_g, UP1))
        slots0 = [(wring[:, s, :], arrive[s], f0_base[s]) for s in f0] + [(more[:, i, :], more_loaded[i], 0) for i in range(6)]
        plan.append("layer0")
        for c in range(4):
            W["w1", c] = stream(node_rows(a["L1_gnn_W1"], c), 2, (table_g, 12 + (3 if c < 2 else 6)))
        for c in range(2):
            W["w2", c] = stream(node_rows(a["L1_gnn_W2"], c), 2, (agg_g, NT))
        plan.append("edges1")
        for c in range(4):
            W["w3", c] = stream(node_rows(a["L1_gnn_W3"], c), 2, (mish_g, MISH + KT))
        for c in range(2):
            W["w4", c] = stream(node_rows(a["L1_gnn_W4"], c), 2, (node_g, NT))
        plan.append("ffn1")
        for c in range(2):
            W["ws", c] = stream(node_rows(a["L2_gnn_Ws"], c), 2, (value_g, 2 * NT))
        f2, f2_before, f2_base = reserve(4, EXPERTS // 2, (down_g, UP3))
        plan.append("ffn2")
        for r in range(4):
            for c in range(2):
                W["wr", r, c] = stream(node_rows(a["L3_gnn_W_rel"][r], c), 2, (rel_g, NT * (r + 1)))
        for c in range(2):
            W["wself", c] = stream(node_rows(a["L3_gnn_W_self"], c), 2, (node_g, 2 * NT))
        for k in range(4):
            W["wf1", k] = stream(a["L3_gnn_W_ffn1"][k * P:(k + 1) * P, :].unsqueeze(1), 1, (node_g, 2 * NT + 8))
        for c in range(4):
            W["wf2", c] = stream(node_rows(a["L3_gnn_W_ffn2"], c), 2, (node_g, 3 * NT + 8))
        f3, f3_before, f3_base = reserve(4, EXPERTS // 2, None)
        plan.append("ffn3")

        def mish_tile(n):
            if n < 4:
                return "z", 0, n
            b, q = divmod(n - 4, 8)
            if b == NB - 1:
                return "m", b, q
            return ("m", b, min(q - 3, 3)) if q in (3, 4, 5, 7) else ("z", b + 1, min(q, 3))

        def mish_input_count(n):
            if n >= MISH:
                return m_in, 4 * NB + n - MISH + 1
            kind, b, s = mish_tile(n)
            return (z_in if kind == "z" else m_in), 4 * b + s + 1

        block = ctx.enter_context(nc.Block())

        @block.sync
        def _(sp):
            sp.dma_start(x[:, :, :], a["x"].rearrange("(t p) d -> p t d", p=P)).then_inc(x_loaded, 16)
            for dst, name in ((srcc, "src_c"), (dstc, "dst_c"), (typc, "typ_c"), (ewc, "ew_c")):
                sp.dma_start(dst[:, :], a[name]).then_inc(edges_loaded, 16)

            def load_index(at):
                sp.dma_start(eidx[:, 0, :], a["src"][bass.ds(at, BLK)].partition_broadcast(P)).then_inc(ix_loaded, 16)
                sp.dma_start(eidx[:, 1, :], a["dst"][bass.ds(at, BLK)].partition_broadcast(P)).then_inc(ix_loaded, 16)

            load_index(0)

            def layer0():
                for k, slot in late_ww.items():
                    sp.dma_start(slot, a["L0_gnn_Ww"][k * P:(k + 1) * P, :]).then_inc(x_loaded, 16)
                with sp.Fori(1, NB) as b:
                    sp.wait_ge(oh_ready, b)
                    load_index(b * BLK)
                sp.wait_ge(written, 16 * ET)
                sp.wait_ge(count_g, NB)
                for t in range(NT):
                    sp.dma_start(big[:, t, :], table0.rearrange("(t p n) h -> t p (n h)", t=NT, p=P)[t]).then_inc(big_loaded[t], 16)
                for wait in f0_before:
                    sp.wait_ge(*wait)

                def load(e, j):
                    for q, lo in ((0, 2 * j * P), (1, FF0 + 2 * j * P)):
                        slot, loaded, _ = slots0[3 * j + q]
                        sp.dma_start(slot.rearrange("p (k n) -> p k n", k=KT), a["L0_ffn_W1"][e, :, lo:lo + 2 * P].rearrange("(k p) n -> p k n", p=P)).then_inc(loaded, 16)
                    slot, loaded, _ = slots0[3 * j + 2]
                    sp.dma_start(slot.rearrange("p (k n) -> p k n", k=2), a["L0_ffn_W2"][e, 2 * j * P:(2 * j + 2) * P, :].rearrange("(k p) n -> p k n", p=P)).then_inc(loaded, 16)

                for j in range(JT0 // 2):
                    if j == 2:
                        sp.wait_ge(routed0.sem["gather_product"], KT * routed0.groups)
                    load(0, j)
                with sp.Fori(1, EXPERTS) as e:
                    for j in range(JT0 // 2):
                        sp.wait_ge(down_g, e * JT0 + (2 * (j + 1) - JT0))
                        load(e, j)

            def edges1():
                sp.wait_ge(oh_ready, NB)
                sp.wait_ge(added, ADD1)
                load_index(0)
                for half in range(2):
                    sp.dma_start(attr[half * 64:half * 64 + 64, :], a["L1_gnn_W1"][2 * DIM:2 * DIM + 64, :]).then_inc(at_loaded, 16)

                def load_attr(b, i2):
                    sp.wait_ge(at_lo, i2 + (b + 1))
                    for half in range(2):
                        sp.dma_start(attr[half * 64:half * 64 + 64, :], a["attrT"][:, bass.ds(i2 * BLK + b * BLK, BLK)]).then_inc(at_loaded, 16)

                load_attr(0, 0)
                load_attr(1, 0)
                sp.wait_ge(oh_ready, NB + 1)
                load_index(BLK)
                with sp.Fori(1, NB // 2) as i:
                    for u in range(2):
                        sp.wait_ge(oh_ready, i * 2 + (NB + u))
                        load_index(i * (2 * BLK) + u * BLK)
                        load_attr(u, i * 2)

            def ffn1():
                def load(u, j):
                    sp.dma_start(qraw[:, u, 0, :], a["L1_ffn_w_gate"][bass.ds(j * P, P), :]).then_inc(q_loaded[u], 16)
                    sp.dma_start(qraw[:, u, 1, :], a["L1_ffn_w_up"][bass.ds(j * P, P), :]).then_inc(q_loaded[u], 16)
                    sp.dma_start(qraw[:, u, 2, :].rearrange("p (g n) -> p g n", g=4),
                                 a["L1_ffn_w_down"][:, bass.ds(j * P, P)].rearrange("(g p) n -> p g n", p=P)).then_inc(q_loaded[u], 16)

                sp.wait_ge(node_g, NT)
                load(0, 0)
                load(1, 1)
                with sp.Fori(1, JT1 // 2) as i:
                    for u in range(2):
                        sp.wait_ge(quant_r, i * 2 + (u - 1))
                        load(u, i * 2 + u)
                sp.wait_ge(quant_r, JT1 - 2)
                load(0, JT1 - 1)

            def ffn2():
                def load(e, v):
                    s1, s2 = f2[2 * v], f2[2 * v + 1]
                    sp.dma_start(wslot(s1, KT), a["L2_ffn_W1"][e].rearrange("(k p) n -> p k n", p=P)).then_inc(arrive[s1], 16)
                    sp.dma_start(wslot(s2, 2), a["L2_ffn_W2"][e].rearrange("(k p) n -> p k n", p=P)).then_inc(arrive[s2], 16)

                for wait in f2_before:
                    sp.wait_ge(*wait)
                load(0, 0)
                load(1, 1)
                with sp.Fori(1, EXPERTS // 2) as i:
                    for v in range(2):
                        sp.wait_ge(down_g, i * (2 * JT2) + (UP2 + JT2 * (v - 1)))
                        load(i * 2 + v, v)

            def ffn3():
                def load(e, v):
                    for c in range(2):
                        s = f3[2 * v + c]
                        sp.dma_start(wslot(s, 2), node_rows(a["L3_ffn_experts"][e], c)).then_inc(arrive[s], 16)

                for wait in f3_before:
                    sp.wait_ge(*wait)
                load(0, 0)
                load(1, 1)
                with sp.Fori(1, EXPERTS // 2) as i:
                    for v in range(2):
                        sp.wait_ge(expert3_g, i * (2 * NT) + NT * (v - 1))
                        load(i * 2 + v, v)

            parts = {"layer0": layer0, "edges1": edges1, "ffn1": ffn1, "ffn2": ffn2, "ffn3": ffn3}
            for item in plan:
                if isinstance(item, str):
                    parts[item]()
                    continue
                s, src, k, before = item
                if before is not None:
                    sp.wait_ge(*before)
                sp.dma_start(wslot(s, k), src).then_inc(arrive[s], 16)
            for t in range(NT):
                sp.wait_ge(added, ADD3 + ((t + 1) * EXPERTS if t < NT - 1 else t * EXPERTS + 1))
                sp.dma_start(out[t * P:(t + 1) * P, :], x[:, t, :]).then_inc(out_done, 16)
            sp.wait_ge(out_done, 16 * NT)

        @block.gpsimd
        def _(pool):
            step = Steps(pool, pool_s)
            step(pool.memset(big[:, 0, :], NONE), none_ready)
            for tile, value in ((ident, 0.0), (zeros, 0.0), (ones, 1.0), (upper, 1.0), (half, -0.5), (two, 2.0), (low8, 1.0)):
                step(pool.memset(tile[:], value))
            step(pool.affine_select(out=ident[:, :], in_=ident[:, :], compare_op=ALU.not_equal, fill=1.0, base=0,
                                    pattern=[[-1, P]], channel_multiplier=1))
            step(pool.affine_select(out=upper[:, :], in_=upper[:, :], compare_op=ALU.is_gt, fill=0.0, base=0,
                                    pattern=[[1, P]], channel_multiplier=-1))
            step(pool.affine_select(out=low8[:, :, :], in_=low8[:, :, :], compare_op=ALU.is_gt, fill=0.0, base=0,
                                    pattern=[[1, 8], [-1, 8]], channel_multiplier=0))
            step(pool.iota(nodeid[:, :], pattern=[[P, NT]], base=0, channel_multiplier=1, allow_small_or_imprecise_dtypes=True))
            step(pool.iota(iota[:, :], pattern=[[1, NODES]], base=0, channel_multiplier=0, allow_small_or_imprecise_dtypes=True), consts_ready)
            done = [0]

            def deviations(n):
                for _ in range(n):
                    done[0] += 1
                    pool.wait_ge(var_ready, done[0])
                    step(pool.tensor_tensor(rstd[:, :], varp[:, :], half[:, :], ALU.pow), rstd_ready)

            deviations(1)
            pool.wait_ge(pairs_r, 1)
            pool.wait_ge(filled, 16 * NT)
            for b in range(NB):
                pool.wait_ge(logit_r, b + 1)
                for s in range(SUB):
                    e = b * SUB + s
                    if e:
                        pool.wait_ge(written, 16 * e)
                    pool.indirect_dma_start(out=table0, out_offset=bass.IndirectOffsetOnAxis(ap=pair[:, e:e + 1], axis=0),
                                            in_=logit[:, e, :], in_offset=None).then_inc(written, 16)
            deviations(3)

            def ratio(n, at):
                pool.wait_ge(mish_sq, at + n + 1)
                pool.wait_ge(mish_rc, at + n + 1)
                pool.tensor_tensor(mt[:, n % 4, :], mt[:, n % 4, :], mr[:, n % 4, :], ALU.mult).then_inc(mish_q, 1)
                pool.wait_ge(mish_q, at + n + 1)
                pool.tensor_tensor(mz[:, n % 4, :], mz[:, n % 4, :], mt[:, n % 4, :], ALU.mult).then_inc(mish_zq, 1)

            for n in range(4):
                ratio(n, 0)
            with pool.Fori(0, NB - 1) as i:
                for q in range(8):
                    ratio(4 + q, i * 8)
            for n in range(MISH - 4, MISH + 4):
                ratio(n, 0)
            deviations(1)
            def signs(j, i):
                pool.wait_ge(quant_c, i * 2 + (j + 1))
                pool.tensor_tensor(qa[:, j % 2, :], qa[:, j % 2, :], qb, ALU.subtract).then_inc(quant_r, 1)

            deviations(1)
            signs(0, 0)
            with pool.Fori(0, JT1 // 2) as i:
                signs(1, i)
                signs(2, i)
            step(pool.memset(sel8[:, :, :], 0.0))
            step(pool.affine_select(out=sel8[:, :, :], in_=sel8[:, :, :], compare_op=ALU.not_equal, fill=1.0, base=0,
                                    pattern=[[-1, 8], [0, P]], channel_multiplier=1), sel_ready)
            deviations(3)
            pool.wait_ge(rel_w, 16 * 4 * NT)
            for e in range(ET):
                if e >= RING:
                    pool.wait_ge(msg_lo, 4 * NB + e - RING + 1)
                pool.indirect_dma_start(out=gather[:, e % RING, :], out_offset=None, in_=table3,
                                        in_offset=bass.IndirectOffsetOnAxis(ap=rrow[:, e:e + 1], axis=0)).then_inc(gathered[e % RING], 16)
            deviations(3)

        @block.scalar
        def _(act):
            step = Steps(act, act_s)
            for r, name in enumerate(ROWS[0]):
                act.dma_start(rows[:, r, :], a[name].partition_broadcast(P)).then_inc(rows_loaded, 16)
            def load_rows(layer, uses):
                act.wait_ge(row_used, uses)
                for r, name in enumerate(ROWS[layer]):
                    act.dma_start(rows[:, r, :], a[name].partition_broadcast(P)).then_inc(rows_loaded, 16)

            turns = [0]

            def turn(dst):
                for k in (0, 2):
                    act.wait_ge(turned, KT * turns[0] + k + 1)
                    step(act.activation(dst[:, k, :], bank[k][:, 0:NODES], ACT.Copy), xT_a)
                turns[0] += 1

            def split_tables(first, n, tabs, cols):
                for g in range(n):
                    act.wait_ge(tab_sum, first + g + 1)
                    which, r = divmod(g, n // 2)
                    t, c = divmod(r, cols)
                    step(act.activation(tabs[:, which, 0, t, c * 512:c * 512 + 512], tmp[:, g % 2, :], ACT.Copy), tab_hi)

            act.wait_ge(consts_ready, 1)
            turn(xT)
            smalls = ((ba[:, :], a["L0_gnn_ba"].partition_broadcast(P)), (wa[:, :], a["L0_gnn_Wa"]),
                      (ab[:, :], a["L2_gnn_a_b"].partition_broadcast(P)), (b1e0[:, :, :], a["L0_ffn_b1"]),
                      (b1e2[:, :, :], a["L2_ffn_b1"]), (b2e[:, 0, :], a["L0_ffn_b2"]), (b2e[:, 1, :], a["L2_ffn_b2"]),
                      (b3c[:, :], a["L1_gnn_b3"]), (bf1[:, :], a["L3_gnn_b_ffn1"]),
                      (gatew[:, 0, :, :], a["L0_ffn_Wg"].rearrange("(k p) e -> p k e", p=P)),
                      (gatew[:, 1, :, :], a["L2_ffn_Wr"].rearrange("(k p) e -> p k e", p=P)),
                      (gatew[:, 2, :, :], a["L3_ffn_gate_w"].rearrange("(k p) e -> p k e", p=P)),
                      (br[:, 0, :], a["L0_ffn_bg"].partition_broadcast(P)), (br[:, 1, :], a["L2_ffn_br"].partition_broadcast(P)))
            assert len(smalls) == N_SMALL
            for dst, src in smalls:
                act.dma_start(dst, src).then_inc(small_loaded, 16)
            act.wait_ge(none_ready, 1)
            for t in range(NT):
                act.dma_start(table0.rearrange("(t p n) h -> t p (n h)", t=NT, p=P)[t], big[:, 0, :]).then_inc(filled, 16)
            act.wait_ge(small_loaded, 16 * N_SMALL)
            step(act.activation(wsel[:, :, :], zeros[:, :].rearrange("p (a b) -> p a b", a=HEADS), ACT.Copy))
            for h in range(HEADS):
                step(act.activation(wsel[:, h, 2 * h:2 * h + 1], wa[:, :], ACT.Copy), wa_hi)
            split_tables(0, 12, tabs0, 2)

            def relu(n, at):
                act.wait_ge(z_g, at + n + 1)
                if n >= 2:
                    act.wait_ge(leaky_r, at + n - 1)
                act.activation(leak[:, 0, n % 2, :], bank[n % 4][:, :], ACT.Relu, scale=0.99).then_inc(relu_r, 1)

            def leaky_high(n, at):
                act.wait_ge(leaky_r, at + n + 1)
                if n >= 2:
                    act.wait_ge(dots_g, at + n - 1)
                act.activation(lsplit[:, n % 2, 0, :], leak[:, 1, n % 2, :], ACT.Copy).then_inc(leaky_hi, 1)

            for n in range(8):
                relu(n, 0)
                if n:
                    leaky_high(n - 1, 0)
            with act.Fori(0, 5) as i:
                for c in range(8, 24):
                    relu(c, i * 16)
                    leaky_high(c - 1, i * 16)
            for n in range(88, 96):
                relu(n, 0)
                leaky_high(n - 1, 0)
            leaky_high(95, 0)
            for h in range(HEADS):
                if h >= 2:
                    act.wait_ge(e_turned, NT * (h - 1))
                for t in range(NT):
                    if h == 0:
                        act.wait_ge(max_r, t + 1)
                    step(act.activation(eh[:, h % 2, t, :], big[:, t, :].rearrange("p (n h) -> p h n", h=HEADS)[:, h, :],
                                        ACT.Exp, bias=mneg[:, t, h:h + 1], accum_out=den[:, t, h:h + 1]), e_ready)

            def elu(first):
                for t in range(NT):
                    act.wait_ge(elu_in, first + t + 1)
                    step(act.activation(vn[:, t, :], vn[:, t, :], ACT.Exp), elu_ex)

            elu(0)
            load_rows(1, 1)
            turn(xT)
            act.wait_ge(small_loaded, 16 * N_SMALL)
            act.wait_ge(route_d, 1)
            step(act.activation(small[:, 1, :], small[:, 1, :], ACT.Exp), route_a)

            def gather_nodes(r):
                s = r.sem
                for t in range(NT):
                    act.activation(xsplit[:, 0, t, :], xn[:, t, :], ACT.Copy).then_inc(s["split_high"], 1)
                for g in range(r.groups):
                    for k in (0, 2):
                        act.wait_ge(s["gather_product"], 4 * g + k + 1)
                        act.activation(r.xgT[k][:, g * 512:g * 512 + 512], bank[4 * (g % 2) + k][:, :], ACT.Copy).then_inc(s["gathered_act"], 1)

            gather_nodes(routed0)
            with act.Fori(0, EXPERTS) as e:
                def expert0(width):
                    for j in range(JT0):
                        act.wait_ge(up_g, e * JT0 + j + 1)
                        act.activation(silu2[:, j % 2, 0:width], bank[j % 2][:, 0:width], ACT.Silu,
                                       bias=b1e0[:, bass.ds(e, 1), j]).then_inc(silu_r, 1)
                    act.wait_ge(down_g, e * JT0 + JT0)
                    if width == 2 * SE:
                        act.activation(tmp[:, 1, :], bank[3][:, :], ACT.Copy)
                    act.activation(tmp[:, 0, :], bank[7][:, :], ACT.Copy).then_inc(routed0.sem["expert_out"], 1)

                chosen_by = act.value_load(crowd[0:1, bass.ds(e, 1)], min_val=0, max_val=NODES)
                with act.If(chosen_by <= SE):
                    expert0(SE)
                with act.Else():
                    with act.If(chosen_by <= 2 * SE):
                        expert0(2 * SE)
                    with act.Else():
                        expert0(NODES)
            turn(xT)
            split_tables(12, 6, tabs1, 1)

            def mish_high(n, at, at_m):
                kind, b, s = mish_tile(n)
                if kind == "m":
                    act.wait_ge(mish_r, at + n + 1)
                    act.activation(mh[:, s, :], mz[:, n % 4, :], ACT.Copy).then_inc(msg_hi, 1)

            def mish_reciprocal(n, at, width=512):
                act.wait_ge(mish_sq, at + n + 1)
                act.activation(mr[:, n % 4, 0:width], mt[:, n % 4, 0:width], ACT.Ln, bias=two[:, 0:1]).then_inc(mish_ln, 1)
                act.wait_ge(mish_ln, at + n + 1)
                act.activation(mr[:, n % 4, 0:width], mr[:, n % 4, 0:width], ACT.Exp, scale=-1.0).then_inc(mish_rc, 1)

            def mish_exp(n, at, width=512, i2=0):
                if n < MISH and mish_tile(n)[0] == "z":
                    act.wait_ge(mish_g, at + n + 1)
                    if n >= 4:
                        act.wait_ge(mish_r, at + n - 3)
                        if mish_tile(n - 4)[0] == "m":
                            act.wait_ge(msg_lo, i2 * 4 + mish_input_count(n - 4)[1])
                    act.activation(mt[:, n % 4, :], bank[n % 4][:, :], ACT.Exp).then_inc(mish_ex, 1)
                    act.activation(mz[:, n % 4, :], bank[n % 4][:, :], ACT.Copy).then_inc(z_in, 1)
                    return
                act.wait_ge(m_in, i2 * 4 + mish_input_count(n)[1])
                act.activation(mt[:, n % 4, 0:width], mz[:, n % 4, 0:width], ACT.Exp).then_inc(mish_ex, 1)

            def mish_step(n, at, first=0, i2=0):
                if n - 4 >= first:
                    mish_high(n - 4, at, at)
                if first <= n - 1 < MISH:
                    mish_reciprocal(n - 1, at)
                if n < MISH:
                    mish_exp(n, at, i2=i2)

            nc.scalar.preload_act_table_set("natural_log_exp_and_others")
            def attr_high(q, i2):
                act.wait_ge(at_loaded, i2 * 32 + 32 * (q + 1))
                dst = attrs[:, (q - 1) % 2, :] if q else w1hi[:, :]
                act.activation(dst, attr[:, :], ACT.Copy).then_inc(at_hi, 1)

            def step1(n, at, i2=0):
                mish_step(n, at, i2=i2)
                if n % 8 == 7 and n >= 4 and (n - 4) // 8 < NB - 2:
                    attr_high((n - 4) // 8 + 3, i2)

            for q in range(3):
                attr_high(q, 0)
            for n in range(12):
                step1(n, 0)
            with act.Fori(0, 4) as i:
                for c in range(12, 28):
                    step1(c, i * 16, i * 2)
            for n in range(76, MISH - 4):
                step1(n, 0)
            mish_high(MISH - 8, 0, 0)
            mish_reciprocal(MISH - 5, 0)
            for n in (MISH - 7, MISH - 6, MISH - 5):
                mish_high(n, 0, 0)
            for n in range(MISH - 4, MISH + 4):
                mish_step(n, 0, MISH - 4)
            turn(yT)
            for m in range(KT + 1):
                if m < KT:
                    mish_exp(MISH + m, 0, NODES)
                if m:
                    mish_reciprocal(MISH + m - 1, 0, NODES)
            load_rows(2, 2)
            magnitudes = holdf[:, 3072:4608].rearrange("p (g n) -> p g n", g=12)

            def group_sums(j, u, i):
                act.wait_ge(q_loaded[u], i * 48 + 48 * (j // 2 + 1))
                if j >= 2:
                    act.wait_ge(quant_c, i * 2 + j - 1)
                if j >= 1:
                    act.wait_ge(sums_r, i * 24 + 12 * j)
                for g in range(12):
                    act.activation(magnitudes[:, g, :], qraw[:, u, g // 4, g % 4 * P:(g % 4 + 1) * P], ACT.Abs,
                                   accum_out=qsum[:, u, g:g + 1]).then_inc(sums_r, 1)

            def turn_quant(j, u, at):
                for c in range(2):
                    act.wait_ge(q_turned, at * 3 + 3 * j + c + 1)
                    act.activation(qT[:, u, c, :], bank[c][:, :], ACT.Copy).then_inc(qT_a, 1)

            def hidden1(j, u, at):
                act.wait_ge(up_g, at + UP1 + j + 1)
                act.activation(silu2[:, u, :], bank[3][:, 0:NODES], ACT.Silu).then_inc(silu_r, 1)

            group_sums(0, 0, 0)
            group_sums(1, 1, 0)
            turn(xT)
            turn_quant(0, 0, 0)
            group_sums(2, 0, 0)
            hidden1(0, 0, 0)
            turn_quant(1, 1, 0)
            with act.Fori(0, 4) as i:
                for j in (1, 2):
                    group_sums(j + 2, j % 2, i)
                    hidden1(j, j % 2, i * 2)
                    turn_quant(j + 1, (j + 1) % 2, i * 2)
            hidden1(9, 1, 0)
            turn_quant(10, 0, 0)
            hidden1(10, 0, 0)
            turn(xT)

            def turned_weights(h):
                for d in range(NT):
                    act.wait_ge(e_turned, (HEADS + h) * NT + d + 1)
                    act.activation(eT[:, h % 2, d, :], bank[d][:, 0:NODES], ACT.Copy).then_inc(eT_ready, 1)

            for h in range(HEADS):
                for t in range(NT):
                    n = h * NT + t
                    act.wait_ge(score_r, n + 1)
                    step(act.activation(srow[:, t, :], srow[:, t, :], ACT.Exp, bias=mneg[:, t, h:h + 1]), exp2_r)
                if h:
                    turned_weights(h - 1)
            turned_weights(HEADS - 1)
            load_rows(3, 3)
            turn(xT)
            act.wait_ge(route_d, 2)
            step(act.activation(small[:, 1, :], small[:, 1, :], ACT.Exp), route_a)
            def experts2():
                s = routed2.sem
                for e in range(0, EXPERTS, 2):
                    act.wait_ge(s["cplace_turned"], e + 1)
                    act.activation(cplaceT[:, e, :], bank[e % 4][:, 0:NODES], ACT.Copy).then_inc(s["cplaceT_act"], 1)

                def expert_out(c, i2):
                    act.wait_ge(down_g, i2 * JT2 + (UP2 + (c + 1) * JT2))
                    if c >= 2:
                        act.wait_ge(s["combined"], i2 + c - 1)
                    act.activation(tmp[:, c % 2, :], bank[3 + c % 2][:, :], ACT.Copy).then_inc(s["expert_out"], 1)

                def body(c, i2):
                    for j in range(JT2):
                        act.wait_ge(up_g, i2 * JT2 + (UP2 + c * JT2 + j + 1))
                        act.activation(act2[:, j % 2, 0:SE], bank[j % 2][:, 0:SE], ACT.Gelu,
                                       bias=b1e2[:, bass.ds(i2 + c, 1), j]).then_inc(hid_r, 1)
                        if j == 0 and c:
                            expert_out(c - 1, i2)

                for c in range(3):
                    body(c, 0)
                with act.Fori(0, 2) as i:
                    body(3, i * 2)
                    body(4, i * 2)
                body(7, 0)
                expert_out(7, 0)

            gather_nodes(routed2)
            experts2()
            act.wait_ge(routed2.sem["combined"], EXPERTS)
            for r in range(4):
                act.dma_start(brel[:, r, :], a["L3_gnn_b_rel"][r, :].partition_broadcast(P)).then_inc(edges_loaded, 16)
            turn(xT)
            for n in range(4 * NT):
                act.wait_ge(rel_r, n + 1)
                r, t = divmod(n, NT)
                act.dma_start(table3.rearrange("(t p r) d -> t r p d", t=NT, p=P)[t, r], stage[:, n, :]).then_inc(rel_w, 16)

            def scaled_high(n, at, turn_value):
                act.wait_ge(gathered[n % RING], turn_value)
                if n >= 4:
                    act.wait_ge(m_used, at + n - 3)
                act.activation(mh[:, n % 4, :], gather[:, n % RING, :], ACT.Copy, scale=ewc[:, bass.ds(at + n, 1)]).then_inc(msg_hi, 1)

            for n in range(RING):
                scaled_high(n, 0, 16)
            with act.Fori(0, 4) as i:
                for c in range(RING, 2 * RING):
                    scaled_high(c, i * RING, i * 16 + 32)
            for n in range(5 * RING, 6 * RING):
                scaled_high(n, 0, 96)
            turn(yT)
            for m in range(8):
                act.wait_ge(node_g, 2 * NT + m + 1)
                step(act.activation(hidT[:, m, :], bank[m % 4][:, 0:NODES], ACT.Gelu, bias=bf1[:, m:m + 1]), gelu_r)
            turn(xT)
            act.wait_ge(sk_d, 1)
            step(act.activation(sink[:, 0, :], sink[:, 0, :], ACT.Ln), sk_a)

            def expert3_out(e, t, i):
                act.wait_ge(expert3_g, i * (2 * NT) + (e * NT + t + 1))
                late = isinstance(i, int) and e >= 6
                dst = y3[1][:, e - 6:e - 5, t * 512:t * 512 + 512] if late else y3[0][:, bass.ds(i * 2 + e, 1), t * 512:t * 512 + 512]
                act.activation(dst.rearrange("p a n -> p (a n)"), bank[2 + 3 * (e % 2) + t][:, :], ACT.Copy).then_inc(y3_out, 1)

            def sinkhorn(v, i, last=False):
                at = i * 16 + 8 * v
                act.wait_ge(sk_d, at + 3)
                step(act.activation(sink[:, 1, :], sink[:, 0, :], ACT.Exp, bias=sinks[:, 0:1], accum_out=sinks[:, 1:2]), sk_a)
                step(act.activation(sinks[:, 2:3], sinks[:, 1:2], ACT.Ln), sk_a)
                if v:
                    expert3_out(v - 1, NT - 1, i)
                act.wait_ge(sk_d, at + 6)
                step(act.activation(sinka[:, 2, :, :], sinka[:, 1, :, :], ACT.Exp), sk_a)
                act.wait_ge(sk_d, at + 7)
                step(act.activation(small1[:, 1, :], small1[:, 0, :], ACT.Ln), sk_a)
                expert3_out(v, 0, i)
                if last:
                    act.wait_ge(sk_d, 1 + 8 * SINKHORN)
                    step(act.activation(sink[:, 0, :], sink[:, 0, :], ACT.Exp), sk_a)
                expert3_out(v, 1, i)

            nc.scalar.preload_act_table_set("natural_log_exp_and_others")
            for v in range(2):
                sinkhorn(v, 0)
            step.fold()
            with act.Fori(0, SINKHORN // 2 - 2) as i:
                step.enter(i, {sk_a: 8})
                for v in range(2, 4):
                    sinkhorn(v, i)
            step.leave(SINKHORN // 2 - 2)
            for v in range(SINKHORN - 2, SINKHORN):
                sinkhorn(v, 0, v == SINKHORN - 1)
            expert3_out(EXPERTS - 1, NT - 1, 0)
            act.wait_ge(coef_r, 3)
            for e in range(EXPERTS):
                step(act.activation(diag[:, e, :], ident[:, :], ACT.Copy, scale=coef[:, NT - 1, e:e + 1]), sk_a)

        @block.vector
        def _(dve):
            step = Steps(dve, dve_s)
            turns = [0]
            norms = [0]

            def norm(src, dst, signal=None):
                for t in range(NT):
                    step(dve.bn_stats(stats[:, :], src[:, t, :]))
                    step(dve.bn_aggr(mv[:, t, :], stats[:, :]))
                norms[0] += 1
                step(dve.tensor_scalar(varp[:, :], mv[:, :, 1], EPS, None, ALU.add), var_ready)
                dve.wait_ge(rstd_ready, norms[0])
                for t in range(NT):
                    step(dve.tensor_scalar(dst[:, t, :], src[:, t, :], mv[:, t, 0:1], rstd[:, t:t + 1], ALU.subtract, ALU.mult), signal)

            def turn(dst):
                for k in (1, 3):
                    dve.wait_ge(turned, KT * turns[0] + k + 1)
                    step(dve.tensor_copy(dst[:, k, :], bank[k][:, 0:NODES]), xT_v)
                turns[0] += 1

            def tables(first, n, tabs, cols, bias, between=None):
                def low(g):
                    which, r = divmod(g, n // 2)
                    t, c = divmod(r, cols)
                    dve.wait_ge(tab_hi, first + g + 1)
                    step(dve.tensor_tensor(tabs[:, which, 1, t, c * 512:c * 512 + 512], tmp[:, g % 2, :],
                                           tabs[:, which, 0, t, c * 512:c * 512 + 512], ALU.subtract), tab_lo)

                for g in range(n):
                    if between and g == n // 2:
                        between()
                    dve.wait_ge(table_g, first + g + 1)
                    which, r = divmod(g, n // 2)
                    if which == 0:
                        step(dve.tensor_tensor(tmp[:, g % 2, :], bank[g % 4][:, :], bias(r % cols), ALU.add), tab_sum)
                    else:
                        step(dve.tensor_copy(tmp[:, g % 2, :], bank[g % 4][:, :]), tab_sum)
                    if g:
                        low(g - 1)
                low(n - 1)

            def onehots(par, at_ix):
                dve.wait_ge(ix_loaded, at_ix)
                for w in range(2):
                    for t in range(NT):
                        last = dve.tensor_scalar(onehot[:, par, w, t, :], eidx[:, w, :], nodeid[:, t:t + 1], None, ALU.is_equal)
                        if (w, t) == (1, NT - 1):
                            last.then_inc(oh_ready, 1)
                        
            dve.wait_ge(x_loaded, 16)
            norm(x, xn, nodes_ready)
            dve.wait_ge(edges_loaded, 64)
            step(dve.tensor_copy(srcf[:, :], srcc[:, :]))
            step(dve.tensor_copy(dstf[:, :], dstc[:, :]))
            step(dve.scalar_tensor_tensor(pair[:, :], srcf[:, :], float(NODES), dstf[:, :], ALU.mult, ALU.add), pairs_r)
            step(dve.scalar_tensor_tensor(rrow[:, :], srcc[:, :], 4.0, typc[:, :], ALU.mult, ALU.add))
            turn(xT)
            dve.wait_ge(rows_loaded, rows_before[0])

            def values(first, layer, name, after=None):
                for t in range(NT):
                    dve.wait_ge(value_g, first + t + 1)
                    step(dve.tensor_tensor(vn[:, t, :], bank[4 + t][:, :], row(layer, name), ALU.add), v_ready)
                    if after is not None:
                        after(t)

            values(0, 0, "L0_gnn_bv")
            dve.wait_ge(small_loaded, 16 * N_SMALL)
            dve.wait_ge(wa_hi, HEADS)
            for h in range(HEADS):
                step(dve.tensor_tensor(wsel[:, h, 2 * h + 1:2 * h + 2], wa[:, :], wsel[:, h, 2 * h:2 * h + 1], ALU.subtract), wa_lo)
            step(dve.tensor_reduce(pairsum[:, :], ident[0:2 * HEADS, 0:2 * HEADS].rearrange("p (h c) -> p h c", c=2), AX.X, ALU.add), wa_lo)

            def first_onehots():
                dve.wait_ge(filled, 16 * NT)
                onehots(0, 32)

            tables(0, 12, tabs0, 2, lambda c: rows[:, 1 + c, :], first_onehots)

            def edge_onehots(b, at):
                for s in range(SUB):
                    for w, f in ((0, srcf), (1, dstf)):
                        last = dve.tensor_scalar(ebf[:, s, w, :], iota[:, :], f[:, bass.ds(at + s, 1)], None, ALU.is_equal)
                last.then_inc(em_ready, 1)

            def leaky(n, at):
                dve.wait_ge(relu_r, at + n + 1)
                if n >= 2:
                    dve.wait_ge(leaky_lo, at + n - 1)
                dve.scalar_tensor_tensor(leak[:, 1, n % 2, :], bank[n % 4][:, :], 0.01, leak[:, 0, n % 2, :], ALU.mult, ALU.add).then_inc(leaky_r, 1)

            def leaky_low(n, at):
                dve.wait_ge(leaky_hi, at + n + 1)
                dve.tensor_tensor(lsplit[:, n % 2, 1, :], leak[:, 1, n % 2, :], lsplit[:, n % 2, 0, :], ALU.subtract).then_inc(leaky_lo, 1)

            def dots_out(b, at):
                dve.wait_ge(dots_g, at * HEADS + HEADS * (b + 1))
                dve.tensor_copy(dots[:, :], bank[4][0:2 * HEADS, :]).then_inc(dots_r, 1)

            def logits(b, at, at_e):
                dve.wait_ge(logit_g, at + b + 1)
                dve.tensor_scalar(logit[:, bass.ds(at_e, SUB), :], bank[4][:, 0:32].rearrange("p (s h) -> p s h", s=SUB),
                                  ba[:, 0:1], None, ALU.add).then_inc(logit_r, 1)

            def block0(b, par, i2, i16):
                for h in range(HEADS):
                    leaky(b * 8 + h, i16)
                    if b or h:
                        leaky_low(b * 8 + h - 1, i16)
                    if h == 0 and b < NB - 1:
                        onehots(1 - par, (i2 + (b + 2)) * 32)
                    if h == 1:
                        if b >= 1:
                            dots_out(b - 1, i2)
                            dve.wait_ge(count_g, i2 + b)
                        edge_onehots(b, (i2 + b) * SUB)
                    if h == 2 and b >= 1:
                        logits(b - 1, i2, (i2 + (b - 1)) * SUB)

            block0(0, 0, 0, 0)
            with dve.Fori(0, 5) as i:
                for u in range(2):
                    block0(1 + u, 1 - u, i * 2, i * 16)
            block0(NB - 1, 1, 0, 0)
            leaky_low(NB * 8 - 1, 0)
            dots_out(NB - 1, 0)
            logits(NB - 1, 0, (NB - 1) * SUB)
            dve.wait_ge(count_g, NB)
            for t in range(NT):
                step(dve.tensor_copy(count[:, t, :], bank[5 + t][:, 0:NODES]))
            for t in range(NT):
                dve.wait_ge(big_loaded[t], 16)
                step(dve.tensor_reduce(mneg[:, t, :], big[:, t, :].rearrange("p (n h) -> p h n", h=HEADS), AX.X, ALU.max))
                step(dve.tensor_scalar(mneg[:, t, :], mneg[:, t, :], -1e30, -1.0, ALU.max, ALU.mult), max_r)

            def turned_weights(h):
                for d in range(NT):
                    dve.wait_ge(e_turned, turned_heads[0] * NT + d + 1)
                    step(dve.tensor_copy(eT[:, h % 2, d, :], bank[d][:, 0:NODES]), eT_ready)
                turned_heads[0] += 1

            turned_heads = [0]
            for h in range(HEADS):
                turned_weights(h)
            step(dve.tensor_scalar(den[:, :, :], den[:, :, :], 1e-30, None, ALU.max))
            step(dve.reciprocal(den[:, :, :], den[:, :, :]))
            def shifted(dst, layer, shift):
                for t in range(NT):
                    step(dve.tensor_tensor(dst[:, t, :], dst[:, t, :], row(layer, shift), ALU.add))

            shifted(x, 0, "L0_gnn_beta")
            dve.wait_ge(y_g, HEADS)

            def per_head(ap, t):
                return ap[:, t, :].unsqueeze(2).to_broadcast([P, HEADS, HD])

            def heads(ap):
                return ap.rearrange("p (h d) -> p h d", h=HEADS)

            for t in range(NT):
                step(dve.tensor_tensor(heads(y[:, t, :]), heads(bank[5 + t][:, :]), per_head(den, t), ALU.mult))
                step(dve.tensor_scalar(vn[:, t, :], y[:, t, :], 0.0, None, ALU.min), elu_in)
            for t in range(NT):
                dve.wait_ge(elu_ex, t + 1)
                step(dve.scalar_tensor_tensor(y[:, t, :], y[:, t, :], 0.0, vn[:, t, :], ALU.max, ALU.add))
                step(dve.scalar_tensor_tensor(y[:, t, :], y[:, t, :], -1.0, xn[:, t, :], ALU.add, ALU.add))

            def affine(src, layer, gain, add=None, shift=None, signal=None):
                for t in range(NT):
                    step(dve.bn_stats(stats[:, :], src[:, t, :]))
                    step(dve.bn_aggr(mv[:, t, :], stats[:, :]))
                norms[0] += 1
                step(dve.tensor_scalar(varp[:, :], mv[:, :, 1], EPS, None, ALU.add), var_ready)
                for t in range(NT):
                    step(dve.scalar_tensor_tensor(src[:, t, :], src[:, t, :], mv[:, t, 0:1], row(layer, gain), ALU.subtract, ALU.mult))
                dve.wait_ge(rstd_ready, norms[0])
                for t in range(NT):
                    dst, other = (src[:, t, :], row(layer, shift)) if add is None else (add[:, t, :], add[:, t, :])
                    step(dve.scalar_tensor_tensor(dst, src[:, t, :], rstd[:, t:t + 1], other, ALU.mult, ALU.add), signal)

            affine(y, 0, "L0_gnn_gamma", add=x)
            step(dve.tensor_copy(stats[:, 0:1], stats[:, 1:2]), row_used)

            def across(ap):
                return ap.unsqueeze(2).to_broadcast([P, NT, 8])

            def top2():
                v = small[:, 0, :]
                others = sm(0).unsqueeze(2).to_broadcast([P, NT, 8, 8])
                own = sm(0).unsqueeze(3).to_broadcast([P, NT, 8, 8])
                g = cmp8[:, 0, :, :].rearrange("p (t e) f -> p t e f", t=NT)
                q = cmp8[:, 1, :, :].rearrange("p (t e) f -> p t e f", t=NT)
                step(dve.tensor_tensor(g, others, own, ALU.is_gt))
                step(dve.tensor_tensor(q, others, own, ALU.is_equal))
                step(dve.tensor_tensor(q, q, low8[:, :, :].unsqueeze(1).to_broadcast([P, NT, 8, 8]), ALU.mult))
                step(dve.tensor_tensor(cmp8[:, 0, :, :], cmp8[:, 0, :, :], cmp8[:, 1, :, :], ALU.add))
                step(dve.tensor_reduce(small[:, 2, :], cmp8[:, 0, :, :], AX.X, ALU.add))
                step(dve.tensor_scalar(small[:, 2, :], small[:, 2, :], 2.0, None, ALU.is_lt))

            def logits_in(n, layer):
                dve.wait_ge(route_g, n)
                step(dve.tensor_tensor(sm(0), bank[7][:, 0:NT * 8].rearrange("p (t e) -> p t e", t=NT),
                                       br[:, layer, :].unsqueeze(1).to_broadcast([P, NT, 8]), ALU.add))
                step(dve.tensor_reduce(small1[:, 0, :], sm(0), AX.X, ALU.max))
                step(dve.tensor_tensor(sm(1), sm(0), across(small1[:, 0, :]), ALU.subtract), route_d)

            def normalized(dst, src, eps):
                step(dve.tensor_reduce(small1[:, 1, :], src, AX.X, ALU.add))
                if eps:
                    step(dve.tensor_scalar(small1[:, 1, :], small1[:, 1, :], eps, None, ALU.add))
                step(dve.reciprocal(small1[:, 1, :], small1[:, 1, :]))
                step(dve.tensor_tensor(dst, src, across(small1[:, 1, :]), ALU.mult))

            def places(n, mask):
                step(dve.scalar_tensor_tensor(sm(5), sm(4), 1.0, mask, ALU.add, ALU.mult))
                step(dve.tensor_scalar(sm(5), sm(5), -1.0, None, ALU.add))
                step(dve.tensor_copy(stats[:, 0:1], stats[:, 1:2]), coef_r)
                dve.wait_ge(coefT_g, n)
                step(dve.tensor_copy(coefT[:, :], bank[7][0:8, 0:NODES]), coefT_r)

            def gather_nodes(r):
                s, w = r.sem, r.width
                for g in range(r.groups):
                    for e in range(g * 512 // w, (g + 1) * 512 // w):
                        for t in range(NT):
                            last = dve.tensor_scalar(r.place[:, t, e * w:(e + 1) * w], iota[:, 0:w], small[:, 5, t * 8 + e:t * 8 + e + 1], None, ALU.is_equal)
                    last.then_inc(s["place_ready"], 1)
                    if g == 0:
                        for t in range(NT):
                            dve.wait_ge(s["split_high"], t + 1)
                            dve.tensor_tensor(xsplit[:, 1, t, :], xn[:, t, :], xsplit[:, 0, t, :], ALU.subtract).then_inc(s["split_low"], 1)

            def take_gathered(r, g):
                s = r.sem
                for k in (1, 3):
                    dve.wait_ge(s["gather_product"], 4 * g + k + 1)
                    dve.tensor_copy(r.xgT[k][:, g * 512:g * 512 + 512], bank[4 * (g % 2) + k][:, :]).then_inc(s["gathered_dve"], 1)

            def experts2():
                s = routed2.sem
                for e in range(EXPERTS):
                    for t in range(NT):
                        last = dve.tensor_scalar(cplace[:, t, e * SE:(e + 1) * SE], iota[:, 0:SE], small[:, 5, t * 8 + e:t * 8 + e + 1],
                                                 coef[:, t, e:e + 1], ALU.is_equal, ALU.mult)
                    last.then_inc(s["cplace_ready"], 1)
                for g in range(routed2.groups):
                    take_gathered(routed2, g)
                for e in range(1, EXPERTS, 2):
                    dve.wait_ge(s["cplace_turned"], e + 1)
                    dve.tensor_copy(cplaceT[:, e, :], bank[e % 4][:, 0:NODES]).then_inc(s["cplaceT_dve"], 1)
                dve.wait_ge(s["cplaceT_act"], 4)
                dve.wait_ge(s["cplaceT_dve"], 4)
                for e in range(EXPERTS):
                    if e >= 2:
                        dve.wait_ge(s["combined"], e - 1)
                    dve.tensor_copy(cp2[:, e % 2, :], cplaceT[:, e, :]).then_inc(s["cplace_copied"], 1)
                dve.wait_ge(s["combined"], EXPERTS)
                for t in range(NT):
                    step(dve.tensor_tensor(x[:, t, :], x[:, t, :], bank[5 + t][:, :], ALU.add))

            norm(x, xn, nodes_ready)
            turn(xT)
            logits_in(1, 0)
            top2()
            step(dve.tensor_copy(stats[:, 0:1], stats[:, 1:2]), mask_r)
            dve.wait_ge(route_a, 1)
            step(dve.tensor_tensor(sm(1), sm(1), sm(2), ALU.mult))
            normalized(coef[:, :, :], sm(1), 0.0)
            dve.wait_ge(pos_g, 1)
            step(dve.tensor_copy(small[:, 4, :], bank[7][:, 32:32 + NT * 8]))
            step(dve.tensor_copy(crowd[:, :], bank[7][:, 64:72]))
            places(1, sm(2))

            for t in range(NT):
                dve.wait_ge(b2_g, t + 1)
                dve.tensor_tensor(x[:, t, :], x[:, t, :], bank[4 + t][:, :], ALU.add).then_inc(expert_added, 1)
            gather_nodes(routed0)
            for g in range(routed0.groups):
                take_gathered(routed0, g)
            with dve.Fori(0, EXPERTS) as e:
                def expert0(width):
                    s = routed0.sem
                    w = min(width, 2 * SE)
                    dve.wait_ge(expert_added, e * NT + NT)
                    for t in range(NT):
                        last = dve.tensor_scalar(cpl[:, t, 0:w], iota[:, 0:w], sm(5)[:, t, bass.ds(e, 1)], coef[:, t, bass.ds(e, 1)],
                                                 ALU.is_equal, ALU.mult)
                    last.then_inc(s["cplace_ready"], 1)
                    dve.wait_ge(s["cplace_turned"], e + 1)
                    if width == 2 * SE:
                        dve.tensor_copy(cp2[:, 1, :], bank[3][:, 0:NODES])
                    dve.tensor_copy(cp2[:, 0, :], bank[7][:, 0:NODES]).then_inc(s["cplace_copied"], 1)
                    for j in range(JT0):
                        dve.wait_ge(silu_r, e * JT0 + j + 1)
                        up = bank[2 + j % 2][:, 0:NODES] if width == NODES else bank[j % 2][:, width:2 * width]
                        dve.scalar_tensor_tensor(act2[:, j % 2, 0:width], up, b1e0[:, bass.ds(e, 1), JT0 + j],
                                                 silu2[:, j % 2, 0:width], ALU.add, ALU.mult).then_inc(hid_r, 1)
                    dve.wait_ge(s["combined"], e + 1)
                    for t in range(NT):
                        if width == NODES:
                            ins = dve.scalar_tensor_tensor(x[:, t, :], bank[4 + t][:, :], coef[:, t, bass.ds(e, 1)], x[:, t, :], ALU.mult, ALU.add)
                        else:
                            ins = dve.tensor_tensor(x[:, t, :], x[:, t, :], bank[4 + t][:, :], ALU.add)
                        ins.then_inc(expert_added, 1)

                chosen_by = dve.value_load(crowd[0:1, bass.ds(e, 1)], min_val=0, max_val=NODES)
                with dve.If(chosen_by <= SE):
                    expert0(SE)
                with dve.Else():
                    with dve.If(chosen_by <= 2 * SE):
                        expert0(2 * SE)
                    with dve.Else():
                        expert0(NODES)
            dve.wait_ge(expert_added, NT + EXPERTS * NT)
            step(dve.tensor_copy(stats[:, 0:1], stats[:, 1:2]), added)

            norm(x, xn, nodes_ready)
            turn(xT)
            dve.wait_ge(rows_loaded, rows_before[1])
            tables(12, 6, tabs1, 1, lambda c: row(1, "L1_gnn_b1"))

            def message_onehots(s, at):
                dve.tensor_scalar(em[:, s, :], iota[:, :], dstf[:, bass.ds(at, 1)], None, ALU.is_equal).then_inc(em_ready, 1)

            def mish_out(n, at):
                kind, b, s = mish_tile(n) if n < MISH else ("u", 0, n - MISH)
                width = 512 if n < MISH else NODES
                dst = {"z": hT[:, b % 2, s, :], "m": mz[:, n % 4, :], "u": hidT[:, s, :]}[kind]
                dve.wait_ge(mish_zq, at + n + 1)
                dve.scalar_tensor_tensor(mr[:, n % 4, 0:width], mr[:, n % 4, 0:width], -2.0, mt[:, n % 4, 0:width], ALU.mult, ALU.subtract).then_inc(mish_fix, 1)
                dve.wait_ge(mish_fix, at + n + 1)
                dve.scalar_tensor_tensor(dst, mr[:, n % 4, 0:width], 2.0, mz[:, n % 4, 0:width], ALU.add, ALU.mult).then_inc(mish_r, 1)

            def mish_square(n, at, width=512):
                dve.wait_ge(mish_ex, at + n + 1)
                dve.tensor_scalar(mt[:, n % 4, 0:width], mt[:, n % 4, 0:width], 1e9, None, ALU.min).then_inc(mish_min, 1)
                dve.wait_ge(mish_min, at + n + 1)
                dve.scalar_tensor_tensor(mt[:, n % 4, 0:width], mt[:, n % 4, 0:width], 2.0, mt[:, n % 4, 0:width], ALU.add, ALU.mult).then_inc(mish_sq, 1)

            def message_low(n, at, at4):
                kind, b, s = mish_tile(n)
                if kind == "m":
                    dve.wait_ge(msg_hi, at4 + (4 * b + s + 1))
                    dve.tensor_tensor(ml[:, s, :], mz[:, n % 4, :], mh[:, s, :], ALU.subtract).then_inc(msg_lo, 1)

            def mish_input(n, at, at4=0):
                kind, b, s = mish_tile(n) if n < MISH else ("u", 0, n - MISH)
                if kind == "z":
                    return
                dve.wait_ge(mish_g, at + n + 1)
                if n >= 4:
                    dve.wait_ge(mish_r, at + n - 3)
                    kind_, b_, s_ = mish_tile(n - 4) if n < MISH else ("u", 0, 0)
                    if kind_ == "m":
                        dve.wait_ge(msg_lo, at4 + (4 * b_ + s_ + 1))
                if kind == "m":
                    ins = dve.tensor_tensor(mz[:, n % 4, :], bank[n % 4][:, :], row(1, "L1_gnn_b2"), ALU.add)
                else:
                    ins = dve.tensor_scalar(mz[:, n % 4, 0:NODES], bank[n % 4][:, 0:NODES], b3c[:, s:s + 1], None, ALU.add)
                ins.then_inc(m_in, 1)

            def mish_step(n, at, at4, first=0):
                if first <= n - 1 < MISH:
                    mish_square(n - 1, at)
                if n - 4 >= first:
                    message_low(n - 4, at, at4)
                if n < MISH:
                    mish_input(n, at, at4)
                if first <= n - 3 < MISH:
                    mish_out(n - 3, at)

            def mish_drain():
                mish_square(MISH - 5, 0)
                message_low(MISH - 8, 0, 0)
                for n in (MISH - 7, MISH - 6, MISH - 5):
                    mish_out(n, 0)
                    message_low(n, 0, 0)

            def attr_low(q, i2):
                dve.wait_ge(at_hi, i2 + (q + 1))
                if q:
                    low, high, raw = attrs[64:P, (q - 1) % 2, :], attrs[64:P, (q - 1) % 2, :], attr[64:P, :]
                else:
                    low, high, raw = w1lo[:, :], w1hi[0:64, :], attr[0:64, :]
                dve.tensor_tensor(low, raw, high, ALU.subtract).then_inc(at_lo, 1)

            def block1(b, i2, at):
                if b == NB - 1:
                    mish_drain()
                for q in range(8 if b < NB - 1 else 4):
                    mish_step(4 + 8 * b + q, at, i2 * 4, MISH - 4 if b == NB - 1 else 0)
                    if q == 2 and b < NB - 2:
                        onehots(b % 2, (i2 + (NB + b + 3)) * 32)
                    if q == 3 and b < NB - 2:
                        attr_low(b + 3, i2)
                    kind, _, s = mish_tile(4 + 8 * b + q)
                    if kind == "m":
                        message_onehots(s, (i2 + b) * SUB + s)

            for q in range(3):
                attr_low(q, 0)
            onehots(0, (NB + 1) * 32)
            onehots(1, (NB + 2) * 32)
            for n in range(4):
                mish_step(n, 0, 0)
            block1(0, 0, 0)
            with dve.Fori(0, 4) as i:
                for u in range(2):
                    block1(1 + u, i * 2, i * 16)
            for b in (NB - 3, NB - 2, NB - 1):
                block1(b, 0, 0)
            for n in range(MISH, MISH + 4):
                mish_step(n, 0, 0, MISH - 4)
            for t in range(NT):
                dve.wait_ge(agg_g, NT)
                step(dve.tensor_copy(y[:, t, :], bank[4 + t][:, :]), nodes_ready)
            turn(yT)
            for m in range(KT + 3):
                if m < KT:
                    mish_input(MISH + m, 0)
                if 1 <= m <= KT:
                    mish_square(MISH + m - 1, 0, NODES)
                if m >= 3:
                    mish_out(MISH + m - 3, 0)
            shifted(x, 1, "L1_gnn_beta")
            shifted(xn, 1, "L1_gnn_b4")
            for t in range(NT):
                dve.wait_ge(node_g, t + 1)
                step(dve.tensor_tensor(y[:, t, :], bank[4 + t][:, :], xn[:, t, :], ALU.add))
            affine(y, 1, "L1_gnn_gamma", add=x)
            step(dve.tensor_copy(stats[:, 0:1], stats[:, 1:2]), row_used)

            def quant(j, u, i):
                raw = qraw[:, u, :, :].rearrange("p c (g n) -> p (c g) n", g=4)
                va = qa[:, u, :].rearrange("p (g n) -> p g n", g=12)
                vb = qb.rearrange("p (g n) -> p g n", g=12)
                at = 0 if i is None else i
                base = (at * 2 + j) * 2

                def link(ins, k):
                    ins.then_inc(quant_s, 1)
                    dve.wait_ge(quant_s, base + k)

                if j >= 1:
                    dve.wait_ge(quant_r, at * 2 + j)
                if j >= 2:
                    dve.wait_ge(q_turned, at * 6 + 3 * (j - 1))
                dve.wait_ge(sums_r, at * 24 + 12 * (j + 1))
                link(dve.tensor_scalar(qs[:, :, 0], qsum[:, u, :], 1.0 / 128, EPS, ALU.mult, ALU.add), 1)
                dve.tensor_scalar(qs[:, :, 1], qs[:, :, 0], 0.5, None, ALU.mult)
                link(dve.tensor_scalar(qs[:, :, 2], qs[:, :, 0], -0.5, None, ALU.mult), 2)
                for g in range(12):
                    dve.tensor_scalar(va[:, g, :], raw[:, g, :], qs[:, g, 1:2], qs[:, g, 0:1], ALU.is_gt, ALU.mult)
                    last = dve.tensor_scalar(vb[:, g, :], raw[:, g, :], qs[:, g, 2:3], qs[:, g, 0:1], ALU.is_lt, ALU.mult)
                last.then_inc(quant_c, 1)

            norm(x, xn, nodes_ready)
            quant(0, 0, None)
            turn(xT)

            def turn_quant(j, u, at):
                dve.wait_ge(q_turned, at * 3 + 3 * j + 3)
                dve.tensor_copy(qT[:, u, 2, :], bank[2][:, :]).then_inc(qT_v, 1)

            def hidden1(j, u, at):
                dve.wait_ge(silu_r, at + UP1 + j + 1)
                dve.tensor_tensor(act2[:, u, :], bank[4][:, 0:NODES], silu2[:, u, :], ALU.mult).then_inc(hid_r, 1)

            quant(1, 1, None)
            turn_quant(0, 0, 0)
            quant(2, 0, None)
            hidden1(0, 0, 0)
            turn_quant(1, 1, 0)
            with dve.Fori(0, 4) as i:
                for j in (1, 2):
                    quant(j + 2, j % 2, i)
                    hidden1(j, j % 2, i * 2)
                    turn_quant(j + 1, (j + 1) % 2, i * 2)
            hidden1(9, 1, 0)
            turn_quant(10, 0, 0)
            hidden1(10, 0, 0)
            dve.wait_ge(down_g, UP2)
            for t in range(NT):
                step(dve.tensor_tensor(x[:, t, :], x[:, t, :], bank[5 + t][:, :], ALU.add), added)

            norm(x, xn, nodes_ready)
            turn(xT)
            dve.wait_ge(rows_loaded, rows_before[2])

            def score_parts(t):
                for k, name in enumerate(("L2_gnn_at", "L2_gnn_as")):
                    step(dve.tensor_tensor(prod, vn[:, t, :], row(2, name), ALU.mult))
                    step(dve.tensor_reduce(pq[:, k, t, :], heads(prod), AX.X, ALU.add))

            values(NT, 2, "L2_gnn_Wb", score_parts)
            step(dve.tensor_tensor(pq[:, 1, :, :], pq[:, 1, :, :], ab[:, :].unsqueeze(1).to_broadcast([P, NT, HEADS]), ALU.add), pq_r)
            step(dve.tensor_copy(stats[:, 0:1], stats[:, 1:2]), row_used)
            for t in range(NT):
                step(dve.tensor_scalar(negm[:, t, :], count[:, t, :], 0.0, -1e30, ALU.is_equal, ALU.mult))
            dve.wait_ge(pqT_g, 1)
            step(dve.tensor_copy(qT2, bank[3][0:8, 0:NODES]), pqT_r)

            def score(h, t):
                dve.wait_ge(srow_g, h + 1)
                step(dve.scalar_tensor_tensor(srow[:, t, :], bank[3 + h % 2][:, 0:NODES], pq[:, 0, t, h:h + 1], negm[:, t, :], ALU.add, ALU.add))
                step(dve.scalar_tensor_tensor(srow[:, t, :], srow[:, t, :], 0.2, srow[:, t, :], ALU.mult, ALU.max))
                step(dve.tensor_reduce(small1[:, 0, 0:1], srow[:, t, :], AX.X, ALU.max))
                step(dve.tensor_scalar(mneg[:, t, h:h + 1], small1[:, 0, 0:1], -1.0, None, ALU.mult), score_r)

            def weigh(h, t):
                dve.wait_ge(exp2_r, h * NT + t + 1)
                if h >= 2:
                    dve.wait_ge(e_turned, NT * (HEADS + h - 1))
                step(dve.tensor_tensor_reduce(eh[:, h % 2, t, :], srow[:, t, :], count[:, t, :], 1.0, 0.0,
                                              ALU.mult, ALU.add, den[:, t, h:h + 1]), weighed)

            for h in range(HEADS):
                for t in range(NT):
                    score(h, t)
                    if t:
                        weigh(h, t - 1)
                weigh(h, NT - 1)
            step(dve.tensor_scalar(den[:, :, :], den[:, :, :], 1e-30, None, ALU.max))
            step(dve.reciprocal(den[:, :, :], den[:, :, :]))
            dve.wait_ge(y_g, 2 * HEADS)
            for t in range(NT):
                step(dve.tensor_tensor(heads(y[:, t, :]), heads(bank[5 + t][:, :]), per_head(den, t), ALU.mult))
                step(dve.tensor_tensor(x[:, t, :], x[:, t, :], y[:, t, :], ALU.add))

            norm(x, xn, nodes_ready)
            turn(xT)
            logits_in(2, 1)
            top2()
            step(dve.tensor_copy(stats[:, 0:1], stats[:, 1:2]), mask_r)
            dve.wait_ge(route_a, 2)
            normalized(sm(1), sm(1), 0.0)
            step(dve.tensor_tensor(sm(3), sm(1), sm(2), ALU.mult))
            normalized(sm(3), sm(3), 1e-9)
            dve.wait_ge(pos_g, 2)
            step(dve.tensor_copy(small[:, 4, :], bank[7][:, 32:32 + NT * 8]))
            step(dve.scalar_tensor_tensor(small[:, 6, :], small[:, 4, :], float(CAP), small[:, 2, :], ALU.is_lt, ALU.mult))
            step(dve.tensor_tensor(sm(3), sm(3), sm(6), ALU.mult))
            normalized(coef[:, :, :], sm(3), 1e-9)
            places(2, sm(6))
            gather_nodes(routed2)
            experts2()
            step(dve.tensor_copy(stats[:, 0:1], stats[:, 1:2]), added)

            norm(x, xn, nodes_ready)
            turn(xT)
            step(dve.tensor_copy(wdeg[:, :, 0], ewc[:, :]))
            step(dve.tensor_tensor(wdeg[:, :, 1], ewc[:, :], wdeg[:, :, 0], ALU.subtract), wdeg_r)
            dve.wait_ge(edges_loaded, 128)
            dve.wait_ge(rows_loaded, rows_before[3])
            for n in range(4 * NT):
                dve.wait_ge(rel_g, n + 1)
                step(dve.tensor_tensor(stage[:, n, :], bank[n % 4][:, :], brel[:, n // NT, :], ALU.add), rel_r)
            for t in range(NT):
                dve.wait_ge(node_g, NT + t + 1)
                step(dve.tensor_tensor(y[:, t, :], bank[4 + t][:, :], row(3, "L3_gnn_b_self"), ALU.add))
                step(dve.tensor_tensor(y[:, t, :], y[:, t, :], xn[:, t, :], ALU.add))

            def scaled_low(n, at):
                dve.wait_ge(msg_hi, at + (4 * NB + n + 1))
                dve.scalar_tensor_tensor(ml[:, n % 4, :], gather[:, n % RING, :], ewc[:, bass.ds(at + n, 1)], mh[:, n % 4, :],
                                         ALU.mult, ALU.subtract).then_inc(msg_lo, 1)

            def destinations(n, at):
                if n >= 4:
                    dve.wait_ge(m_used, at + n - 3)
                dve.tensor_scalar(em[:, n % 4, :], iota[:, :], dstf[:, bass.ds(at + n, 1)], None, ALU.is_equal).then_inc(em_ready, 1)

            for n in range(RING):
                destinations(n, 0)
                scaled_low(n, 0)
            with dve.Fori(0, 4) as i:
                for c in range(RING, 2 * RING):
                    destinations(c, i * RING)
                    scaled_low(c, i * RING)
            for n in range(5 * RING, 6 * RING):
                destinations(n, 0)
                scaled_low(n, 0)
            dve.wait_ge(agg_g, 2 * NT + 1)
            step(dve.tensor_reduce(small1[:, 0, :], bank[3][:, 0:2 * NT].rearrange("p (t c) -> p t c", c=2), AX.X, ALU.add))
            step(dve.tensor_scalar(small1[:, 0, :], small1[:, 0, :], 1.0, None, ALU.max))
            step(dve.reciprocal(small1[:, 0, :], small1[:, 0, :]))
            for t in range(NT):
                step(dve.scalar_tensor_tensor(y[:, t, :], bank[t][:, :], small1[:, 0, t:t + 1], y[:, t, :], ALU.mult, ALU.add))
            affine(y, 3, "L3_gnn_ln1_g", shift="L3_gnn_ln1_b", signal=nodes_ready)
            turn(yT)
            shifted(y, 3, "L3_gnn_b_ffn2")
            shifted(x, 3, "L3_gnn_ln2_b")
            for t in range(NT):
                dve.wait_ge(node_g, 2 * NT + 8 + t + 1)
                step(dve.tensor_tensor(y[:, t, :], y[:, t, :], bank[4 + t][:, :], ALU.add))
            affine(y, 3, "L3_gnn_ln2_g", add=x)

            norm(x, xn, nodes_ready)
            turn(xT)
            dve.wait_ge(route_g, 3)
            step(dve.tensor_scalar(sink[:, 0, :], bank[7][0:8, 0:NODES], 1e-10, None, ALU.max), sk_d)
            turned_gates = bank[0][:, 0:NT * 8].rearrange("p (t e) -> p t e", t=NT)

            def sinkhorn(v, i):
                at_a, at_p = i * 8 + 4 * v, i * 4 + 2 * v
                dve.wait_ge(sk_a, at_a + 1)
                step(dve.tensor_reduce(sinks[:, 3:4], sink[:, 0, :], AX.X, ALU.max), sk_d)
                step(dve.tensor_scalar(sinks[:, 0:1], sinks[:, 3:4], -1.0, None, ALU.mult), sk_d)
                dve.wait_ge(sk_a, at_a + 3)
                step(dve.tensor_scalar(sink[:, 0, :], sink[:, 0, :], sinks[:, 3:4], sinks[:, 2:3], ALU.subtract, ALU.subtract), sk_d)
                dve.wait_ge(sk_p, at_p + 1)
                step(dve.tensor_reduce(small1[:, 2, :], turned_gates, AX.X, ALU.max), sk_d)
                step(dve.tensor_tensor(sinka[:, 1, :, :], turned_gates, across(small1[:, 2, :]), ALU.subtract), sk_d)
                dve.wait_ge(sk_a, at_a + 4)
                step(dve.tensor_reduce(small1[:, 0, :], sinka[:, 2, :, :], AX.X, ALU.add), sk_d)
                dve.wait_ge(sk_a, at_a + 5)
                step(dve.tensor_tensor(sinka[:, 0, :, :], sinka[:, 1, :, :], across(small1[:, 1, :]), ALU.subtract), sk_d)
                dve.wait_ge(sk_p, at_p + 2)
                step(dve.tensor_copy(sink[:, 0, :], bank[1][0:8, 0:NODES]), sk_d)

            with dve.Fori(0, SINKHORN // 2) as i:
                step.enter(i, {sk_d: 16})
                for v in range(2):
                    sinkhorn(v, i)
            step.leave(SINKHORN // 2)
            dve.wait_ge(sk_a, 4 * SINKHORN + 2)
            for k in range(TOP // 8):
                src = sink[:, 0 if k == 0 else 1 + (k - 1) % 2, :]
                step(dve.max(sinks[:, 0:8], src))
                step(dve.match_replace(sink[:, 1 + k % 2, :], sinks[:, 0:8], src, -1.0))
            step(dve.tensor_scalar(sink[:, 3, :], sink[:, 1 + (TOP // 8 - 1) % 2, :], -1.0, None, ALU.is_equal))
            step(dve.scalar_tensor_tensor(sink[:, 4, :], sink[:, 0, :], 0.5, sink[:, 3, :], ALU.is_gt, ALU.mult), mask_r)
            dve.wait_ge(sk_p, 2 * SINKHORN + 1)
            chosen = bank[1][:, 0:2 * NT * 8].rearrange("p (c t e) -> p c t e", c=2, t=NT)
            step(dve.tensor_reduce(small1[:, 0, :], chosen[:, 0, :, :], AX.X, ALU.add))
            step(dve.tensor_scalar(small1[:, 0, :], small1[:, 0, :], 1.0, None, ALU.add))
            step(dve.reciprocal(small1[:, 0, :], small1[:, 0, :]))
            step(dve.tensor_tensor(coef[:, :, :], chosen[:, 1, :, :], across(small1[:, 0, :]), ALU.mult), coef_r)
            dve.wait_ge(y3_out, NT * EXPERTS)
            for t in range(NT - 1):
                for e in range(EXPERTS):
                    y3e = y3[e // 6][:, e % 6, t * 512:t * 512 + 512]
                    step(dve.scalar_tensor_tensor(x[:, t, :], y3e, coef[:, t, e:e + 1], x[:, t, :], ALU.mult, ALU.add), added)
            dve.wait_ge(expert3_g, NT * EXPERTS + 1)
            step(dve.tensor_tensor(x[:, NT - 1, :], x[:, NT - 1, :], bank[2][:, :], ALU.add), added)

        @block.tensor
        def _(pe):
            turns = [0]

            def turn(src):
                pe.wait_ge(nodes_ready, NT * (turns[0] + 1))
                for k in range(KT):
                    for t in range(NT):
                        last = pe.transpose(bank[k][:, t * P:(t + 1) * P], src[:, t, k * P:(k + 1) * P], ident[:, :])
                    last.then_inc(turned, 1)
                turns[0] += 1
                pe.wait_ge(xT_a, 2 * turns[0])
                pe.wait_ge(xT_v, 2 * turns[0])

            def arrived(*key):
                s, value = W[key]
                pe.wait_ge(arrive[s], value)

            def weight(name, k):
                return wslot(W[(*name, k // 2)][0], 2)[:, k % 2, :]

            def product(out, lhs, rhs, n, signal):
                for k in range(n):
                    last = pe.matmul(out, lhs(k), rhs(k), start=(k == 0), stop=(k == n - 1))
                last.then_inc(signal, 1)

            def tile(ap, k, t):
                return ap[:, k, t * P:(t + 1) * P]

            def values(name, signal):
                arrived(*name, 0)
                arrived(*name, 1)
                for t in range(NT):
                    product(bank[4 + t][:, :], lambda k: tile(xT, k, t), lambda k: weight(name, k), KT, signal)

            def router(which):
                for t in range(NT):
                    for k in range(KT):
                        last = pe.matmul(bank[7][:, t * 8:t * 8 + 8], tile(xT, k, t), gatew[:, which, k, :],
                                         start=(k == 0), stop=(k == KT - 1))
                last.then_inc(route_g, 1)

            def positions(n):
                pe.wait_ge(mask_r, n)
                for t in range(NT):
                    for k in range(t + 1):
                        pe.matmul(bank[7][:, 32 + t * 8:40 + t * 8], (upper if k == t else ones)[:, :], sm(2)[:, k, :],
                                  start=(k == 0), stop=(k == t))
                for k in range(NT):
                    last = pe.matmul(bank[7][:, 64:72], ones[:, :], sm(2)[:, k, :], start=(k == 0), stop=(k == NT - 1))
                last.then_inc(pos_g, 1)

            def turn_coef(n):
                pe.wait_ge(coef_r, n)
                for t in range(NT):
                    last = pe.transpose(bank[7][0:8, t * P:(t + 1) * P], coef[:, t, :], ident[:, :])
                last.then_inc(coefT_g, 1)
                pe.wait_ge(coefT_r, n)

            def gather_nodes(r):
                s = r.sem
                pe.wait_ge(s["split_high"], NT)
                pe.wait_ge(s["split_low"], NT)
                for g in range(r.groups):
                    pe.wait_ge(s["place_ready"], g + 1)
                    if g >= 2:
                        pe.wait_ge(s["gathered_act"], 2 * (g - 1))
                        pe.wait_ge(s["gathered_dve"], 2 * (g - 1))
                    for k in range(KT):
                        for t in range(NT):
                            for p in range(2):
                                last = pe.matmul(bank[4 * (g % 2) + k][:, :], xsplit[:, p, t, k * P:(k + 1) * P], r.place[:, t, g * 512:g * 512 + 512],
                                                 start=(t, p) == (0, 0), stop=(t, p) == (NT - 1, 1))
                        last.then_inc(s["gather_product"], 1)

            def experts2():
                s = routed2.sem
                pe.wait_ge(s["gathered_act"], 2)
                pe.wait_ge(s["gathered_dve"], 2)
                for e in range(EXPERTS):
                    pe.wait_ge(s["cplace_ready"], e + 1)
                    if e >= 4:
                        pe.wait_ge(s["cplaceT_dve" if e % 2 else "cplaceT_act"], e // 2 - 1)
                    for t in range(NT):
                        last = pe.transpose(bank[e % 4][:, t * P:(t + 1) * P], cplace[:, t, e * SE:(e + 1) * SE], ident[:, :])
                    last.then_inc(s["cplace_turned"], 1)
                pe.wait_ge(s["gathered_act"], 4)
                pe.wait_ge(s["gathered_dve"], 4)
                for t in range(NT):
                    pe.matmul(bank[5 + t][:, :], coefT[:, t * P:(t + 1) * P], b2e[:, 1, :], start=True, stop=False, skip_group_check=True)
                pe.wait_ge(s["cplaceT_act"], 4)
                pe.wait_ge(s["cplaceT_dve"], 4)

                def loaded(c, i2, part):
                    slot = f2[2 * (c % 2) + part]
                    pe.wait_ge(arrive[slot], i2 * 8 + (16 * (c // 2 + 1) + f2_base[slot]))

                def up(c, i2, j):
                    if j == 0:
                        loaded(c, i2, 0)
                    for k in range(KT):
                        last = pe.matmul(bank[j % 2][:, 0:SE], wslot(f2[2 * (c % 2)], KT)[:, k, j * P:(j + 1) * P],
                                         routed2.xgT[k][:, bass.ds((i2 + c) * SE, SE)], start=(k == 0), stop=(k == KT - 1))
                    last.then_inc(up_g, 1)

                def down(c, i2, j):
                    if j == 0:
                        loaded(c, i2, 1)
                    pe.wait_ge(hid_r, i2 * JT2 + (UP2 + c * JT2 + j + 1))
                    pe.matmul(bank[3 + c % 2][:, :], act2[:, j % 2, 0:SE], wslot(f2[2 * (c % 2) + 1], 2)[:, j, :], start=(j == 0), stop=(j == JT2 - 1),
                              skip_group_check=True).then_inc(down_g, 1)

                def combine(c, i2):
                    pe.wait_ge(s["cplace_copied"], i2 + c + 1)
                    pe.wait_ge(s["expert_out"], i2 + c + 1)
                    for t in range(NT):
                        last = pe.matmul(bank[5 + t][:, :], cp2[:, c % 2, t * P:(t + 1) * P], tmp[:, c % 2, :],
                                         start=False, stop=(c == EXPERTS - 1), skip_group_check=True)
                    last.then_inc(s["combined"], 1)

                def body(c, i2):
                    for j in range(JT2):
                        up(c, i2, j)
                        if j:
                            down(c, i2, j - 1)
                        if j == 1 and c:
                            combine(c - 1, i2)
                    down(c, i2, JT2 - 1)

                for c in range(3):
                    body(c, 0)
                with pe.Fori(0, 2) as i:
                    body(3, i * 2)
                    body(4, i * 2)
                body(7, 0)
                combine(7, 0)

            pe.wait_ge(consts_ready, 1)
            turn(xn)
            values(("wv",), value_g)

            def ww_slot(k):
                return late_ww[k] if k in late_ww else wring[:, W["ww", k][0], :]

            for g in range(12):
                which, r = divmod(g, 6)
                t, c = divmod(r, 2)
                if r == 0:
                    for k in range(4 * which, 4 * which + 4):
                        if k in late_ww:
                            pe.wait_ge(x_loaded, 16 * (1 + len(late_ww)))
                        else:
                            arrived("ww", k)
                if g >= 4:
                    pe.wait_ge(tab_sum, g - 3)
                product(bank[g % 4][:, :], lambda k: tile(xT, k, t),
                        lambda k: ww_slot(4 * which + k)[:, c * 512:c * 512 + 512], KT, table_g)
            pe.wait_ge(tab_lo, 12)
            pe.wait_ge(tab_hi, 12)
            pe.wait_ge(small_loaded, 16 * N_SMALL)
            pe.wait_ge(v_ready, NT)

            pe.wait_ge(wa_lo, HEADS + 1)

            def z0(n, par, at):
                h = n % 8
                for w in range(2):
                    for t in range(NT):
                        for p in range(2):
                            last = pe.matmul(bank[n % 4][:, :], tabs0[:, w, p, t, h * P:(h + 1) * P], onehot[:, par, w, t, :],
                                             start=(w, t, p) == (0, 0, 0), stop=(w, t, p) == (1, NT - 1, 1))
                last.then_inc(z_g, 1)

            def logit_parts(n, par, at):
                h = n % 8
                pe.wait_ge(leaky_lo, at + n + 1)
                for p in range(2):
                    last = pe.matmul(bank[4][0:2 * HEADS, :], wsel[:, h, :], lsplit[:, n % 2, p, :],
                                     start=(h, p) == (0, 0), stop=(h, p) == (HEADS - 1, 1))
                last.then_inc(dots_g, 1)

            def edge_logits(b, at):
                pe.wait_ge(dots_r, at + b + 1)
                for s in range(SUB):
                    last = pe.matmul(bank[4][:, s * 8:s * 8 + 8], dots[:, s * P:(s + 1) * P], pairsum[:, :], start=True, stop=True)
                last.then_inc(logit_g, 1)

            def count0(b, at):
                pe.wait_ge(em_ready, at + b + 1)
                for s in range(SUB):
                    for t in range(NT):
                        last = pe.matmul(bank[5 + t][:, 0:NODES], ebf[:, s, 1, t * P:(t + 1) * P], ebf[:, s, 0, :],
                                         start=(b, s) == (0, 0), stop=(b, s) == (NB - 1, SUB - 1), skip_group_check=True)
                last.then_inc(count_g, 1)

            def block0(b, par, i2, i16):
                pe.wait_ge(oh_ready, i2 + b + 1)
                for h in range(HEADS):
                    n = b * 8 + h
                    z0(n, par, i16)
                    if h == 2:
                        if b:
                            edge_logits(b - 1, i2)
                    elif h == 3:
                        if b:
                            pe.wait_ge(logit_r, i2 + b)
                        logit_parts(n - 3, par, i16)
                        logit_parts(n - 2, par, i16)
                    elif n >= 2:
                        logit_parts(n - 2, par if h >= 2 else 1 - par, i16)
                    if h == 4:
                        count0(b, i2)

            block0(0, 0, 0, 0)
            with pe.Fori(0, 5) as i:
                for u in range(2):
                    block0(1 + u, 1 - u, i * 2, i * 16)
            block0(NB - 1, 1, 0, 0)
            logit_parts(NB * 8 - 2, 1, 0)
            logit_parts(NB * 8 - 1, 1, 0)
            edge_logits(NB - 1, 0)

            def attend(first, ready, ready_first):
                def turn_head(h):
                    pe.wait_ge(ready, ready_first + NT * (h + 1))
                    if h:
                        pe.wait_ge(eT_ready, (first + h) * NT)
                    for d in range(NT):
                        for t in range(NT):
                            last = pe.transpose(bank[d][:, t * P:(t + 1) * P], eh[:, h % 2, t, d * P:(d + 1) * P], ident[:, :])
                        last.then_inc(e_turned, 1)

                def weighted(h):
                    pe.wait_ge(eT_ready, (first + h + 1) * NT)
                    for t in range(NT):
                        for d in range(NT):
                            last = pe.matmul(bank[5 + t][:, h * HD:(h + 1) * HD], eT[:, h % 2, d, t * P:(t + 1) * P],
                                             vn[:, d, h * HD:(h + 1) * HD], start=(d == 0), stop=(d == NT - 1))
                    last.then_inc(y_g, 1)
                return turn_head, weighted

            turn_head, weighted = attend(0, e_ready, 0)
            for h in range(HEADS):
                turn_head(h)
                if h:
                    weighted(h - 1)
            weighted(HEADS - 1)

            turn(xn)
            router(0)
            positions(1)
            turn_coef(1)

            for t in range(NT):
                pe.matmul(bank[4 + t][:, :], coefT[:, t * P:(t + 1) * P], b2e[:, 0, :], start=True, stop=True).then_inc(b2_g, 1)
            pe.wait_ge(expert_added, NT)
            gather_nodes(routed0)
            pe.wait_ge(routed0.sem["gathered_act"], 2 * routed0.groups)
            pe.wait_ge(routed0.sem["gathered_dve"], 2 * routed0.groups)
            with pe.Fori(0, EXPERTS) as e:
                def loaded(jj, q):
                    slot, arrived, base = slots0[3 * jj + q]
                    pe.wait_ge(arrived, e * 16 + (base + 16))
                    return slot.rearrange("p (k n) -> p k n", k=KT if q < 2 else 2)

                def expert0(width):
                    s = routed0.sem
                    blocks = (7, 3)[:width // SE]
                    slots = {}

                    def up(j):
                        for q in range(2):
                            if j % 2 == 0:
                                slots[j // 2, q] = loaded(j // 2, q)
                            out = bank[2 * q + j % 2][:, 0:NODES] if width == NODES else bank[j % 2][:, q * width:(q + 1) * width]
                            for k in range(KT):
                                rhs = xT[:, k, :] if width == NODES else routed0.xgT[k][:, bass.ds(e * (2 * SE), width)]
                                last = pe.matmul(out, slots[j // 2, q][:, k, j % 2 * P:(j % 2 + 1) * P], rhs,
                                                 start=(k == 0), stop=(k == KT - 1))
                        last.then_inc(up_g, 1)

                    def down(j):
                        if j % 2 == 0:
                            slots[j // 2, 2] = loaded(j // 2, 2)
                        if j == 0:
                            pe.wait_ge(s["cplace_copied"], e + 1)
                            if width == NODES:
                                pe.wait_ge(expert_added, e * NT + NT)
                        pe.wait_ge(hid_r, e * JT0 + j + 1)
                        for i, b in enumerate((4, 5, 6) if width == NODES else blocks):
                            last = pe.matmul(bank[b][:, :], act2[:, j % 2, i * P:(i + 1) * P], slots[j // 2, 2][:, j % 2, :],
                                             start=(j == 0), stop=(j == JT0 - 1), skip_group_check=True)
                        last.then_inc(down_g, 1)

                    up(0)
                    pe.wait_ge(s["cplace_ready"], e + 1)
                    for i, b in enumerate(blocks if width < NODES else (7,)):
                        for t in range(NT):
                            last = pe.transpose(bank[b][:, t * P:(t + 1) * P], cpl[:, t, i * SE:(i + 1) * SE], ident[:, :])
                    last.then_inc(s["cplace_turned"], 1)
                    for j in range(1, JT0):
                        up(j)
                        down(j - 1)
                    down(JT0 - 1)
                    pe.wait_ge(s["expert_out"], e + 1)
                    if width == NODES:
                        pe.transpose(bank[7][:, 0:P], cpl[:, 0, 0:SE], ident[:, :]).then_inc(s["combined"], 1)
                        return
                    pe.wait_ge(expert_added, e * NT + NT)
                    for t in range(NT):
                        for i in range(len(blocks)):
                            last = pe.matmul(bank[4 + t][:, :], cp2[:, i, t * P:(t + 1) * P], tmp[:, i, :], start=(i == 0), stop=(i == len(blocks) - 1))
                    last.then_inc(s["combined"], 1)

                chosen_by = pe.value_load(crowd[0:1, bass.ds(e, 1)], min_val=0, max_val=NODES)
                with pe.If(chosen_by <= SE):
                    expert0(SE)
                with pe.Else():
                    with pe.If(chosen_by <= 2 * SE):
                        expert0(2 * SE)
                    with pe.Else():
                        expert0(NODES)

            turn(xn)
            for g in range(6):
                which, t = divmod(g, NT)
                if t == 0:
                    arrived("w1", 2 * which)
                    arrived("w1", 2 * which + 1)
                if g >= 4:
                    pe.wait_ge(tab_sum, 12 + g - 3)
                product(bank[g % 4][:, :], lambda k: tile(xT, k, t), lambda k: weight(("w1",), 4 * which + k), KT, table_g)
            pe.wait_ge(tab_lo, 18)
            pe.wait_ge(tab_hi, 18)
            arrived("w2", 0)
            arrived("w2", 1)

            def z1(n, b, f, at, at_b):
                for w in range(2):
                    for t in range(NT):
                        for p in range(2):
                            pe.matmul(bank[n % 4][:, :], tabs1[:, w, p, t, f * P:(f + 1) * P], onehot[:, b % 2, w, t, :],
                                      start=(w, t, p) == (0, 0, 0), stop=False)
                if f == 0:
                    pe.wait_ge(at_lo, at_b)
                pe.matmul(bank[n % 4][:, :], w1hi[:, f * P:(f + 1) * P], attrs[:, b % 2, :], start=False, stop=False)
                pe.matmul(bank[n % 4][:, :], w1lo[:, f * P:(f + 1) * P], attrs[0:64, b % 2, :], start=False, stop=True).then_inc(mish_g, 1)

            def message(n, b, s):
                product(bank[n % 4][:, :], lambda k: hT[:, b % 2, k, s * P:(s + 1) * P], lambda k: weight(("w2",), k), KT, mish_g)

            def mish_product(n, at, i2):
                kind, b, s = mish_tile(n)
                if n >= 4:
                    out_of, value = mish_input_count(n - 4)
                    pe.wait_ge(out_of, i2 * 4 + value)
                if kind == "z":
                    if s == 0:
                        pe.wait_ge(oh_ready, i2 + (NB + b + 1))
                    z1(n, b, s, at, i2 + (b + 2))
                else:
                    if s == 0:
                        pe.wait_ge(mish_r, at + (8 * b + 3) if b else 4)
                    message(n, b, s)

            def aggregate(b, s, i2):
                pe.wait_ge(em_ready, i2 * 4 + (NB + 4 * b + s + 1))
                pe.wait_ge(msg_lo, i2 * 4 + (4 * b + s + 1))
                if True:
                    for t in range(NT):
                        for p, part in enumerate((mh, ml)):
                            last = pe.matmul(bank[4 + t][:, :], em[:, s, t * P:(t + 1) * P], part[:, s, :],
                                             start=(b, s, p) == (0, 0, 0), stop=(b, s, p) == (NB - 1, SUB - 1, 1), skip_group_check=True)
                            if b == NB - 1 and s == SUB - 1 and p == 1:
                                last.then_inc(agg_g, 1)

            def block1(b, i2, at):
                for q in range(8 if b < NB - 1 else 4):
                    kind, _, s = mish_tile(4 + 8 * b + q)
                    if kind == "m" and b:
                        aggregate(b - 1, s, i2)
                    mish_product(4 + 8 * b + q, at, i2)

            for n in range(4):
                mish_product(n, 0, 0)
            for b in range(3):
                block1(b, 0, 0)
            with pe.Fori(0, 4) as i:
                for u in range(2):
                    block1(3 + u, i * 2, i * 16)
            block1(NB - 1, 0, 0)
            for s in range(SUB):
                aggregate(NB - 1, s, 0)
            turn(y)
            for c in range(4):
                arrived("w3", c)
            for m in range(KT):
                product(bank[m][:, 0:NODES], lambda k: weight(("w3",), k)[:, m * P:(m + 1) * P],
                        lambda k: xT[:, k, :] if k < KT else yT[:, k - KT, :], 2 * KT, mish_g)
            arrived("w4", 0)
            arrived("w4", 1)
            pe.wait_ge(mish_r, MISH + KT)
            for t in range(NT):
                product(bank[4 + t][:, :], lambda k: tile(hidT, k, t), lambda k: weight(("w4",), k), KT, node_g)

            turn(xn)

            def turn_quant(j, u, at):
                pe.wait_ge(quant_r, at + j + 1)
                for c in range(3):
                    for g in range(4):
                        last = pe.transpose(bank[c][:, g * P:(g + 1) * P], qa[:, u, (4 * c + g) * P:(4 * c + g + 1) * P], ident[:, :])
                    last.then_inc(q_turned, 1)

            def up1(j, u, at):
                pe.wait_ge(qT_a, at * 2 + 2 * j + 2)
                pe.wait_ge(qT_v, at + j + 1)
                for c in range(2):
                    for k in range(KT):
                        last = pe.matmul(bank[3 + c][:, 0:NODES], qT[:, u, c, k * P:(k + 1) * P], xT[:, k, :], start=(k == 0), stop=(k == KT - 1))
                last.then_inc(up_g, 1)

            def step1(j, at):
                up1(j, j % 2, at)
                if j < JT1 - 1:
                    turn_quant(j + 1, (j + 1) % 2, at)
                pe.wait_ge(hid_r, at + UP1 + j + 1)
                for t in range(NT):
                    last = pe.matmul(bank[5 + t][:, :], act2[:, j % 2, t * P:(t + 1) * P], qT[:, j % 2, 2, :],
                                     start=(j == 0), stop=(j == JT1 - 1), skip_group_check=True)
                last.then_inc(down_g, 1)

            turn_quant(0, 0, 0)
            step1(0, 0)
            with pe.Fori(0, 4) as i:
                for j in (1, 2):
                    step1(j, i * 2)
            step1(9, 0)
            step1(10, 0)

            turn(xn)
            values(("ws",), value_g)
            pe.wait_ge(pq_r, 1)
            for t in range(NT):
                last = pe.transpose(bank[3][0:8, t * P:(t + 1) * P], pq[:, 1, t, :], ident[:, :])
            last.then_inc(pqT_g, 1)
            pe.wait_ge(pqT_r, 1)

            def source_row(h):
                if h >= 2:
                    pe.wait_ge(score_r, NT * (h - 1))
                if h == 0:
                    pe.wait_ge(sel_ready, 1)
                pe.matmul(bank[3 + h % 2][:, 0:NODES], sel8[:, h, :], qT2, start=True, stop=True).then_inc(srow_g, 1)

            turn_head, weighted = attend(HEADS, weighed, 0)
            source_row(0)
            source_row(1)
            for h in range(HEADS):
                turn_head(h)
                if h + 2 < HEADS:
                    source_row(h + 2)
                if h:
                    weighted(h - 1)
            weighted(HEADS - 1)

            turn(xn)
            router(1)
            positions(2)
            turn_coef(2)

            gather_nodes(routed2)
            experts2()

            turn(xn)
            for r in range(4):
                arrived("wr", r, 0)
                arrived("wr", r, 1)
                for t in range(NT):
                    n = r * NT + t
                    if n >= 4:
                        pe.wait_ge(rel_r, n - 3)
                    product(bank[n % 4][:, :], lambda k: tile(xT, k, t), lambda k: weight(("wr", r), k), KT, rel_g)
            values(("wself",), node_g)
            pe.wait_ge(wdeg_r, 1)
            pe.wait_ge(rel_r, 4 * NT)
            pe.matmul(bank[3][:, 0:2 * NT], zeros[:, :], zeros[:, 0:2 * NT], start=True, stop=False, skip_group_check=True)

            def sum3(n, at):
                pe.wait_ge(em_ready, at + (5 * NB + n + 1))
                pe.wait_ge(msg_lo, at + (4 * NB + n + 1))
                for t in range(NT):
                    lhs = em[:, n % 4, t * P:(t + 1) * P]
                    for p, part in enumerate((mh, ml)):
                        last = pe.matmul(bank[t][:, :], lhs, part[:, n % 4, :], start=(n, p) == (0, 0), stop=(n, p) == (ET - 1, 1), skip_group_check=True)
                        if (n, p) == (ET - 1, 1):
                            last.then_inc(agg_g, 1)
                    last = pe.matmul(bank[3][:, 2 * t:2 * t + 2], lhs, wdeg[:, bass.ds(at + n, 1), :].rearrange("p a b -> p (a b)"),
                                     start=False, stop=(n, t) == (ET - 1, NT - 1), skip_group_check=True)
                last.then_inc(agg_g if n == ET - 1 else m_used, 1)

            for n in range(RING):
                sum3(n, 0)
            with pe.Fori(0, 4) as i:
                for c in range(RING, 2 * RING):
                    sum3(c, i * RING)
            for n in range(5 * RING, 6 * RING):
                sum3(n, 0)
            turn(y)
            for k in range(4):
                arrived("wf1", k)
            for m in range(8):
                if m >= 4:
                    pe.wait_ge(gelu_r, m - 3)
                product(bank[m % 4][:, 0:NODES], lambda k: wring[:, W["wf1", k][0], m * P:(m + 1) * P], lambda k: yT[:, k, :], KT, node_g)
            for c in range(4):
                arrived("wf2", c)
            pe.wait_ge(gelu_r, 8)
            for t in range(NT):
                product(bank[4 + t][:, :], lambda k: tile(hidT, k, t), lambda k: weight(("wf2",), k), 8, node_g)

            turn(xn)
            for k in range(KT):
                last = pe.matmul(bank[7][0:8, 0:NODES], gatew[:, 2, k, :], xT[:, k, :], start=(k == 0), stop=(k == KT - 1))
            last.then_inc(route_g, 1)

            def expert3(v, t, i, fresh):
                if t == 0:
                    for c in range(2):
                        slot = f3[2 * v + c]
                        pe.wait_ge(arrive[slot], i * 16 + (f3_base[slot] + 16))
                if not fresh:
                    pe.wait_ge(y3_out, i * (2 * NT) + ((v - 2) * NT + t + 1))
                for k in range(KT):
                    last = pe.matmul(bank[2 + 3 * v + t][:, :], tile(xT, k, t), wslot(f3[2 * v + k // 2], 2)[:, k % 2, :],
                                     start=(k == 0), stop=(k == KT - 1))
                last.then_inc(expert3_g, 1)

            def sinkhorn(v, i, fresh=False):
                at = i * 16 + 8 * v
                pe.wait_ge(sk_d, at + 4)
                for t in range(NT):
                    last = pe.matmul(bank[0][:, t * 8:t * 8 + 8], sink[:, 0, t * P:(t + 1) * P], ident[0:8, 0:8], start=True, stop=True)
                last.then_inc(sk_p, 1)
                expert3(v, 0, i, fresh)
                pe.wait_ge(sk_d, at + 8)
                for t in range(NT):
                    last = pe.transpose(bank[1][0:8, t * P:(t + 1) * P], sinka[:, 0, t, :], ident[:, :])
                last.then_inc(sk_p, 1)
                expert3(v, 1, i, fresh)
                expert3(v, 2, i, fresh)

            for v in range(2):
                sinkhorn(v, 0, True)
            with pe.Fori(1, SINKHORN // 2) as i:
                for v in range(2):
                    sinkhorn(v, i)
            pe.wait_ge(mask_r, 3)
            for c in range(2):
                for t in range(NT):
                    last = pe.transpose(bank[1][:, (c * NT + t) * 8:(c * NT + t) * 8 + 8], sink[:, 3 + c, t * P:(t + 1) * P], ident[0:8, 0:8])
            last.then_inc(sk_p, 1)
            pe.wait_ge(y3_out, NT * EXPERTS)
            for e in range(EXPERTS):
                pe.wait_ge(sk_a, 4 * SINKHORN + 2 + e + 1)
                last = pe.matmul(bank[2][:, :], diag[:, e, :], y3[e // 6][:, e % 6, (NT - 1) * 512:NT * 512],
                                 start=(e == 0), stop=(e == EXPERTS - 1))
            last.then_inc(expert3_g, 1)


def kernel(**inputs):
    import numpy as np
    import concourse.bacc as bacc
    from concourse.bass_utils import run_bass_kernel_spmd

    given = {k: np.ascontiguousarray(v) for k, v in inputs.items()}
    sent = dict(given)
    for name, new in (("src", "src_c"), ("dst", "dst_c"), ("edge_type_4", "typ_c"), ("edge_weight", "ew_c")):
        sent[new] = given[name].reshape(ET, P).T
    sent["attrT"] = given["edge_attr_64"].T
    sent["bwa"], sent["bwb"] = given["L0_gnn_bw"][:512], given["L0_gnn_bw"][512:]
    sent["L0_ffn_b1"] = given["L0_ffn_b1"].reshape(EXPERTS, 2 * JT0, P).transpose(2, 0, 1)
    sent["L2_ffn_b1"] = given["L2_ffn_b1"].reshape(EXPERTS, JT2, P).transpose(2, 0, 1)
    sent["L1_gnn_b3"] = given["L1_gnn_b3"].reshape(KT, P).T
    sent["L3_gnn_b_ffn1"] = given["L3_gnn_b_ffn1"].reshape(8, P).T
    sent["L2_gnn_Ws"] = given["L2_gnn_Ws"].transpose(1, 0, 2).reshape(DIM, DIM)
    sent["L2_gnn_Wb"] = given["L2_gnn_Wb"].reshape(DIM)
    sent["L2_gnn_at"] = given["L2_gnn_a_w"][:, :HD].reshape(DIM)
    sent["L2_gnn_as"] = given["L2_gnn_a_w"][:, HD:].reshape(DIM)
    sent["L3_ffn_gate_w"] = given["L3_ffn_gate_w"][0]
    for name in ("edge_attr_64", "edge_type_4", "edge_weight", "L0_gnn_bw", "L2_gnn_a_w"):
        del sent[name]

    nc = bacc.Bacc("TRN2", target_bir_lowering=False, num_devices=1)
    arrays, a = {}, {}
    for name, value in sent.items():
        value = np.ascontiguousarray(value)
        arrays[f"in_{name}"] = value
        a[name] = nc.dram_tensor(f"in_{name}", value.shape, mybir.dt.from_np(value.dtype), kind="ExternalInput").ap()
    out = nc.dram_tensor("out", (NODES, DIM), F32, kind="ExternalOutput").ap()
    table0 = nc.dram_tensor("pair_logits", (NODES * NODES, HEADS), F32, kind="Internal").ap()
    table3 = nc.dram_tensor("relation_rows", (NODES * 4, DIM), F32, kind="Internal").ap()
    build(nc, a, out, table0, table3)
    return run_bass_kernel_spmd(nc, [arrays], core_ids=[0]).results[0]["out"]
```
